# Optimizing a Trainium2 kernel written in Bass

```python
import numpy as np
import jax
import jax.numpy as jnp

def _softmax(x, axis=-1):
    return jax.nn.softmax(x, axis=axis)

def _gelu(x):
    return jax.nn.gelu(x, approximate=True)

def _silu(x):
    return jax.nn.silu(x)

def _sigmoid(x):
    return jax.nn.sigmoid(x)

def _layernorm(x, axis=-1, eps=1e-05):
    m = jnp.mean(x, axis=axis, keepdims=True)
    v = jnp.var(x, axis=axis, keepdims=True)
    return (x - m) / jnp.sqrt(v + eps)

def _scatter_add(tgt, idx, src, axis=0):
    return tgt.at[idx].add(src)

def _segment_sum(src, seg, n):
    return jax.ops.segment_sum(src, seg, n)
kernel_name = 'mk_gnn_ffn_d2_gnn_r8_33bae9'

def setup_inputs(seed: int=0):
    np.random.seed(seed)
    _w = jnp.asarray

    def _rec_inputs():
        import jax
        import jax.numpy as jnp
        _gk = jax.random.key(seed)
        x = -8.776e-05 + 1 * jax.random.normal(jax.random.fold_in(_gk, 1), (1250, 512), jnp.float32)
        _s = jax.random.randint(jax.random.fold_in(_gk, 2), (20000,), 0, 1250, jnp.int32)
        _d = jax.random.randint(jax.random.fold_in(_gk, 3), (20000,), 0, 1250, jnp.int32)
        _loop = jnp.arange(1250, dtype=jnp.int32)
        src = jnp.concatenate([_s, _d, _loop])
        dst = jnp.concatenate([_d, _s, _loop])
        _o = jnp.argsort(dst, stable=True)
        src = src[_o]
        dst = dst[_o]
        return (x, src, dst)
    x, src, dst = _rec_inputs()

    def _L0_gnn_setup():
        import jax, jax.numpy as jnp
        import numpy as np
        N_NODES = 1250
        IN_FEAT = 512
        OUT_FEAT = 512
        N_EDGES = 20000
        key = jax.random.key(seed)
        kx, kw, ks, kd = jax.random.split(key, 4)
        x = jax.random.normal(kx, (N_NODES, IN_FEAT), dtype=jnp.float32)
        fan_in, fan_out = (2 * IN_FEAT, OUT_FEAT)
        limit = float(np.sqrt(6.0 / (fan_in + fan_out)))
        w = jax.random.uniform(kw, (OUT_FEAT, 2 * IN_FEAT), dtype=jnp.float32, minval=-limit, maxval=limit)
        src = jax.random.randint(ks, (N_EDGES,), 0, N_NODES, dtype=jnp.int32)
        dst = jax.random.randint(kd, (N_EDGES,), 0, N_NODES, dtype=jnp.int32)
        edge_index = jnp.stack([src, dst], axis=0)
        return {'x': x, 'w': w, 'edge_index': edge_index}
    _L0_gnn_all = _L0_gnn_setup()
    _L0_gnn_in = {k: v for k, v in _L0_gnn_all.items() if k in ('w',)}
    del _L0_gnn_all

    def _L0_ffn_setup():
        import jax, jax.numpy as jnp
        import numpy as np
        D = 512
        E = 8
        K = 2
        EXP = 4
        LN_EPS = 1e-05
        key = jax.random.key(seed)
        ks = jax.random.split(key, 8)
        B, T = (8, 256)
        Dh = D * EXP
        x = jax.random.normal(ks[0], (B, T, D), dtype=jnp.float32)
        ln_g = jnp.ones((D,), dtype=jnp.float32)
        ln_b = jnp.zeros((D,), dtype=jnp.float32)
        lim_r = np.sqrt(6.0 / (D + E)).astype(np.float32)
        w_r = jax.random.uniform(ks[1], (E, D), dtype=jnp.float32, minval=-lim_r, maxval=lim_r)
        b_r = jnp.zeros((E,), dtype=jnp.float32)
        lim1 = np.sqrt(6.0 / (D + Dh)).astype(np.float32)
        W1 = jax.random.uniform(ks[2], (E, D, Dh), dtype=jnp.float32, minval=-lim1, maxval=lim1)
        b1 = jnp.zeros((E, Dh), dtype=jnp.float32)
        W2 = jax.random.uniform(ks[3], (E, Dh, D), dtype=jnp.float32, minval=-lim1, maxval=lim1)
        b2 = jnp.zeros((E, D), dtype=jnp.float32)
        return {'x': x, 'ln_g': ln_g, 'ln_b': ln_b, 'w_r': w_r, 'b_r': b_r, 'W1': W1, 'b1': b1, 'W2': W2, 'b2': b2}
    _L0_ffn_all = _L0_ffn_setup()
    _L0_ffn_in = {k: v for k, v in _L0_ffn_all.items() if k in ('ln_g', 'ln_b', 'w_r', 'b_r', 'W1', 'b1', 'W2', 'b2')}
    del _L0_ffn_all

    def _L1_gnn_setup():
        import jax, jax.numpy as jnp
        import numpy as np
        N_NODES = 2500
        N_EDGES = 40000
        D = 512
        L = 3
        key = jax.random.key(seed)
        ks = jax.random.split(key, 6)
        x = jax.random.normal(ks[0], (N_NODES, D), dtype=jnp.float32)
        Ws_self = jax.random.normal(ks[1], (L, D, D), dtype=jnp.float32) * 0.05
        Ws_neigh = jax.random.normal(ks[2], (L, D, D), dtype=jnp.float32) * 0.05
        bs = jax.random.normal(ks[3], (L, D), dtype=jnp.float32) * 0.05
        src = jax.random.randint(ks[4], (N_EDGES,), 0, N_NODES, dtype=jnp.int64)
        dst = jax.random.randint(ks[5], (N_EDGES,), 0, N_NODES, dtype=jnp.int64)
        return {'x': x, 'Ws_self': Ws_self, 'Ws_neigh': Ws_neigh, 'bs': bs, 'src': src, 'dst': dst}
    _L1_gnn_all = _L1_gnn_setup()
    _L1_gnn_in = {k: v for k, v in _L1_gnn_all.items() if k in ('Ws_self', 'Ws_neigh', 'bs')}
    del _L1_gnn_all

    def _L1_ffn_setup():
        import jax, jax.numpy as jnp
        import numpy as np
        CAPACITY_FACTOR = 1.2
        key = jax.random.key(seed)
        k1, k2, k3 = jax.random.split(key, 3)
        B, S, D, E = (8, 512, 512, 16)
        x = jax.random.normal(k1, (B, S, D), dtype=jnp.float32)
        switch_w = jax.random.normal(k2, (E, D), dtype=jnp.float32) * 0.02
        switch_b = jnp.zeros((E,), dtype=jnp.float32)
        expert_w = jax.random.normal(k3, (E, D, D), dtype=jnp.float32) * 0.02
        expert_b = jnp.zeros((E, D), dtype=jnp.float32)
        return {'x': x, 'switch_w': switch_w, 'switch_b': switch_b, 'expert_w': expert_w, 'expert_b': expert_b}
    _L1_ffn_all = _L1_ffn_setup()
    _L1_ffn_in = {k: v for k, v in _L1_ffn_all.items() if k in ('switch_w', 'switch_b', 'expert_w', 'expert_b')}
    del _L1_ffn_all
    return {'x': x, 'src': src, 'dst': dst, 'L0_gnn_w': _L0_gnn_in['w'], 'L0_ffn_ln_g': _L0_ffn_in['ln_g'], 'L0_ffn_ln_b': _L0_ffn_in['ln_b'], 'L0_ffn_w_r': _L0_ffn_in['w_r'], 'L0_ffn_b_r': _L0_ffn_in['b_r'], 'L0_ffn_W1': _L0_ffn_in['W1'], 'L0_ffn_b1': _L0_ffn_in['b1'], 'L0_ffn_W2': _L0_ffn_in['W2'], 'L0_ffn_b2': _L0_ffn_in['b2'], 'L1_gnn_Ws_self': _L1_gnn_in['Ws_self'], 'L1_gnn_Ws_neigh': _L1_gnn_in['Ws_neigh'], 'L1_gnn_bs': _L1_gnn_in['bs'], 'L1_ffn_switch_w': _L1_ffn_in['switch_w'], 'L1_ffn_switch_b': _L1_ffn_in['switch_b'], 'L1_ffn_expert_w': _L1_ffn_in['expert_w'], 'L1_ffn_expert_b': _L1_ffn_in['expert_b']}

def reference(x, src, dst, L0_gnn_w, L0_ffn_ln_g, L0_ffn_ln_b, L0_ffn_w_r, L0_ffn_b_r, L0_ffn_W1, L0_ffn_b1, L0_ffn_W2, L0_ffn_b2, L1_gnn_Ws_self, L1_gnn_Ws_neigh, L1_gnn_bs, L1_ffn_switch_w, L1_ffn_switch_b, L1_ffn_expert_w, L1_ffn_expert_b):
    import jax
    import jax.numpy as jnp

    def _L0_gnn_ref(x, w, edge_index):
        import jax, jax.numpy as jnp
        import numpy as np
        N_NODES = 1250
        IN_FEAT = 512
        OUT_FEAT = 512
        N_EDGES = 20000
        src, dst = (edge_index[0], edge_index[1])
        msgs = x[src]
        summed = jax.ops.segment_sum(msgs, dst, num_segments=x.shape[0])
        deg = jax.ops.segment_sum(jnp.ones_like(dst, dtype=x.dtype), dst, num_segments=x.shape[0])
        neighbor_mean = summed / jnp.maximum(deg, 1.0)[:, None]
        message = jnp.concatenate([x, neighbor_mean], axis=-1)
        weighted = jnp.einsum('of,nf->no', w, message)
        return jax.nn.relu(weighted)

    def _L0_ffn_ref(x, ln_g, ln_b, w_r, b_r, W1, b1, W2, b2):
        import jax, jax.numpy as jnp
        import numpy as np
        D = 512
        E = 8
        K = 2
        EXP = 4
        LN_EPS = 1e-05
        B, T, d = x.shape
        mu = jnp.mean(x, axis=-1, keepdims=True)
        var = jnp.mean(jnp.square(x - mu), axis=-1, keepdims=True)
        h = (x - mu) * jax.lax.rsqrt(var + LN_EPS) * ln_g + ln_b
        logits = jnp.einsum('btd,ed->bte', h, w_r) + b_r
        topk_vals, topk_idx = jax.lax.top_k(logits, K)
        gates = jax.nn.softmax(topk_vals, axis=-1)
        hf = h.reshape(B * T, d)
        hid = jax.nn.gelu(jnp.einsum('nd,edf->nef', hf, W1) + b1, approximate=False)
        expert_stack = jnp.einsum('nef,efd->ned', hid, W2) + b2
        idx_flat = topk_idx.reshape(B * T, K)
        gates_flat = gates.reshape(B * T, K)
        gathered = jnp.take_along_axis(expert_stack, idx_flat[:, :, None], axis=1)
        mixed = jnp.sum(gathered * gates_flat[:, :, None], axis=1).reshape(B, T, d)
        return x + mixed

    def _L1_gnn_ref(x, Ws_self, Ws_neigh, bs, src, dst):
        import jax, jax.numpy as jnp
        import numpy as np
        N_NODES = 2500
        N_EDGES = 40000
        D = 512
        L = 3
        n = x.shape[0]
        deg = jax.ops.segment_sum(jnp.ones_like(dst, dtype=x.dtype), dst, num_segments=n)
        inv_deg = (1.0 / jnp.clip(deg, 1.0))[:, None]
        h = x
        n_layers = Ws_self.shape[0]
        for l in range(n_layers):
            neigh = jax.ops.segment_sum(h[src], dst, num_segments=n) * inv_deg
            h = h @ Ws_self[l] + neigh @ Ws_neigh[l] + bs[l]
            if l != n_layers - 1:
                h = jax.nn.relu(h)
        return h

    def _L1_ffn_ref(x, switch_w, switch_b, expert_w, expert_b):
        import jax, jax.numpy as jnp
        import numpy as np
        CAPACITY_FACTOR = 1.2
        B, S, D = x.shape
        E = switch_w.shape[0]
        N = B * S
        xf = x.reshape(N, D)
        logits = xf @ switch_w.T + switch_b
        probs = jax.nn.softmax(logits, axis=-1)
        route_probs = jnp.max(probs, axis=-1)
        routes = jnp.argmax(probs, axis=-1)
        oh = jax.nn.one_hot(routes, E, dtype=jnp.int32)
        pos = jnp.take_along_axis(jnp.cumsum(oh, axis=0), routes[:, None], axis=1)[:, 0] - 1
        capacity = int(CAPACITY_FACTOR * N / E)
        keep = pos < capacity
        buf = jnp.zeros((E, capacity, D), dtype=xf.dtype).at[routes, pos].set(xf)
        y = jnp.einsum('ecd,efd->ecf', buf, expert_w) + expert_b[:, None, :]
        gathered = y[routes, jnp.minimum(pos, capacity - 1)]
        out = jnp.where(keep[:, None], gathered, xf) * route_probs[:, None]
        return out.reshape(B, S, D)
    edge_index = jnp.stack([src, dst])
    x = x + _L0_gnn_ref(_layernorm(x, axis=-1), L0_gnn_w, edge_index)
    x = x + _L0_ffn_ref(_layernorm(x, axis=-1)[None], L0_ffn_ln_g, L0_ffn_ln_b, L0_ffn_w_r, L0_ffn_b_r, L0_ffn_W1, L0_ffn_b1, L0_ffn_W2, L0_ffn_b2)[0]
    x = x + _L1_gnn_ref(_layernorm(x, axis=-1), L1_gnn_Ws_self, L1_gnn_Ws_neigh, L1_gnn_bs, src, dst)
    x = x + _L1_ffn_ref(_layernorm(x, axis=-1)[None], L1_ffn_switch_w, L1_ffn_switch_b, L1_ffn_expert_w, L1_ffn_expert_b)[0]
    return x

_drawn_inputs = setup_inputs


def setup_inputs(seed=0):
    import zlib

    import numpy as np

    out = dict(_drawn_inputs(seed))
    spreads = {'L0_ffn_ln_g': (1.0, 0.2),
     'L0_ffn_ln_b': (0.0, 0.1),
     'L0_ffn_b_r': (0.0, 0.1),
     'L0_ffn_b1': (0.0, 0.299),
     'L0_ffn_b2': (0.0, 0.1),
     'L1_ffn_switch_b': (0.0, 0.374),
     'L1_ffn_expert_b': (0.0, 0.8)}
    factors = {}
    for name, (base, spread) in spreads.items():
        noise = np.random.default_rng([zlib.crc32(name.encode()), seed]).standard_normal(out[name].shape)
        drawn = base * np.exp(spread * noise) if base else spread * noise
        out[name] = jnp.asarray(drawn.astype(out[name].dtype))
    for name, factor in factors.items():
        out[name] = (out[name] * factor).astype(out[name].dtype)
    return out
```

```python
from contextlib import ExitStack

import numpy as np
import concourse.bass as bass
import concourse.mybir as mybir

ALU = mybir.AluOpType
ACT = mybir.ActivationFunctionType
AX = mybir.AxisListType
F32 = mybir.dt.float32
F32R = mybir.dt.float32r
BF16 = mybir.dt.bfloat16
I32 = mybir.dt.int32
U32 = mybir.dt.uint32
I16 = mybir.dt.int16
U16 = mybir.dt.uint16

P = 128
N = 1250
D = 512
E_ALL = 41250
NT = -(-N // P)
NPAD = NT * P
LAST = N - (NT - 1) * P
KD = D // P
EPS = 1e-5

CH = 4
GE = CH * P
NG = -(-E_ALL // GE)
TAIL = E_ALL - (NG - 1) * GE
WIN = 32
AW = NPAD + WIN
PASSES = -(-N // WIN)

E1 = 8
F1 = 2048
FB = 512
NFB = F1 // FB
T = 384
TB = T // P
UNITS = E1 + 2 * N // T
SLOTS = UNITS * T
FEWEST = -(-2 * N // T)

E2 = 16
CAP = int(1.2 * N / E2)
PLACES = E2 * P


class Stage:

    def __init__(self, nc, tag):
        self.nc, self.tag, self.ctx = nc, tag, ExitStack()

    def __enter__(self):
        self.ctx.__enter__()
        return self

    def __exit__(self, *a):
        return self.ctx.__exit__(*a)

    def sbuf(self, name, shape, dt):
        return self.ctx.enter_context(self.nc.sbuf_tensor(f"{self.tag}_{name}", shape, dt))

    def psum(self, name, shape, dt=F32):
        return self.ctx.enter_context(self.nc.psum_tensor(f"{self.tag}_{name}", shape, dt))

    def sem(self, name):
        return self.ctx.enter_context(self.nc.semaphore(f"{self.tag}_{name}"))



def by_tile(ap):
    return ap.rearrange("(t p) d -> p t d", p=P)


def make_constants(nc, keep):
    c = {
        "ident": keep.sbuf("ident", [P, P], F32),
        "upper": keep.sbuf("upper", [P, P], F32),
        "ones": keep.sbuf("ones", [P, P], F32),
        "half": keep.sbuf("minus_half", [P, NT], F32),
        "real": keep.sbuf("real_node", [P, NT], F32),
        "node": keep.sbuf("node_id", [P, NT], I32),
    }
    made = keep.sem("constants_made")
    with nc.Block() as block:
        @block.gpsimd
        def _(pool):
            pool.memset(c["ident"][:], 0.0).then_inc(made, 1)
            pool.memset(c["upper"][:], 1.0).then_inc(made, 1)
            pool.memset(c["ones"][:], 1.0).then_inc(made, 1)
            pool.memset(c["half"][:], -0.5).then_inc(made, 1)
            pool.memset(c["real"][:], 1.0).then_inc(made, 1)
            pool.iota(c["node"][:], pattern=[[P, NT]], base=0, channel_multiplier=1).then_inc(made, 1)
            pool.wait_ge(made, 6)
            pool.affine_select(out=c["ident"][:], in_=c["ident"][:], compare_op=ALU.not_equal, fill=1.0,
                               base=0, pattern=[[-1, P]], channel_multiplier=1).then_inc(made, 1)
            pool.affine_select(out=c["upper"][:], in_=c["upper"][:], compare_op=ALU.is_gt, fill=0.0,
                               base=0, pattern=[[1, P]], channel_multiplier=-1).then_inc(made, 1)
            pool.affine_select(out=c["real"][:], in_=c["real"][:], compare_op=ALU.is_gt, fill=0.0,
                               base=N, pattern=[[-P, NT]], channel_multiplier=-1).then_inc(made, 1)
            pool.wait_ge(made, 9)
    return c


def normalize(nc, c, tag, source, target):
    with Stage(nc, tag) as s:
        stats = s.sbuf("bn_stats", [P, NT, 6], F32)
        mean_var = s.sbuf("mean_var", [P, NT, 2], F32)
        rstd = s.sbuf("rstd", [P, NT], F32)
        measured, scaled, done = s.sem("ln_measured"), s.sem("ln_scaled"), s.sem("ln_done")
        with nc.Block() as block:
            @block.vector
            def _(dve):
                for t in range(NT):
                    dve.bn_stats(stats[:, t, :], source[:, t, :]).then_inc(measured, 1)
                for t in range(NT):
                    dve.wait_ge(measured, t + 1)
                    dve.bn_aggr(mean_var[:, t, :], stats[:, t, :]).then_inc(measured, 1)
                dve.wait_ge(scaled, 2)
                for t in range(NT):
                    dve.tensor_scalar(target[:, t, :], source[:, t, :], mean_var[:, t, 0:1], rstd[:, t:t + 1],
                                      ALU.subtract, ALU.mult).then_inc(done, 1)

            @block.gpsimd
            def _(pool):
                pool.wait_ge(measured, 2 * NT)
                pool.tensor_scalar(rstd[:], mean_var[:, :, 1], EPS, None, ALU.add).then_inc(scaled, 1)
                pool.wait_ge(scaled, 1)
                pool.tensor_tensor(rstd[:], rstd[:], c["half"][:], ALU.pow).then_inc(scaled, 1)


def build_adjacency(nc, c, keep, src, dst, counts, y_rows):
    NP = 10 * WIN
    with Stage(nc, "adjacency") as s:
        edge_src = s.sbuf("edge_src", [NG, GE], I32)
        edge_dst = s.sbuf("edge_dst", [NG, GE], I32)
        low_i = s.sbuf("src_low_i", [NG, GE], I32)
        high_i = s.sbuf("src_high_i", [NG, GE], I32)
        dst_f = s.sbuf("dst_f", [NG, GE], F32)
        low_f = s.sbuf("src_low_f", [NG, GE], F32)
        high_f = s.sbuf("src_high_f", [NG, GE], F32)
        rel = s.sbuf("dst_in_window", [NG, GE], F32)
        inside = s.sbuf("inside_window", [NG, GE], F32)
        place = s.sbuf("place", [NG, GE], F32)
        base = s.sbuf("window_base", [NG, 1], F32)
        top = s.sbuf("greatest_dst", [NG, 1], F32)
        wide = s.sbuf("wide_columns", [NG, 2, P], F32)
        low_t = s.sbuf("src_low_t", [P, CH, NG], F32)
        place_t = s.sbuf("place_t", [P, CH, NG], F32)
        base_row = s.sbuf("base_row", [1, NG], I32)
        span = s.sbuf("greatest_span", [1, 2], F32)
        span_i = s.sbuf("greatest_span_i", [1, 1], I32)
        count_low = s.sbuf("count_low", [P, P], I16)
        count_place = s.sbuf("count_place", [P, NP], I16)
        hot_low = s.sbuf("onehot_low", [P, 2, CH, P], BF16)
        hot_place = s.sbuf("onehot_place", [P, 2, CH, NP], BF16)
        ps_t = [s.psum(f"ps_edges_{i}", [P, 512]) for i in range(3)]
        ps_n = [s.psum(f"ps_window_{i}", [P, 512]) for i in range(2)]
        edges_in, filled = s.sem("edges_in"), s.sem("edges_filled")
        step, turned, taken = s.sem("edge_step"), s.sem("edges_turned"), s.sem("edges_taken")
        hot, counted, added = s.sem("onehots_ready"), s.sem("window_counted"), s.sem("window_added")
        zeros = s.sbuf("zero_rows", [P, D], F32)
        zeroed, cleared = s.sem("zero_rows_made"), s.sem("y_rows_cleared")

        FIRST, PREP = 12, 7
        turns = (3, 2)

        def prepare(dve, at, k_turn, k_taken):
            dve.tensor_scalar(rel[:], dst_f[:], base[:, 0:1], None, ALU.subtract).then_inc(step, 1)
            dve.wait_ge(step, at + 1)
            dve.tensor_scalar(inside[:], rel[:], 0.0, None, ALU.is_ge).then_inc(step, 1)
            dve.wait_ge(step, at + 2)
            dve.scalar_tensor_tensor(inside[:], rel[:], float(WIN), inside[:], ALU.is_lt, ALU.mult).then_inc(step, 1)
            dve.scalar_tensor_tensor(place[:], rel[:], 1.0, high_f[:], ALU.add, ALU.add).then_inc(step, 1)
            dve.wait_ge(step, at + 4)
            dve.tensor_tensor(place[:], place[:], inside[:], ALU.mult).then_inc(step, 1)
            dve.tensor_copy(wide[:, 0, 0:1], base[:, 0:1]).then_inc(step, 1)
            dve.wait_ge(turned, k_turn)
            dve.tensor_copy(place_t[:], ps_t[0][:, 0:CH * NG].rearrange("p (c g) -> p c g", c=CH)).then_inc(taken, 1)
            dve.tensor_copy(base_row[:], ps_t[1][0:1, 0:NG]).then_inc(taken, 1)
            dve.tensor_scalar(base[:], base[:], float(WIN), float(NPAD), ALU.add, ALU.min).then_inc(step, 1)
            dve.wait_ge(taken, k_taken)
            dve.wait_ge(step, at + 7)

        def turn_places(pe, at, k_turn):
            pe.wait_ge(step, at + 6)
            for ch in range(CH):
                last = pe.transpose(ps_t[0][:, ch * NG:(ch + 1) * NG], place[:, ch * P:(ch + 1) * P], c["ident"][0:NG, 0:NG])
            last.then_inc(turned, 1)
            pe.transpose(ps_t[1][:, 0:NG], wide[:, 0, :], c["ident"][0:NG, 0:NG]).then_inc(turned, 1)

        def onehots(dve, g, u):
            for ch in range(CH):
                dve.tensor_scalar(hot_low[:, u, ch, :], count_low[:], low_t[:, ch, bass.ds(g, 1)], None, ALU.is_equal)
                last = dve.tensor_scalar(hot_place[:, u, ch, :], count_place[:], place_t[:, ch, bass.ds(g, 1)],
                                         None, ALU.is_equal)
            last.then_inc(hot, 1)

        def add_window(dve, g, u, done, start):
            at = counts[:, :, bass.ds(start, WIN)]
            dve.wait_ge(counted, done + 1)
            dve.wait_ge(added, done + 1)
            dve.tensor_tensor(at, ps_n[u][:, 0:NP].rearrange("p (a b) -> p a b", b=WIN), at, ALU.add).then_inc(added, 1)

        def base_of(dve, g):
            return dve.value_load(base_row[0:1, bass.ds(g, 1)], min_val=0, max_val=NPAD)

        def count_pass(dve, before):
            onehots(dve, 0, 0)
            with dve.Fori(0, (NG - 1) // 2) as i:
                for u in range(2):
                    g = 2 * i + u
                    start = base_of(dve, g)
                    onehots(dve, g + 1, 1 - u)
                    add_window(dve, g, u, before + g, start)
            start = base_of(dve, NG - 1)
            add_window(dve, NG - 1, 0, before + NG - 1, start)
            dve.wait_ge(added, before + NG + 1)

        def multiply(pe, g, u, before):
            pe.wait_ge(hot, before + g + 1)
            for ch in range(CH):
                last = pe.matmul(ps_n[u][:, 0:NP], hot_low[:, u, ch, :], hot_place[:, u, ch, :],
                                 start=(ch == 0), stop=(ch == CH - 1))
            last.then_inc(counted, 1)

        def multiply_pass(pe, before):
            multiply(pe, 0, 0, before)
            with pe.Fori(0, (NG - 1) // 2) as i:
                for u in range(2):
                    multiply(pe, 2 * i + u + 1, 1 - u, before)

        with nc.Block() as block:
            @block.sync
            def _(sp):
                sp.wait_ge(filled, 1)
                full = (NG - 1) * GE
                sp.dma_start(edge_src[0:NG - 1, :], src[0:full].rearrange("(g e) -> g e", e=GE)).then_inc(edges_in, 16)
                sp.dma_start(edge_src[NG - 1:NG, 0:TAIL], src[full:E_ALL].rearrange("(g e) -> g e", g=1)).then_inc(edges_in, 16)
                sp.dma_start(edge_dst[0:NG - 1, :], dst[0:full].rearrange("(g e) -> g e", e=GE)).then_inc(edges_in, 16)
                sp.dma_start(edge_dst[NG - 1:NG, 0:TAIL], dst[full:E_ALL].rearrange("(g e) -> g e", g=1)).then_inc(edges_in, 16)
                sp.dma_start(edge_dst[NG - 1:NG, TAIL:GE], dst[E_ALL - (GE - TAIL):E_ALL].rearrange("(g e) -> g e", g=1)).then_inc(edges_in, 16)

            @block.scalar
            def _(act):
                act.wait_ge(zeroed, 1)
                for b in range(FEWEST * TB, UNITS * TB):
                    act.dma_start(y_rows[b * P:(b + 1) * P, :], zeros[:]).then_inc(cleared, 16)
                act.wait_ge(cleared, 16 * (UNITS - FEWEST) * TB)

            @block.gpsimd
            def _(pool):
                pool.memset(zeros[:], 0.0).then_inc(zeroed, 1)
                pool.memset(edge_src[:], -100 * P).then_inc(filled, 1)
                pool.memset(wide[:], 0.0).then_inc(filled, 1)
                pool.iota(count_low[:], pattern=[[1, P]], base=0, channel_multiplier=0,
                          allow_small_or_imprecise_dtypes=True).then_inc(filled, 1)
                pool.iota(count_place[:], pattern=[[1, NP]], base=1, channel_multiplier=0,
                          allow_small_or_imprecise_dtypes=True).then_inc(filled, 1)

            @block.vector
            def _(dve):
                dve.memset(counts[:], 0.0).then_inc(added, 1)
                dve.wait_ge(filled, 4)
                dve.wait_ge(edges_in, 80)
                dve.tensor_scalar(low_i[:], edge_src[:], P - 1, None, ALU.bitwise_and).then_inc(step, 1)
                dve.tensor_scalar(high_i[:], edge_src[:], 7, None, ALU.arith_shift_right).then_inc(step, 1)
                dve.tensor_copy(dst_f[:], edge_dst[:]).then_inc(step, 1)
                dve.wait_ge(step, 3)
                dve.tensor_copy(low_f[:], low_i[:]).then_inc(step, 1)
                dve.tensor_scalar(high_f[:], high_i[:], float(WIN), None, ALU.mult).then_inc(step, 1)
                dve.tensor_reduce(base[:], dst_f[:], AX.X, ALU.min).then_inc(step, 1)
                dve.tensor_reduce(top[:], dst_f[:], AX.X, ALU.max).then_inc(step, 1)
                dve.wait_ge(step, 7)
                dve.tensor_tensor(wide[:, 1, 0:1], top[:], base[:], ALU.subtract).then_inc(step, 1)
                dve.wait_ge(turned, 2)
                dve.tensor_copy(low_t[:], ps_t[2][:, 0:CH * NG].rearrange("p (c g) -> p c g", c=CH)).then_inc(taken, 1)
                dve.tensor_reduce(span[0:1, 0:1], ps_t[1][0:1, 0:NG], AX.X, ALU.max).then_inc(step, 1)
                dve.wait_ge(step, 9)
                dve.tensor_copy(span_i[:], span[0:1, 0:1]).then_inc(step, 1)
                dve.wait_ge(step, 10)
                dve.wait_ge(taken, 1)
                prepare(dve, 10, 4, 3)
                count_pass(dve, 0)
                reach = dve.value_load(span_i[0:1, 0:1], min_val=0, max_val=NPAD)
                with dve.If(reach > WIN - 1):
                    with dve.Fori(1, PASSES) as k:
                        prepare(dve, 10 + 7 * k, 4 + 2 * k, 3 + 2 * k)
                        count_pass(dve, NG * k)

            @block.tensor
            def _(pe):
                pe.wait_ge(step, 8)
                for ch in range(CH):
                    last = pe.transpose(ps_t[2][:, ch * NG:(ch + 1) * NG], low_f[:, ch * P:(ch + 1) * P], c["ident"][0:NG, 0:NG])
                last.then_inc(turned, 1)
                pe.transpose(ps_t[1][:, 0:NG], wide[:, 1, :], c["ident"][0:NG, 0:NG]).then_inc(turned, 1)
                pe.wait_ge(step, 10)
                turn_places(pe, 10, 4)
                multiply_pass(pe, 0)
                reach = pe.value_load(span_i[0:1, 0:1], min_val=0, max_val=NPAD)
                with pe.If(reach > WIN - 1):
                    with pe.Fori(1, PASSES) as k:
                        pe.wait_ge(added, NG * k + 1)
                        turn_places(pe, 10 + 7 * k, 4 + 2 * k)
                        multiply_pass(pe, NG * k)



def count_degrees(nc, c, counts, inverse):
    with Stage(nc, "degrees") as s:
        partial = s.sbuf("degree_partial", [P, NPAD], F32)
        degree = s.psum("ps_degree", [P, 512])
        step, summed = s.sem("degree_step"), s.sem("degree_summed")
        with nc.Block() as block:
            @block.vector
            def _(dve):
                dve.tensor_reduce(partial[:], counts[:, :, 0:NPAD].rearrange("p s d -> p d s"), AX.X,
                                  ALU.add).then_inc(step, 1)
                dve.wait_ge(summed, 1)
                dve.tensor_scalar(inverse[:], degree[:, 0:NT], 1.0, None, ALU.max).then_inc(step, 1)
                dve.wait_ge(step, 2)
                dve.reciprocal(inverse[:], inverse[:]).then_inc(step, 1)

            @block.tensor
            def _(pe):
                pe.wait_ge(step, 1)
                for t in range(NT):
                    last = pe.matmul(degree[:, t:t + 1], partial[:, t * P:(t + 1) * P], c["ones"][:, 0:1],
                                     start=True, stop=True)
                last.then_inc(summed, 1)


class Sage:

    def __init__(self, s):
        self.high = s.sbuf("h_high", [P, NT, D], F32R)
        self.low = s.sbuf("h_low", [P, NT, D], F32R)
        self.w_high = s.sbuf("w_high", [P, 2 * KD, D], F32R)
        self.w_low = s.sbuf("w_low", [P, 2 * KD, D], F32R)
        self.count_tile = [s.sbuf(f"count_tile_{u}", [P, NT, P], F32R) for u in range(2)]
        self.h_tile = [s.sbuf(f"h_tile_{u}", [P, D], F32) for u in range(2)]
        self.mean_tile = [s.sbuf(f"mean_tile_{u}", [P, D], F32) for u in range(2)]
        self.ht_high = [s.sbuf(f"ht_high_{u}", [P, KD, P], F32R) for u in range(2)]
        self.ht_low = [s.sbuf(f"ht_low_{u}", [P, KD, P], F32R) for u in range(2)]
        self.mt_high = [s.sbuf(f"mt_high_{u}", [P, KD, P], F32R) for u in range(2)]
        self.mt_low = [s.sbuf(f"mt_low_{u}", [P, KD, P], F32R) for u in range(2)]
        self.ps_h = s.psum("ps_h", [P, KD, P])
        self.ps_m = s.psum("ps_m", [P, KD, P])
        self.ps_sum = [s.psum(f"ps_sum_{u}", [P, D]) for u in range(2)]
        self.ps_y = [s.psum(f"ps_y_{u}", [P, D]) for u in range(2)]
        self.staged = s.sem("tile_staged")
        self.turned_h = s.sem("h_turned")
        self.summed = s.sem("neighbours_summed")
        self.turned_m = s.sem("mean_turned")
        self.multiplied = s.sem("y_multiplied")
        self.high_h = s.sem("ht_high_ready")
        self.mean = s.sem("mean_ready")
        self.high_m = s.sem("mt_high_ready")
        self.low_h = s.sem("ht_low_ready")
        self.low_m = s.sem("mt_low_ready")
        self.finished = s.sem("y_finished")
        self.seen = s.sem("h_seen")
        self.cut = s.sem("h_cut")

    def pool_tiles(self, pool, counts, h, before, h_ready, h_value):
        pool.wait_ge(h_ready, h_value)
        pool.sem_inc(self.seen, 1)
        with pool.Fori(0, NT // 2) as i:
            for u in range(2):
                n = before + 2 * i + u
                pool.wait_ge(self.summed, n + 1)
                pool.tensor_copy(self.count_tile[u][:], counts[:, :, bass.ds((2 * i + u) * P, P)]).then_inc(self.staged, 1)
                pool.wait_ge(self.turned_h, n + 1)
                pool.tensor_copy(self.h_tile[u][:], h[:, bass.ds(2 * i + u, 1), :].rearrange("p a d -> p (a d)")).then_inc(self.staged, 1)

    def pe_credits(self, pe):
        pe.sem_inc(self.turned_h, 2)
        pe.sem_inc(self.summed, 2)
        pe.sem_inc(self.turned_m, 2)
        pe.sem_inc(self.multiplied, 2)

    def act_credits(self, act):
        act.sem_inc(self.mean, 2)

    def dve_credits(self, dve):
        dve.sem_inc(self.low_h, 1)
        dve.sem_inc(self.low_m, 1)
        dve.sem_inc(self.finished, 2)

    def pe_gather(self, pe, c, n, u):
        pe.wait_ge(self.staged, 2 * n + 2)
        pe.wait_ge(self.low_h, n + 1)
        for k in range(KD):
            last = pe.transpose(self.ps_h[:, k, :], self.h_tile[u][:, k * P:(k + 1) * P], c["ident"][:])
        last.then_inc(self.turned_h, 1)
        pe.wait_ge(self.mean, n + 1)
        for j in range(NT):
            for part, h in enumerate((self.high, self.low)):
                last = pe.matmul(self.ps_sum[u][:], self.count_tile[u][:, j, :], h[:, j, :],
                                 start=(j == 0 and part == 0), stop=(j == NT - 1 and part == 1))
        last.then_inc(self.summed, 1)

    def products(self, pe, u, high, low, first, start, stop):
        for k in range(KD):
            w = first + k
            pe.matmul(self.ps_y[u][:], high[:, k, :], self.w_high[:, w, :], start=(start and k == 0), stop=False)
            pe.matmul(self.ps_y[u][:], high[:, k, :], self.w_low[:, w, :], start=False, stop=False)
            last = pe.matmul(self.ps_y[u][:], low[:, k, :], self.w_high[:, w, :], start=False,
                             stop=(stop and k == KD - 1))
        return last

    def pe_tile(self, pe, c, n, u, more):
        pe.wait_ge(self.low_h, n + 2)
        pe.wait_ge(self.finished, n + 1)
        self.products(pe, u, self.ht_high[u], self.ht_low[u], 0, True, False)
        pe.wait_ge(self.mean, n + 3)
        pe.wait_ge(self.low_m, n + 1)
        for k in range(KD):
            last = pe.transpose(self.ps_m[:, k, :], self.mean_tile[u][:, k * P:(k + 1) * P], c["ident"][:])
        last.then_inc(self.turned_m, 1)
        if more:
            self.pe_gather(pe, c, n + 1, 1 - u)
        pe.wait_ge(self.low_m, n + 2)
        self.products(pe, u, self.mt_high[u], self.mt_low[u], KD, False, True).then_inc(self.multiplied, 1)

    def pe_tiles(self, pe, c, before, cuts):
        pe.wait_ge(self.cut, cuts)
        self.pe_gather(pe, c, before, 0)
        with pe.Fori(0, NT // 2 - 1) as i:
            for u in range(2):
                self.pe_tile(pe, c, before + 2 * i + u, u, True)
        self.pe_tile(pe, c, before + NT - 2, 0, True)
        self.pe_tile(pe, c, before + NT - 1, 1, False)

    def act_tiles(self, act, inverse, before):
        with act.Fori(0, NT // 2) as i:
            for u in range(2):
                n = before + 2 * i + u
                act.wait_ge(self.turned_h, n + 3)
                act.wait_ge(self.multiplied, n + 1)
                act.copy(self.ht_high[u][:], self.ps_h[:]).then_inc(self.high_h, 1)
                act.wait_ge(self.summed, n + 3)
                act.wait_ge(self.turned_m, n + 1)
                act.activation(self.mean_tile[u][:], self.ps_sum[u][:], ACT.Copy,
                               scale=inverse[:, bass.ds(2 * i + u, 1)]).then_inc(self.mean, 1)
                act.wait_ge(self.turned_m, n + 3)
                act.copy(self.mt_high[u][:], self.ps_m[:]).then_inc(self.high_m, 1)

    def dve_tiles(self, dve, before, finish):
        with dve.Fori(0, NT // 2) as i:
            for u in range(2):
                n = before + 2 * i + u
                dve.wait_ge(self.high_h, n + 1)
                dve.tensor_tensor(self.ht_low[u][:], self.ps_h[:], self.ht_high[u][:].bitcast(F32),
                                  ALU.subtract).then_inc(self.low_h, 1)
                dve.wait_ge(self.high_m, n + 1)
                dve.tensor_tensor(self.mt_low[u][:], self.ps_m[:], self.mt_high[u][:].bitcast(F32),
                                  ALU.subtract).then_inc(self.low_m, 1)
                dve.wait_ge(self.multiplied, n + 3)
                finish(dve, 2 * i + u, n, u).then_inc(self.finished, 1)


def sage_layer(nc, c, w, h, x, counts, inverse):
    with Stage(nc, "sage") as s:
        g = Sage(s)
        natural = s.sbuf("w_natural", [P, KD, 2 * D], F32)
        loaded, turned, w_high, w_low = s.sem("w_loaded"), s.sem("w_turned"), s.sem("w_high_cut"), s.sem("w_low_cut")
        with nc.Block() as block:
            @block.sync
            def _(sp):
                sp.dma_start(natural[:], w.rearrange("(o p) f -> p o f", p=P)).then_inc(loaded, 16)

            @block.gpsimd
            def _(pool):
                pool.wait_ge(g.cut, 1)
                g.pool_tiles(pool, counts, h, 0, g.cut, 1)

            @block.scalar
            def _(act):
                g.act_credits(act)
                act.copy(g.high[:], h[:]).then_inc(g.cut, 1)
                for k in range(2 * KD):
                    act.wait_ge(turned, k + 1)
                    act.copy(g.w_high[:, k, :], g.ps_y[k % 2][:]).then_inc(w_high, 1)
                act.wait_ge(w_high, 2 * KD)
                act.sem_inc(g.cut, 1)
                g.act_tiles(act, inverse, 0)

            @block.vector
            def _(dve):
                g.dve_credits(dve)
                dve.wait_ge(g.cut, 1)
                dve.tensor_tensor(g.low[:], h[:], g.high[:].bitcast(F32), ALU.subtract).then_inc(w_low, 1)
                for k in range(2 * KD):
                    dve.wait_ge(w_high, k + 1)
                    dve.tensor_tensor(g.w_low[:, k, :], g.ps_y[k % 2][:], g.w_high[:, k, :].bitcast(F32),
                                      ALU.subtract).then_inc(w_low, 1)
                dve.wait_ge(w_low, 2 * KD + 1)
                dve.sem_inc(g.cut, 2)

                def finish(dve, t, n, u):
                    at = x[:, bass.ds(t, 1), :].rearrange("p a d -> p (a d)")
                    return dve.scalar_tensor_tensor(at, g.ps_y[u][:], 0.0, at, ALU.max, ALU.add)

                g.dve_tiles(dve, 0, finish)

            @block.tensor
            def _(pe):
                g.pe_credits(pe)
                pe.wait_ge(loaded, 16)
                for k in range(2 * KD):
                    if k >= 2:
                        pe.wait_ge(w_low, k)
                    for o in range(KD):
                        last = pe.transpose(g.ps_y[k % 2][:, o * P:(o + 1) * P], natural[:, o, k * P:(k + 1) * P], c["ident"][:])
                    last.then_inc(turned, 1)
                g.pe_tiles(pe, c, 0, 4)


def graph_layers(nc, c, ws, wn, bs, h, counts, inverse):
    L = ws.shape[0]
    with Stage(nc, "layers") as s:
        g = Sage(s)
        w = s.sbuf("w_whole", [P, 2 * KD, D], F32)
        bias = s.sbuf("layer_bias", [P, L, D], F32)
        floor = s.sbuf("relu_floor", [P, L], F32)
        y = s.sbuf("y_with_bias", [P, 2, D], F32)
        loaded, used, biased, extra = s.sem("w_loaded"), s.sem("w_used"), s.sem("y_biased"), s.sem("layer_extra")
        with nc.Block() as block:
            @block.sync
            def _(sp):
                sp.dma_start(bias[:], bs.rearrange("l d -> (l d)").partition_broadcast(P)).then_inc(extra, 16)
                with sp.Fori(0, L) as l:
                    sp.wait_ge(used, 2 * l + 2)
                    sp.dma_start(w[:, 0:KD, :], ws[bass.ds(l, 1), :, :].rearrange("l (k p) d -> p (l k) d", p=P)).then_inc(loaded, 16)
                    sp.dma_start(w[:, KD:2 * KD, :], wn[bass.ds(l, 1), :, :].rearrange("l (k p) d -> p (l k) d", p=P)).then_inc(loaded, 16)

            @block.gpsimd
            def _(pool):
                pool.memset(floor[:, 0:L - 1], 0.0).then_inc(extra, 1)
                pool.memset(floor[:, L - 1:L], -3.4e38).then_inc(extra, 1)
                with pool.Fori(0, L) as l:
                    g.pool_tiles(pool, counts, h, l * NT, g.cut, 4 * l + 4)

            @block.scalar
            def _(act):
                g.act_credits(act)
                act.sem_inc(used, 1)
                with act.Fori(0, L) as l:
                    act.wait_ge(g.finished, l * NT + 2)
                    act.copy(g.high[:], h[:]).then_inc(g.cut, 1)
                    act.wait_ge(loaded, 32 * l + 32)
                    act.copy(g.w_high[:], w[:]).then_inc(g.cut, 1)
                    act.wait_ge(g.cut, 4 * l + 4)
                    act.sem_inc(used, 1)
                    g.act_tiles(act, inverse, l * NT)

            @block.vector
            def _(dve):
                g.dve_credits(dve)
                dve.sem_inc(used, 1)
                dve.wait_ge(extra, 18)
                with dve.Fori(0, L) as l:
                    dve.wait_ge(g.cut, 4 * l + 2)
                    dve.tensor_tensor(g.low[:], h[:], g.high[:].bitcast(F32), ALU.subtract).then_inc(g.cut, 1)
                    dve.tensor_tensor(g.w_low[:], w[:], g.w_high[:].bitcast(F32), ALU.subtract).then_inc(g.cut, 1)
                    dve.wait_ge(g.cut, 4 * l + 4)
                    dve.sem_inc(used, 1)

                    def finish(dve, t, n, u):
                        dve.tensor_tensor(y[:, u, :], g.ps_y[u][:], bias[:, bass.ds(l, 1), :].rearrange("p a d -> p (a d)"),
                                          ALU.add).then_inc(biased, 1)
                        dve.wait_ge(biased, n + 1)
                        return dve.tensor_scalar(h[:, bass.ds(t, 1), :].rearrange("p a d -> p (a d)"), y[:, u, :],
                                                 floor[:, bass.ds(l, 1)], None, ALU.max)

                    g.dve_tiles(dve, l * NT, finish)

            @block.tensor
            def _(pe):
                g.pe_credits(pe)
                with pe.Fori(0, L) as l:
                    g.pe_tiles(pe, c, l * NT, 4 * l + 4)


def scale_shift(nc, ln_g, ln_b, h, target, nodes, rows):
    with Stage(nc, "affine") as s:
        gain = s.sbuf("gain", [P, D], F32)
        shift = s.sbuf("shift", [P, D], F32)
        loaded, step, stored = s.sem("loaded"), s.sem("step"), s.sem("stored")
        with nc.Block() as block:
            @block.sync
            def _(sp):
                sp.dma_start(gain[:], ln_g.partition_broadcast(P)).then_inc(loaded, 16)
                sp.dma_start(shift[:], ln_b.partition_broadcast(P)).then_inc(loaded, 16)
                sp.wait_ge(step, 2)
                sp.dma_start(by_tile(rows), target[:]).then_inc(stored, 16)
                sp.wait_ge(stored, 16)

            @block.vector
            def _(dve):
                dve.wait_ge(loaded, 32)
                dve.tensor_tensor(target[:], target[:], gain[:].unsqueeze(1).to_broadcast([P, NT, D]), ALU.mult).then_inc(step, 1)
                dve.wait_ge(step, 1)
                dve.tensor_tensor(target[:], target[:], shift[:].unsqueeze(1).to_broadcast([P, NT, D]), ALU.add).then_inc(step, 1)
                dve.tensor_tensor(nodes[:], nodes[:], h[:], ALU.add).then_inc(step, 1)


def router_logits(nc, c, tag, h, w, b, E, logits):
    with Stage(nc, tag) as s:
        w_rows = s.sbuf("w_rows", [E, D], F32)
        w_t = s.sbuf("w_t", [P, KD, E], F32)
        bias = s.sbuf("bias", [P, E], F32)
        tile = [s.sbuf(f"tile_{u}", [P, D], F32) for u in range(2)]
        tile_t = [s.sbuf(f"tile_t_{u}", [P, KD, P], F32) for u in range(2)]
        ps_w = s.psum("ps_w", [P, 512])
        ps_t = [s.psum(f"ps_t_{u}", [P, KD, P]) for u in range(2)]
        ps_l = [s.psum(f"ps_l_{u}", [P, 512]) for u in range(2)]
        loaded, w_turned, w_ready = s.sem("loaded"), s.sem("w_turned"), s.sem("w_ready")
        staged = s.sem("staged")
        turned = s.sem("turned")
        taken = s.sem("taken")
        product = s.sem("product")
        done = s.sem("done")
        with nc.Block() as block:
            @block.sync
            def _(sp):
                sp.dma_start(w_rows[:], w).then_inc(loaded, 16)
                sp.dma_start(bias[:], b.partition_broadcast(P)).then_inc(loaded, 16)

            @block.gpsimd
            def _(pool):
                with pool.Fori(0, NT // 2) as i:
                    for u in range(2):
                        pool.wait_ge(turned, 2 * i + u + 1)
                        pool.tensor_copy(tile[u][:], h[:, bass.ds(2 * i + u, 1), :].rearrange("p a d -> p (a d)")).then_inc(staged, 1)

            @block.scalar
            def _(act):
                act.sem_inc(taken, 2)
                with act.Fori(0, NT // 2) as i:
                    for u in range(2):
                        act.wait_ge(turned, 2 * i + u + 3)
                        act.wait_ge(product, 2 * i + u + 1)
                        act.copy(tile_t[u][:], ps_t[u][:]).then_inc(taken, 1)

            @block.vector
            def _(dve):
                dve.sem_inc(done, 2)
                dve.wait_ge(w_turned, 1)
                dve.wait_ge(loaded, 32)
                dve.tensor_copy(w_t[:], ps_w[:, 0:KD * E].rearrange("p (k e) -> p k e", e=E)).then_inc(w_ready, 1)
                with dve.Fori(0, NT // 2) as i:
                    for u in range(2):
                        dve.wait_ge(product, 2 * i + u + 3)
                        dve.tensor_tensor(logits[:, bass.ds(2 * i + u, 1), :].rearrange("p a e -> p (a e)"), ps_l[u][:, 0:E], bias[:], ALU.add).then_inc(done, 1)

            @block.tensor
            def _(pe):
                pe.sem_inc(turned, 2)
                pe.sem_inc(product, 2)
                pe.wait_ge(loaded, 32)
                for k in range(KD):
                    last = pe.transpose(ps_w[:, k * E:(k + 1) * E], w_rows[:, k * P:(k + 1) * P], c["ident"][0:E, 0:E])
                last.then_inc(w_turned, 1)
                pe.wait_ge(w_ready, 1)
                with pe.Fori(0, NT // 2) as i:
                    for u in range(2):
                        n = 2 * i + u
                        pe.wait_ge(staged, n + 1)
                        pe.wait_ge(taken, n + 1)
                        for k in range(KD):
                            last = pe.transpose(ps_t[u][:, k, :], tile[u][:, k * P:(k + 1) * P], c["ident"][:])
                        last.then_inc(turned, 1)
                        pe.wait_ge(taken, n + 3)
                        pe.wait_ge(done, n + 1)
                        for k in range(KD):
                            last = pe.matmul(ps_l[u][:, 0:E], tile_t[u][:, k, :], w_t[:, k, :], start=(k == 0), stop=(k == KD - 1))
                        last.then_inc(product, 1)


def rank_tokens(nc, c, tag, member, E, rank, total):
    with Stage(nc, tag) as s:
        ps = s.psum("ps_ranks", [P, 2, 256])
        step, summed = s.sem("step"), s.sem("summed")
        flat = member[:].rearrange("p t e -> p (t e)")
        before = s.sbuf("before", [P, NT, E], F32)
        W = NT * E
        with nc.Block() as block:
            @block.tensor
            def _(pe):
                pe.matmul(ps[:, 0, 0:W], c["upper"][:], flat, start=True, stop=True).then_inc(summed, 1)
                pe.matmul(ps[:, 1, 0:W], c["ones"][:], flat, start=True, stop=True).then_inc(summed, 1)

            @block.vector
            def _(dve):
                whole = ps[:, 1, 0:W].rearrange("p (t e) -> p t e", e=E)
                dve.memset(before[:, 0, :], 0.0).then_inc(step, 1)
                dve.wait_ge(summed, 2)
                for t in range(1, NT):
                    dve.wait_ge(step, t)
                    dve.tensor_tensor(before[:, t, :], whole[:, t - 1, :], before[:, t - 1, :], ALU.add).then_inc(step, 1)
                dve.wait_ge(step, NT)
                dve.tensor_tensor(total[:], whole[:, NT - 1, :], before[:, NT - 1, :], ALU.add).then_inc(step, 1)
                dve.tensor_tensor(rank[:], ps[:, 0, 0:W].rearrange("p (t e) -> p t e", e=E), before[:], ALU.add).then_inc(step, 1)


def choose(dve, step, at, logits, best, where):
    for t in range(NT):
        dve.max(best[:, t, :], logits[:, t, :]).then_inc(step, 1)
    for t in range(NT):
        dve.wait_ge(step, at + t + 1)
        dve.max_index(where[:, t, :], best[:, t, :], logits[:, t, :]).then_inc(step, 1)


def store_list(nc, tag, ids, node, slots, columns):
    n_rows = ids.shape[0]
    with Stage(nc, tag) as s:
        zeros = s.sbuf("zeros", [n_rows // P, P], I32)
        filled, stored = s.sem("filled"), s.sem("stored")
        with nc.Block() as block:
            @block.gpsimd
            def _(pool):
                pool.memset(zeros[:], 0).then_inc(filled, 1)
                pool.wait_ge(filled, 1)
                pool.dma_start(ids.rearrange("(c p) o -> c (p o)", p=P), zeros[:]).then_inc(stored, 16)
                pool.wait_ge(stored, 16)
                for i in range(columns):
                    t = i % NT
                    real = P if t < NT - 1 else LAST
                    pool.indirect_dma_start(ids, bass.IndirectOffsetOnAxis(ap=slots[0:real, i:i + 1], axis=0),
                                            node[0:real, t:t + 1], None).then_inc(stored, 16)
                pool.wait_ge(stored, 16 * (columns + 1))


def load_list(nc, c, tag, ids, list_t):
    blocks = ids.shape[0] // P
    with Stage(nc, tag) as s:
        rows_i = s.sbuf("rows_i", [blocks, P], I32)
        rows = s.sbuf("rows", [blocks, P], F32)
        ps = s.psum("ps", [P, 512])
        loaded, step, turned = s.sem("loaded"), s.sem("step"), s.sem("turned")
        with nc.Block() as block:
            @block.sync
            def _(sp):
                sp.dma_start(rows_i[:], ids.rearrange("(c p) o -> c (p o)", p=P)).then_inc(loaded, 16)

            @block.vector
            def _(dve):
                dve.wait_ge(loaded, 16)
                dve.tensor_copy(rows[:], rows_i[:]).then_inc(step, 1)
                dve.wait_ge(turned, 1)
                dve.tensor_copy(list_t[:], ps[:, 0:blocks]).then_inc(step, 1)

            @block.tensor
            def _(pe):
                pe.wait_ge(step, 1)
                pe.transpose(ps[:, 0:blocks], rows[:], c["ident"][0:blocks, 0:blocks]).then_inc(turned, 1)


def route_top2(nc, c, h, w_r, b_r, ids, gates, slots, unit_expert, n_units, list_t):
    E = E1
    with Stage(nc, "top2") as s:
        logits = s.sbuf("logits", [P, NT, E], F32)
        best = s.sbuf("best", [P, NT, 8], F32)
        where = s.sbuf("where", [P, NT, 8], U32)
        column = s.sbuf("expert_column", [P, NT, E], F32)
        chosen = s.sbuf("chosen", [P, 2, NT], F32)
        one = [s.sbuf(f"onehot_{k}", [P, NT, E], F32) for k in range(2)]
        member = s.sbuf("member", [P, NT, E], F32)
        rank = s.sbuf("rank", [P, NT, E], F32)
        total = s.sbuf("total", [P, E], F32)
        gap = s.sbuf("gap", [P, NT], F32)
        small = s.sbuf("small_exp", [P, NT], F32)
        started, step, risen = s.sem("started"), s.sem("step"), s.sem("risen")
        router_logits(nc, c, "logits2", h, w_r, b_r, E, logits)
        with nc.Block() as block:
            @block.gpsimd
            def _(pool):
                pool.iota(column[:], pattern=[[0, NT], [1, E]], base=0, channel_multiplier=0,
                          allow_small_or_imprecise_dtypes=True).then_inc(started, 1)

            @block.vector
            def _(dve):
                choose(dve, step, 0, logits, best, where)
                n = 2 * NT
                dve.wait_ge(step, n)
                dve.tensor_tensor(gap[:], best[:, :, 1], best[:, :, 0], ALU.subtract).then_inc(step, 1)
                for k in range(2):
                    dve.tensor_copy(chosen[:, k, :], where[:, :, k]).then_inc(step, 1)
                dve.wait_ge(step, n + 3)
                dve.wait_ge(started, 1)
                for k in range(2):
                    dve.tensor_tensor(one[k][:], column[:], chosen[:, k, :].unsqueeze(2).to_broadcast([P, NT, E]),
                                      ALU.is_equal).then_inc(step, 1)
                dve.wait_ge(step, n + 5)
                dve.tensor_tensor(member[:], one[0][:], one[1][:], ALU.add).then_inc(step, 1)
                dve.wait_ge(step, n + 6)
                dve.tensor_tensor(member[:], member[:], c["real"][:].unsqueeze(2).to_broadcast([P, NT, E]), ALU.mult).then_inc(step, 1)
                dve.wait_ge(risen, 1)
                dve.tensor_scalar(gates[:, 0, :], small[:], 1.0, None, ALU.add).then_inc(step, 1)
                dve.wait_ge(step, n + 8)
                dve.reciprocal(gates[:, 0, :], gates[:, 0, :]).then_inc(step, 1)
                dve.wait_ge(step, n + 9)
                dve.tensor_tensor(gates[:, 1, :], gates[:, 0, :], small[:], ALU.mult).then_inc(step, 1)

            @block.scalar
            def _(act):
                act.wait_ge(step, 2 * NT + 1)
                act.activation(small[:], gap[:], ACT.Exp).then_inc(risen, 1)
        rank_tokens(nc, c, "rank2", member, E, rank, total)
        units = s.sbuf("units", [P, E], F32)
        above = s.sbuf("above", [P, E], F32)
        ends = s.sbuf("unit_ends", [P, E], F32)
        starts = s.sbuf("unit_starts", [P, E], F32)
        ones = s.sbuf("ones_e", [P, E], F32)
        product = s.sbuf("product", [P, NT, E], F32)
        slot = s.sbuf("slot", [P, 2, NT], F32)
        unit_no = s.sbuf("unit_no", [1, UNITS + 1, E], F32)
        passed = s.sbuf("units_passed", [1, UNITS + 1], F32)
        with nc.Block() as block:
            step, began = s.sem("slot_step"), s.sem("slot_began")

            @block.gpsimd
            def _(pool):
                pool.iota(unit_no[:], pattern=[[1, UNITS + 1], [0, E]], base=0, channel_multiplier=0,
                          allow_small_or_imprecise_dtypes=True).then_inc(began, 1)
                pool.memset(ones[:], 1.0).then_inc(began, 1)

            @block.vector
            def _(dve):
                dve.wait_ge(began, 2)
                dve.tensor_scalar(units[:], total[:], 0.0, None, ALU.is_gt).then_inc(step, 1)
                n = 1
                for b in range(1, -(-N // T)):
                    dve.tensor_scalar(above[:], total[:], float(b * T), None, ALU.is_gt).then_inc(step, 1)
                    dve.wait_ge(step, n + 1)
                    dve.tensor_tensor(units[:], units[:], above[:], ALU.add).then_inc(step, 1)
                    n += 2
                    dve.wait_ge(step, n)
                dve.tensor_tensor_scan(ends[:], ones[:], units[:], 0.0, ALU.mult, ALU.add).then_inc(step, 1)
                dve.wait_ge(step, n + 1)
                dve.tensor_tensor(starts[:], ends[:], units[:], ALU.subtract).then_inc(step, 1)
                dve.wait_ge(step, n + 2)
                dve.tensor_scalar(starts[:], starts[:], float(T), None, ALU.mult).then_inc(step, 1)
                dve.wait_ge(step, n + 3)
                dve.tensor_tensor(rank[:], rank[:], starts[:].unsqueeze(1).to_broadcast([P, NT, E]), ALU.add).then_inc(step, 1)
                n += 4
                dve.wait_ge(step, n)
                for k in range(2):
                    dve.tensor_tensor(product[:], one[k][:], rank[:], ALU.mult).then_inc(step, 1)
                    dve.wait_ge(step, n + 1)
                    dve.tensor_reduce(slot[:, k, :], product[:], AX.X, ALU.add).then_inc(step, 1)
                    dve.wait_ge(step, n + 2)
                    dve.tensor_tensor(slots[:, k * NT:(k + 1) * NT], slot[:, k, :], c["real"][:], ALU.mult).then_inc(step, 1)
                    n += 3
                dve.tensor_tensor(unit_no[:], unit_no[:], ends[0:1, :].unsqueeze(1).to_broadcast([1, UNITS + 1, E]), ALU.is_ge).then_inc(step, 1)
                dve.wait_ge(step, n + 1)
                dve.tensor_reduce(passed[:], unit_no[:], AX.X, ALU.add).then_inc(step, 1)
                dve.wait_ge(step, n + 2)
                dve.tensor_scalar(unit_expert[:], passed[:], float(E - 1), None, ALU.min).then_inc(step, 1)
                dve.tensor_copy(n_units[:], ends[0:1, E - 1:E]).then_inc(step, 1)
        store_list(nc, "list2", ids, c["node"], slots, 2 * NT)
        load_list(nc, c, "loadlist2", ids, list_t)


def top2_experts(nc, c, rows, W1, b1, W2, b2, unit_expert, n_units, list_t, y_rows):
    NB = TB
    with Stage(nc, "ffn") as s:
        index_seen = s.sem("index_seen")
        raw1 = [s.sbuf(f"w1_raw_{u}", [P, KD, FB], F32) for u in range(2)]
        raw2 = [s.sbuf(f"w2_raw_{u}", [P, KD, D], F32) for u in range(2)]
        w1h = [s.sbuf(f"w1_high_{u}", [P, KD, FB], F32R) for u in range(2)]
        w1l = [s.sbuf(f"w1_low_{u}", [P, KD, FB], F32R) for u in range(2)]
        w2h = [s.sbuf(f"w2_high_{u}", [P, KD, D], F32R) for u in range(2)]
        w2l = [s.sbuf(f"w2_low_{u}", [P, KD, D], F32R) for u in range(2)]
        token = [s.sbuf(f"token_{j}", [P, D], F32) for j in range(NB)]
        index = [s.sbuf(f"index_{j}", [P, 1], I32) for j in range(NB)]
        xh = s.sbuf("x_high", [P, KD, T], F32R)
        xl = s.sbuf("x_low", [P, KD, T], F32R)
        hid = s.sbuf("hidden", [P, KD, T], F32)
        hh = s.sbuf("hidden_high", [P, KD, T], F32R)
        hl = s.sbuf("hidden_low", [P, KD, T], F32R)
        y = s.sbuf("y", [P, NB, D], F32)
        bias1_rows = s.sbuf("b1_rows", [P, P], F32)
        bias1 = s.sbuf("b1_t", [P, E1 * F1 // P], F32)
        bias2 = s.sbuf("b2", [P, E1, D], F32)
        ps_h = [s.psum(f"ps_hidden_{u}", [P, 512]) for u in range(2)]
        ps_y = [s.psum(f"ps_y_{j}", [P, D]) for j in range(NB)]
        ps_x = s.psum("ps_x", [P, KD, P])
        biases, turned_b, biases_t = s.sem("biases"), s.sem("b1_turned"), s.sem("b1_ready")
        loaded = [s.sem(f"w_loaded_{u}") for u in range(2)]
        gathered = [s.sem(f"gathered_{j}") for j in range(NB)]
        index_set = s.sem("index_set")
        w_high = s.sem("w_high")
        w_low = s.sem("w_low")
        turned = s.sem("x_turned")
        x_high = s.sem("x_high_ready")
        x_low = s.sem("x_low_ready")
        first = s.sem("first_product")
        gelu = s.sem("gelu_done")
        h_high = s.sem("hidden_high_ready")
        h_low = s.sem("hidden_low_ready")
        second = s.sem("second_product")
        biased = s.sem("y_biased")
        stored = s.sem("y_stored")
        all_stored = s.sem("all_stored")

        def each_unit(eng, body):
            units = eng.value_load(n_units[0:1, 0:1], min_val=0, max_val=UNITS)
            with eng.Fori(0, UNITS) as v:
                with eng.If(units > v):
                    body(v)
            return units

        def expert_of(eng, v):
            return eng.value_load(unit_expert[0:1, bass.ds(v, 1)], min_val=0, max_val=E1 - 1)

        with nc.Block() as block:
            @block.sync
            def _(sp):
                sp.dma_start(bias1_rows[:], b1.rearrange("e (c f) -> (e c) f", f=P)).then_inc(biases, 16)
                sp.dma_start(bias2[:], b2.rearrange("e d -> (e d)").partition_broadcast(P)).then_inc(biases, 16)

                def load(e, f, n):
                    u = f % 2
                    sp.wait_ge(w_low, 2 * n + 2)
                    sp.dma_start(raw1[u][:], W1[bass.ds(e, 1), :, f * FB:(f + 1) * FB].rearrange("e (k p) f -> p (e k) f", p=P)).then_inc(loaded[u], 16)
                    sp.dma_start(raw2[u][:], W2[bass.ds(e, 1), f * FB:(f + 1) * FB, :].rearrange("e (k p) d -> p (e k) d", p=P)).then_inc(loaded[u], 16)

                load(expert_of(sp, 0), 0, 0)

                def unit(v):
                    e = expert_of(sp, v)
                    for f in range(1, NFB):
                        load(e, f, NFB * v + f)
                    load(expert_of(sp, v + 1), 0, NFB * v + NFB)
                    sp.wait_ge(biased, NB * v + 2 * NB)
                    sp.dma_start(y_rows[bass.ds(v * T, T), :].rearrange("(j p) d -> p j d", p=P), y[:]).then_inc(stored, 16)

                units = each_unit(sp, unit)
                sp.wait_ge(stored, 16 * units + 16)
                sp.sem_inc(all_stored, 1)

            @block.gpsimd
            def _(pool):
                def unit(v):
                    for j in range(NB):
                        pool.wait_ge(turned, NB * v + j + 1)
                        pool.tensor_copy(index[j][:], list_t[:, bass.ds(NB * v + j, 1)]).then_inc(index_set, 1)
                        pool.wait_ge(index_set, NB * v + j + 1)
                        pool.sem_inc(index_seen, 1)
                        pool.indirect_dma_start(token[j][:], None, rows, bass.IndirectOffsetOnAxis(ap=index[j][:, 0:1], axis=0)).then_inc(gathered[j], 16)

                each_unit(pool, unit)

            @block.scalar
            def _(act):
                act.sem_inc(gelu, 2)

                act.wait_ge(loaded[0], 32)
                act.copy(w1h[0][:], raw1[0][:]).then_inc(w_high, 1)
                act.copy(w2h[0][:], raw2[0][:]).then_inc(w_high, 1)
                act.wait_ge(biases_t, 1)

                def unit(v):
                    e = expert_of(act, v)
                    for j in range(NB):
                        act.wait_ge(turned, NB * v + j + 1 + NB)
                        if j == 0:
                            act.wait_ge(second, 4 * NFB * v + 4)
                        act.copy(xh[:, :, j * P:(j + 1) * P], ps_x[:]).then_inc(x_high, 1)
                    for f in range(NFB):
                        n = NFB * v + f
                        nu = (f + 1) % 2
                        times = 2 * v + (f + 1) // 2
                        for m in range(KD):
                            q = 4 * n + m
                            act.wait_ge(first, q + 1)
                            act.wait_ge(h_low, q + 1)
                            act.activation(hid[:, m, :], ps_h[m % 2][:, 0:T], ACT.Gelu,
                                           bias=bias1[:, bass.ds(e * (F1 // P) + f * KD + m, 1)]).then_inc(gelu, 1)
                            act.wait_ge(gelu, q + 3)
                            act.wait_ge(second, q + 1)
                            act.copy(hh[:, m, :], hid[:, m, :]).then_inc(h_high, 1)
                            if m < 2:
                                act.wait_ge(loaded[nu], 32 * times + 32)
                                act.wait_ge(second, 4 * n + 4)
                                raw, high = ((raw1, w1h), (raw2, w2h))[m]
                                act.copy(high[nu][:], raw[nu][:]).then_inc(w_high, 1)

                each_unit(act, unit)

            @block.vector
            def _(dve):
                dve.sem_inc(w_low, 4)
                dve.sem_inc(x_low, 1)
                dve.sem_inc(h_low, 4)
                dve.sem_inc(biased, NB)
                dve.sem_inc(stored, 16)

                def cut(n, part, u):
                    raw, high, low = ((raw1, w1h, w1l), (raw2, w2h, w2l))[part]
                    dve.wait_ge(w_high, 2 * n + part + 1)
                    dve.tensor_tensor(low[u][:], raw[u][:], high[u][:].bitcast(F32), ALU.subtract).then_inc(w_low, 1)

                cut(0, 0, 0)
                cut(0, 1, 0)
                dve.wait_ge(turned_b, 1)
                dve.tensor_copy(bias1[:], ps_x[:, 0, :]).then_inc(biases_t, 1)
                dve.wait_ge(biases, 32)

                def unit(v):
                    e = expert_of(dve, v)
                    for j in range(NB):
                        dve.wait_ge(x_high, NB * v + j + 1)
                        dve.tensor_tensor(xl[:, :, j * P:(j + 1) * P], ps_x[:], xh[:, :, j * P:(j + 1) * P].bitcast(F32),
                                          ALU.subtract).then_inc(x_low, 1)
                    for f in range(NFB):
                        n = NFB * v + f
                        for m in range(KD):
                            q = 4 * n + m
                            dve.wait_ge(h_high, q + 1)
                            dve.tensor_tensor(hl[:, m, :], hid[:, m, :], hh[:, m, :].bitcast(F32), ALU.subtract).then_inc(h_low, 1)
                            if m < 2:
                                cut(n + 1, m, (f + 1) % 2)
                    dve.wait_ge(second, 4 * NFB * (v + 1) + 4)
                    dve.wait_ge(stored, 16 * v + 16)
                    for j in range(NB):
                        dve.tensor_tensor(y[:, j, :], ps_y[j][:], bias2[:, bass.ds(e, 1), :].rearrange("p a d -> p (a d)"),
                                          ALU.add).then_inc(biased, 1)

                each_unit(dve, unit)

            @block.tensor
            def _(pe):
                pe.sem_inc(turned, NB)
                pe.sem_inc(second, 4)
                pe.wait_ge(biases, 32)
                pe.transpose(ps_x[:, 0, :], bias1_rows[:], c["ident"][:]).then_inc(turned_b, 1)
                pe.wait_ge(biases_t, 1)

                def unit(v):
                    for j in range(NB):
                        pe.wait_ge(gathered[j], 16 * v + 16)
                        pe.wait_ge(x_low, NB * v + j + 1)
                        for k in range(KD):
                            last = pe.transpose(ps_x[:, k, :], token[j][:, k * P:(k + 1) * P], c["ident"][:])
                        last.then_inc(turned, 1)
                    pe.wait_ge(x_low, NB * v + NB + 1)
                    for f in range(NFB):
                        n = NFB * v + f
                        u = f % 2
                        pe.wait_ge(w_low, 2 * n + 2 + 4)
                        for m in range(KD):
                            q = 4 * n + m
                            pe.wait_ge(gelu, q + 1)
                            out = ps_h[m % 2][:, 0:T]
                            for k in range(KD):
                                cols = slice(m * P, (m + 1) * P)
                                pe.matmul(out, w1h[u][:, k, cols], xh[:, k, :], start=(k == 0), stop=False)
                                pe.matmul(out, w1h[u][:, k, cols], xl[:, k, :], start=False, stop=False)
                                last = pe.matmul(out, w1l[u][:, k, cols], xh[:, k, :], start=False, stop=(k == KD - 1))
                            last.then_inc(first, 1)
                        for m in range(KD):
                            q = 4 * n + m
                            pe.wait_ge(h_low, q + 5)
                            if f == 0 and m == 0:
                                pe.wait_ge(biased, NB * v + NB)
                            for j in range(NB):
                                cols = slice(j * P, (j + 1) * P)
                                pe.matmul(ps_y[j][:], hh[:, m, cols], w2h[u][:, m, :], start=(f == 0 and m == 0), stop=False)
                                pe.matmul(ps_y[j][:], hh[:, m, cols], w2l[u][:, m, :], start=False, stop=False)
                                last = pe.matmul(ps_y[j][:], hl[:, m, cols], w2h[u][:, m, :], start=False,
                                                 stop=(f == NFB - 1 and m == KD - 1))
                            last.then_inc(second, 1)

                each_unit(pe, unit)


def gather_top2(nc, c, y_rows, slots, gates, nodes):
    with Stage(nc, "mix") as s:
        index_seen = s.sem("index_seen")
        index = [s.sbuf(f"index_{k}", [P, 1], I32) for k in range(2)]
        y = [s.sbuf(f"y_{k}", [P, D], F32) for k in range(2)]
        index_set = s.sem("index_set")
        gathered = [s.sem(f"gathered_{k}") for k in range(2)]
        mixed = s.sem("mixed")
        with nc.Block() as block:
            @block.gpsimd
            def _(pool):
                with pool.Fori(0, NT) as t:
                    for k in range(2):
                        pool.wait_ge(mixed, 2 * t + k + 1)
                        pool.tensor_copy(index[k][:], slots[:, bass.ds(k * NT + t, 1)]).then_inc(index_set, 1)
                        pool.wait_ge(index_set, 2 * t + k + 1)
                        pool.sem_inc(index_seen, 1)
                        pool.indirect_dma_start(y[k][:], None, y_rows, bass.IndirectOffsetOnAxis(ap=index[k][:, 0:1], axis=0)).then_inc(gathered[k], 16)

            @block.vector
            def _(dve):
                dve.sem_inc(mixed, 2)
                with dve.Fori(0, NT) as t:
                    at = nodes[:, bass.ds(t, 1), :].rearrange("p a d -> p (a d)")
                    for k in range(2):
                        dve.wait_ge(gathered[k], 16 * t + 16)
                        dve.wait_ge(mixed, 2 * t + k + 2)
                        dve.scalar_tensor_tensor(at, y[k][:], gates[:, k, bass.ds(t, 1)], at, ALU.mult, ALU.add).then_inc(mixed, 1)


def route_switch(nc, c, h, sw_w, sw_b, ids, keep_weight, pass_weight, places, list_t):
    E = E2
    with Stage(nc, "switch") as s:
        logits = s.sbuf("logits", [P, NT, E], F32)
        best = s.sbuf("best", [P, NT, 8], F32)
        where = s.sbuf("where", [P, NT, 8], U32)
        column = s.sbuf("expert_column", [P, NT, E], F32)
        chosen = s.sbuf("chosen", [P, NT], F32)
        one = s.sbuf("onehot", [P, NT, E], F32)
        member = s.sbuf("member", [P, NT, E], F32)
        rank = s.sbuf("rank", [P, NT, E], F32)
        total = s.sbuf("total", [P, E], F32)
        shifted = s.sbuf("shifted", [P, NT, E], F32)
        powers = s.sbuf("powers", [P, NT, E], F32)
        prob = s.sbuf("prob", [P, NT], F32)
        started, step, risen = s.sem("started"), s.sem("step"), s.sem("risen")
        router_logits(nc, c, "logits1", h, sw_w, sw_b, E, logits)
        with nc.Block() as block:
            @block.gpsimd
            def _(pool):
                pool.iota(column[:], pattern=[[0, NT], [1, E]], base=0, channel_multiplier=0,
                          allow_small_or_imprecise_dtypes=True).then_inc(started, 1)

            @block.vector
            def _(dve):
                choose(dve, step, 0, logits, best, where)
                n = 2 * NT
                dve.wait_ge(step, n)
                dve.tensor_tensor(shifted[:], logits[:], best[:, :, 0:1].to_broadcast([P, NT, E]), ALU.subtract).then_inc(step, 1)
                dve.tensor_copy(chosen[:], where[:, :, 0]).then_inc(step, 1)
                dve.wait_ge(step, n + 2)
                dve.wait_ge(started, 1)
                dve.tensor_tensor(one[:], column[:], chosen[:].unsqueeze(2).to_broadcast([P, NT, E]), ALU.is_equal).then_inc(step, 1)
                dve.wait_ge(step, n + 3)
                dve.tensor_tensor(member[:], one[:], c["real"][:].unsqueeze(2).to_broadcast([P, NT, E]), ALU.mult).then_inc(step, 1)
                dve.wait_ge(risen, 1)
                dve.tensor_reduce(prob[:], powers[:], AX.X, ALU.add).then_inc(step, 1)
                dve.wait_ge(step, n + 5)
                dve.reciprocal(prob[:], prob[:]).then_inc(step, 1)

            @block.scalar
            def _(act):
                act.wait_ge(step, 2 * NT + 1)
                act.activation(powers[:], shifted[:], ACT.Exp).then_inc(risen, 1)
        rank_tokens(nc, c, "rank1", member, E, rank, total)
        pos = s.sbuf("position", [P, NT], F32)
        kept = s.sbuf("kept", [P, NT], F32)
        left = s.sbuf("left", [P, NT], F32)
        start = s.sbuf("expert_start", [P, NT], F32)
        place = s.sbuf("place", [P, NT], F32)
        spare = s.sbuf("spare_place", [P, NT], F32)
        drop_i = s.sbuf("list_place", [P, NT], I32)
        with nc.Block() as block:
            step, began = s.sem("place_step"), s.sem("place_began")

            @block.gpsimd
            def _(pool):
                pool.iota(spare[:], pattern=[[P, NT]], base=PLACES, channel_multiplier=1,
                          allow_small_or_imprecise_dtypes=True).then_inc(began, 1)

            @block.vector
            def _(dve):
                dve.wait_ge(began, 1)
                dve.tensor_tensor(one[:], one[:], rank[:], ALU.mult).then_inc(step, 1)
                dve.tensor_scalar(start[:], chosen[:], float(P), None, ALU.mult).then_inc(step, 1)
                dve.wait_ge(step, 2)
                dve.tensor_reduce(pos[:], one[:], AX.X, ALU.add).then_inc(step, 1)
                dve.wait_ge(step, 3)
                dve.scalar_tensor_tensor(kept[:], pos[:], float(CAP), c["real"][:], ALU.is_lt, ALU.mult).then_inc(step, 1)
                dve.scalar_tensor_tensor(place[:], pos[:], float(CAP - 1), start[:], ALU.min, ALU.add).then_inc(step, 1)
                dve.wait_ge(step, 5)
                dve.tensor_copy(places[:], place[:]).then_inc(step, 1)
                dve.tensor_scalar(left[:], kept[:], -1.0, 1.0, ALU.mult, ALU.add).then_inc(step, 1)
                dve.tensor_tensor(keep_weight[:], kept[:], prob[:], ALU.mult).then_inc(step, 1)
                dve.wait_ge(step, 8)
                dve.tensor_tensor(pass_weight[:], left[:], prob[:], ALU.mult).then_inc(step, 1)
                dve.tensor_tensor(spare[:], spare[:], left[:], ALU.mult).then_inc(step, 1)
                dve.tensor_tensor(place[:], place[:], kept[:], ALU.mult).then_inc(step, 1)
                dve.wait_ge(step, 11)
                dve.tensor_tensor(drop_i[:], place[:], spare[:], ALU.add).then_inc(step, 1)
        store_list(nc, "list1", ids, c["node"], drop_i, NT)
        load_list(nc, c, "loadlist1", ids, list_t)


def switch_experts(nc, c, rows, ex_w, ex_b, list_t, y_rows):
    with Stage(nc, "experts") as s:
        index_seen = s.sem("index_seen")
        w = [s.sbuf(f"w_{u}", [P, KD, D], F32) for u in range(2)]
        token = [s.sbuf(f"token_{u}", [P, D], F32) for u in range(2)]
        index = [s.sbuf(f"index_{u}", [P, 1], I32) for u in range(2)]
        wh = [s.sbuf(f"w_high_{u}", [P, KD, D], F32R) for u in range(2)]
        wl = [s.sbuf(f"w_low_{u}", [P, KD, D], F32R) for u in range(2)]
        xh = [s.sbuf(f"x_high_{u}", [P, KD, P], F32R) for u in range(2)]
        xl = [s.sbuf(f"x_low_{u}", [P, KD, P], F32R) for u in range(2)]
        y = [s.sbuf(f"y_{u}", [P, D], F32) for u in range(2)]
        bias = s.sbuf("bias", [P, E2, D], F32)
        ps_t = [s.psum(f"ps_t_{i}", [P, 512]) for i in range(4)]
        ps_y = [s.psum(f"ps_y_{u}", [P, D]) for u in range(2)]
        biases, index_set = s.sem("biases"), s.sem("index_set")
        loaded = [s.sem(f"loaded_{u}") for u in range(2)]
        gathered = [s.sem(f"gathered_{u}") for u in range(2)]
        turned = s.sem("turned")
        high = s.sem("high")
        low = s.sem("low")
        product = s.sem("product")
        biased = s.sem("biased")
        stored = [s.sem(f"stored_{u}") for u in range(2)]
        with nc.Block() as block:
            @block.sync
            def _(sp):
                sp.dma_start(bias[:], ex_b.rearrange("e d -> (e d)").partition_broadcast(P)).then_inc(biases, 16)
                with sp.Fori(0, E2 // 2) as i:
                    for u in range(2):
                        e = 2 * i + u
                        sp.wait_ge(turned, 5 * e + 5)
                        sp.dma_start(w[u][:], ex_w[bass.ds(e, 1), :, :].rearrange("e (o p) d -> p (e o) d", p=P)).then_inc(loaded[u], 16)

            @block.gpsimd
            def _(pool):
                with pool.Fori(0, E2 // 2) as i:
                    for u in range(2):
                        e = 2 * i + u
                        pool.wait_ge(turned, 5 * e + 1)
                        pool.tensor_copy(index[u][:], list_t[:, bass.ds(e, 1)]).then_inc(index_set, 1)
                        pool.wait_ge(index_set, e + 1)
                        pool.sem_inc(index_seen, 1)
                        pool.indirect_dma_start(token[u][:], None, rows, bass.IndirectOffsetOnAxis(ap=index[u][:, 0:1], axis=0)).then_inc(gathered[u], 16)

            @block.scalar
            def _(act):
                for u in range(2):
                    act.sem_inc(stored[u], 16)

                def store(i, u):
                    e = 2 * i + u
                    act.wait_ge(biased, e + 3)
                    act.dma_start(y_rows[bass.ds(e * P, P), :], y[u][:]).then_inc(stored[u], 16)

                with act.Fori(0, E2 // 2) as i:
                    for u in range(2):
                        e = 2 * i + u
                        act.wait_ge(product, e + 1)
                        for j in range(5):
                            act.wait_ge(turned, 5 * e + j + 11)
                            target = xh[u][:].rearrange("p k n -> p (k n)") if j == 0 else wh[u][:, j - 1, :]
                            act.copy(target, ps_t[j % 4 if j < 4 else 0][:]).then_inc(high, 1)
                        store(i, u)
                for u in range(2):
                    act.wait_ge(stored[u], 16 * (E2 // 2 + 1))

            @block.vector
            def _(dve):
                dve.sem_inc(low, 4)
                dve.sem_inc(biased, 2)
                dve.wait_ge(biases, 16)
                with dve.Fori(0, E2 // 2) as i:
                    for u in range(2):
                        e = 2 * i + u
                        for j in range(5):
                            dve.wait_ge(high, 5 * e + j + 1)
                            if j == 0:
                                target, upper = xl[u][:].rearrange("p k n -> p (k n)"), xh[u][:].rearrange("p k n -> p (k n)")
                            else:
                                target, upper = wl[u][:, j - 1, :], wh[u][:, j - 1, :]
                            dve.tensor_tensor(target, ps_t[j % 4 if j < 4 else 0][:], upper.bitcast(F32), ALU.subtract).then_inc(low, 1)
                        dve.wait_ge(product, e + 3)
                        dve.wait_ge(stored[u], 16 * i + 16)
                        dve.tensor_tensor(y[u][:], ps_y[u][:], bias[:, bass.ds(e, 1), :].rearrange("p a d -> p (a d)"), ALU.add).then_inc(biased, 1)

            @block.tensor
            def _(pe):
                pe.sem_inc(turned, 10)
                pe.sem_inc(product, 2)
                with pe.Fori(0, E2 // 2) as i:
                    for u in range(2):
                        e = 2 * i + u
                        pe.wait_ge(gathered[u], 16 * i + 16)
                        pe.wait_ge(loaded[u], 16 * i + 16)
                        for j in range(5):
                            pe.wait_ge(low, 5 * e + j + 4 if j < 4 else 5 * e + 5)
                            for o in range(KD):
                                src = token[u][:, o * P:(o + 1) * P] if j == 0 else w[u][:, o, (j - 1) * P:j * P]
                                last = pe.transpose(ps_t[j % 4 if j < 4 else 0][:, o * P:(o + 1) * P], src, c["ident"][:])
                            last.then_inc(turned, 1)
                        pe.wait_ge(low, 5 * e + 9)
                        pe.wait_ge(biased, e + 1)
                        for k in range(KD):
                            pe.matmul(ps_y[u][:], xh[u][:, k, :], wh[u][:, k, :], start=(k == 0), stop=False)
                            pe.matmul(ps_y[u][:], xh[u][:, k, :], wl[u][:, k, :], start=False, stop=False)
                            last = pe.matmul(ps_y[u][:], xl[u][:, k, :], wh[u][:, k, :], start=False, stop=(k == KD - 1))
                        last.then_inc(product, 1)


def switch_output(nc, c, y_rows, places, keep_weight, pass_weight, h, nodes, out):
    with Stage(nc, "output") as s:
        index_seen = s.sem("index_seen")
        index = [s.sbuf(f"index_{u}", [P, 1], I32) for u in range(2)]
        y = [s.sbuf(f"y_{u}", [P, D], F32) for u in range(2)]
        index_set, step, stored = s.sem("index_set"), s.sem("step"), s.sem("stored")
        gathered = [s.sem(f"gathered_{u}") for u in range(2)]
        with nc.Block() as block:
            @block.gpsimd
            def _(pool):
                with pool.Fori(0, NT // 2) as i:
                    for u in range(2):
                        t = 2 * i + u
                        pool.wait_ge(step, 2 * t + 2)
                        pool.tensor_copy(index[u][:], places[:, bass.ds(t, 1)]).then_inc(index_set, 1)
                        pool.wait_ge(index_set, t + 1)
                        pool.sem_inc(index_seen, 1)
                        pool.indirect_dma_start(y[u][:], None, y_rows, bass.IndirectOffsetOnAxis(ap=index[u][:, 0:1], axis=0)).then_inc(gathered[u], 16)

            @block.vector
            def _(dve):
                dve.sem_inc(step, 4)
                with dve.Fori(0, NT // 2) as i:
                    for u in range(2):
                        t = 2 * i + u
                        at = nodes[:, bass.ds(t, 1), :].rearrange("p a d -> p (a d)")
                        dve.scalar_tensor_tensor(at, h[:, bass.ds(t, 1), :].rearrange("p a d -> p (a d)"), pass_weight[:, bass.ds(t, 1)], at,
                                                 ALU.mult, ALU.add).then_inc(step, 1)
                        dve.wait_ge(gathered[u], 16 * i + 16)
                        dve.wait_ge(step, 2 * t + 5)
                        dve.scalar_tensor_tensor(at, y[u][:], keep_weight[:, bass.ds(t, 1)], at, ALU.mult, ALU.add).then_inc(step, 1)

            @block.sync
            def _(sp):
                with sp.Fori(0, NT - 1) as t:
                    sp.wait_ge(step, 2 * t + 6)
                    sp.dma_start(out[bass.ds(t * P, P), :], nodes[:, bass.ds(t, 1), :].rearrange("p a d -> p (a d)")).then_inc(stored, 16)
                sp.wait_ge(step, 2 * NT + 4)
                sp.dma_start(out[(NT - 1) * P:N, :], nodes[0:LAST, NT - 1, :]).then_inc(stored, 16)
                sp.wait_ge(stored, 16 * NT)


def add_nodes(nc, h, nodes):
    with Stage(nc, "residual") as s:
        added = s.sem("added")
        with nc.Block() as block:
            @block.vector
            def _(dve):
                dve.tensor_tensor(nodes[:], nodes[:], h[:], ALU.add).then_inc(added, 1)


def store_rows(nc, tag, tile, rows):
    with Stage(nc, tag) as s:
        stored = s.sem("stored")
        with nc.Block() as block:
            @block.sync
            def _(sp):
                sp.dma_start(by_tile(rows), tile[:]).then_inc(stored, 16)
                sp.wait_ge(stored, 16)


def load_nodes(nc, x, nodes):
    with Stage(nc, "load") as s:
        cleared, loaded = s.sem("cleared"), s.sem("loaded")
        with nc.Block() as block:
            @block.vector
            def _(dve):
                dve.memset(nodes[:, NT - 1, :], 0.0).then_inc(cleared, 1)

            @block.sync
            def _(sp):
                sp.dma_start(nodes[:, 0:NT - 1, :], by_tile(x[0:(NT - 1) * P, :])).then_inc(loaded, 16)
                sp.wait_ge(cleared, 1)
                sp.dma_start(nodes[0:LAST, NT - 1, :], x[(NT - 1) * P:N, :]).then_inc(loaded, 16)
                sp.wait_ge(loaded, 32)


def program(nc, x, src, dst, gnn_w, ln_g, ln_b, w_r, b_r, W1, b1, W2, b2, Ws, Wn, bs, sw_w, sw_b, ex_w, ex_b, out):
    rows = nc.dram_tensor("token_rows", [NPAD, D], F32, kind="Internal").ap()
    rows2 = nc.dram_tensor("token_rows_2", [NPAD, D], F32, kind="Internal").ap()
    ids = nc.dram_tensor("unit_list", [SLOTS, 1], I32, kind="Internal").ap()
    ids2 = nc.dram_tensor("expert_list", [PLACES + NPAD, 1], I32, kind="Internal").ap()
    y_rows = nc.dram_tensor("unit_rows", [SLOTS, D], F32, kind="Internal").ap()
    y_rows2 = nc.dram_tensor("expert_rows", [PLACES, D], F32, kind="Internal").ap()
    with Stage(nc, "keep") as keep:
        c = make_constants(nc, keep)
        counts = keep.sbuf("edge_counts", [P, NT, AW], U16)
        nodes = keep.sbuf("nodes", [P, NT, D], F32)
        inverse = keep.sbuf("inverse_degree", [P, NT], F32)
        load_nodes(nc, x, nodes)
        build_adjacency(nc, c, keep, src, dst, counts, y_rows)
        count_degrees(nc, c, counts, inverse)
        with Stage(nc, "a") as s:
            h = s.sbuf("h", [P, NT, D], F32)
            normalize(nc, c, "ln0", nodes, h)
            sage_layer(nc, c, gnn_w, h, nodes, counts, inverse)
        with Stage(nc, "b") as s:
            gates = s.sbuf("gates", [P, 2, NT], F32)
            slots = s.sbuf("slots", [P, 2 * NT], I32)
            unit_expert = s.sbuf("unit_expert", [1, UNITS + 1], I32)
            n_units = s.sbuf("n_units", [1, 1], I32)
            list_t = s.sbuf("list", [P, SLOTS // P], I32)
            with Stage(nc, "b2") as q:
                h = q.sbuf("h", [P, NT, D], F32)
                hn = q.sbuf("h_norm", [P, NT, D], F32)
                normalize(nc, c, "ln1", nodes, h)
                normalize(nc, c, "ln2", h, hn)
                scale_shift(nc, ln_g, ln_b, h, hn, nodes, rows)
                route_top2(nc, c, hn, w_r, b_r, ids, gates, slots, unit_expert, n_units, list_t)
            top2_experts(nc, c, rows, W1, b1, W2, b2, unit_expert, n_units, list_t, y_rows)
            gather_top2(nc, c, y_rows, slots, gates, nodes)
        with Stage(nc, "c") as s:
            h = s.sbuf("h", [P, NT, D], F32)
            normalize(nc, c, "ln3", nodes, h)
            graph_layers(nc, c, Ws, Wn, bs, h, counts, inverse)
            add_nodes(nc, h, nodes)
        with Stage(nc, "d") as s:
            h = s.sbuf("h", [P, NT, D], F32)
            keep_weight = s.sbuf("keep_weight", [P, NT], F32)
            pass_weight = s.sbuf("pass_weight", [P, NT], F32)
            places = s.sbuf("places", [P, NT], I32)
            list_t = s.sbuf("list", [P, (PLACES + NPAD) // P], I32)
            normalize(nc, c, "ln4", nodes, h)
            store_rows(nc, "rows2", h, rows2)
            route_switch(nc, c, h, sw_w, sw_b, ids2, keep_weight, pass_weight, places, list_t)
            switch_experts(nc, c, rows2, ex_w, ex_b, list_t, y_rows2)
            switch_output(nc, c, y_rows2, places, keep_weight, pass_weight, h, nodes, out)


_INS = ["x", "src", "dst", "L0_gnn_w", "L0_ffn_ln_g", "L0_ffn_ln_b", "L0_ffn_w_r", "L0_ffn_b_r", "L0_ffn_W1",
        "L0_ffn_b1", "L0_ffn_W2", "L0_ffn_b2", "L1_gnn_Ws_self", "L1_gnn_Ws_neigh", "L1_gnn_bs",
        "L1_ffn_switch_w", "L1_ffn_switch_b", "L1_ffn_expert_w", "L1_ffn_expert_b"]


def kernel(**inputs):
    import numpy as _np
    import concourse.bacc as _bacc
    from concourse import mybir as _mybir
    from concourse.bass_utils import run_bass_kernel_spmd as _run

    nc = _bacc.Bacc("TRN2", target_bir_lowering=False, num_devices=1)
    arrays, args = {}, []
    for name in _INS:
        a = _np.ascontiguousarray(inputs[name])
        arrays[f"in_{name}"] = a
        args.append(nc.dram_tensor(f"in_{name}", a.shape, _mybir.dt.from_np(a.dtype), kind="ExternalInput").ap())
    result = nc.dram_tensor("result", (N, D), F32, kind="ExternalOutput").ap()
    program(nc, *args, result)
    r = _run(nc, [arrays], core_ids=[0])
    return r.results[0]["result"]
```

```python
from contextlib import ExitStack

import numpy as np
import concourse.bass as bass
import concourse.mybir as mybir

ALU = mybir.AluOpType
ACT = mybir.ActivationFunctionType
AX = mybir.AxisListType
F32 = mybir.dt.float32
F32R = mybir.dt.float32r
BF16 = mybir.dt.bfloat16
I32 = mybir.dt.int32
U32 = mybir.dt.uint32
I16 = mybir.dt.int16
U16 = mybir.dt.uint16

P = 128
N = 1250
D = 512
E_ALL = 41250
NT = -(-N // P)
NPAD = NT * P
LAST = N - (NT - 1) * P
KD = D // P
EPS = 1e-5

CH = 4
GE = CH * P
NG = -(-E_ALL // GE)
TAIL = E_ALL - (NG - 1) * GE
WIN = 32
AW = NPAD + WIN
PASSES = -(-N // WIN)

E1 = 8
F1 = 2048
FB = 512
NFB = F1 // FB
T = 512
TB = T // P
UNITS = E1 + 2 * N // T
SLOTS = UNITS * T
FEWEST = -(-2 * N // T)

E2 = 16
CAP = int(1.2 * N / E2)
PLACES = E2 * P


class Stage:

    def __init__(self, nc, tag):
        self.nc, self.tag, self.ctx = nc, tag, ExitStack()

    def __enter__(self):
        self.ctx.__enter__()
        return self

    def __exit__(self, *a):
        return self.ctx.__exit__(*a)

    def sbuf(self, name, shape, dt):
        return self.ctx.enter_context(self.nc.sbuf_tensor(f"{self.tag}_{name}", shape, dt))

    def psum(self, name, shape, dt=F32):
        return self.ctx.enter_context(self.nc.psum_tensor(f"{self.tag}_{name}", shape, dt))

    def sem(self, name):
        return self.ctx.enter_context(self.nc.semaphore(f"{self.tag}_{name}"))



def by_tile(ap):
    return ap.rearrange("(t p) d -> p t d", p=P)


def make_constants(nc, keep):
    c = {
        "ident": keep.sbuf("ident", [P, P], F32),
        "upper": keep.sbuf("upper", [P, P], F32),
        "ones": keep.sbuf("ones", [P, P], F32),
        "half": keep.sbuf("minus_half", [P, NT], F32),
        "real": keep.sbuf("real_node", [P, NT], F32),
        "node": keep.sbuf("node_id", [P, NT], I32),
    }
    c["carrier"] = keep.sem("wait_carrier")
    made = keep.sem("constants_made")
    with nc.Block() as block:
        @block.gpsimd
        def _(pool):
            pool.memset(c["ident"][:], 0.0).then_inc(made, 1)
            pool.memset(c["upper"][:], 1.0).then_inc(made, 1)
            pool.memset(c["ones"][:], 1.0).then_inc(made, 1)
            pool.memset(c["half"][:], -0.5).then_inc(made, 1)
            pool.memset(c["real"][:], 1.0).then_inc(made, 1)
            pool.iota(c["node"][:], pattern=[[P, NT]], base=0, channel_multiplier=1).then_inc(made, 1)
            pool.wait_ge(made, 6)
            pool.affine_select(out=c["ident"][:], in_=c["ident"][:], compare_op=ALU.not_equal, fill=1.0,
                               base=0, pattern=[[-1, P]], channel_multiplier=1).then_inc(made, 1)
            pool.affine_select(out=c["upper"][:], in_=c["upper"][:], compare_op=ALU.is_gt, fill=0.0,
                               base=0, pattern=[[1, P]], channel_multiplier=-1).then_inc(made, 1)
            pool.affine_select(out=c["real"][:], in_=c["real"][:], compare_op=ALU.is_gt, fill=0.0,
                               base=N, pattern=[[-P, NT]], channel_multiplier=-1).then_inc(made, 1)
            pool.wait_ge(made, 9)
    return c


class Normalizer:

    def __init__(self, keep):
        self.measured, self.scaled, self.done = keep.sem("ln_measured"), keep.sem("ln_scaled"), keep.sem("ln_done")
        self.calls = 0

    def __call__(self, nc, c, tag, source, target):
        measured, scaled, done = self.measured, self.scaled, self.done
        m, k = 2 * NT * self.calls, 2 * self.calls
        self.calls += 1
        with Stage(nc, tag) as s:
            stats = s.sbuf("bn_stats", [P, NT, 6], F32)
            mean_var = s.sbuf("mean_var", [P, NT, 2], F32)
            rstd = s.sbuf("rstd", [P, NT], F32)
            with nc.Block() as block:
                @block.vector
                def _(dve):
                    for t in range(NT):
                        dve.bn_stats(stats[:, t, :], source[:, t, :]).then_inc(measured, 1)
                    for t in range(NT):
                        dve.wait_ge(measured, m + t + 1)
                        dve.bn_aggr(mean_var[:, t, :], stats[:, t, :]).then_inc(measured, 1)
                    dve.wait_ge(scaled, k + 2)
                    for t in range(NT):
                        dve.tensor_scalar(target[:, t, :], source[:, t, :], mean_var[:, t, 0:1], rstd[:, t:t + 1],
                                          ALU.subtract, ALU.mult).then_inc(done, 1)

                @block.gpsimd
                def _(pool):
                    pool.wait_ge(measured, m + 2 * NT)
                    pool.tensor_scalar(rstd[:], mean_var[:, :, 1], EPS, None, ALU.add).then_inc(scaled, 1)
                    pool.wait_ge(scaled, k + 1)
                    pool.tensor_tensor(rstd[:], rstd[:], c["half"][:], ALU.pow).then_inc(scaled, 1)


def build_adjacency(nc, c, keep, src, dst, counts, crowded, y_rows):
    NP = 10 * WIN
    with Stage(nc, "adjacency") as s:
        edge_src = s.sbuf("edge_src", [NG, GE], I32)
        edge_dst = s.sbuf("edge_dst", [NG, GE], I32)
        low_i = s.sbuf("src_low_i", [NG, GE], I32)
        high_i = s.sbuf("src_high_i", [NG, GE], I32)
        dst_f = s.sbuf("dst_f", [NG, GE], F32)
        low_f = s.sbuf("src_low_f", [NG, GE], F32)
        high_f = s.sbuf("src_high_f", [NG, GE], F32)
        rel = s.sbuf("dst_in_window", [NG, GE], F32)
        inside = s.sbuf("inside_window", [NG, GE], F32)
        place = s.sbuf("place", [NG, GE], F32)
        base = s.sbuf("window_base", [NG, 1], F32)
        top = s.sbuf("greatest_dst", [NG, 1], F32)
        wide = s.sbuf("wide_columns", [NG, 2, P], F32)
        place_t = s.sbuf("place_t", [P, CH, NG], F32)
        base_row = s.sbuf("base_row", [1, NG], I32)
        span = s.sbuf("greatest_span", [1, 2], F32)
        span_i = s.sbuf("greatest_span_i", [1, 1], I32)
        first_base = s.sbuf("first_base", [NG, 1], F32)
        node_row = s.sbuf("node_row", [NG, NPAD], F32)
        reached = s.sbuf("reached", [NG, 2, NPAD], F32)
        most = s.sbuf("most_groups", [1, 4], F32)
        based, covered = s.sem("first_base_kept"), s.sem("groups_reach")
        overlaid, crowd = s.sem("groups_overlaid"), s.sem("crowd_step")
        count_low = s.sbuf("count_low", [P, P], I16)
        count_place = s.sbuf("count_place", [P, NP], I16)
        hot_low = s.sbuf("onehot_low", [P, 2, CH, P], BF16)
        hot_place = s.sbuf("onehot_place", [P, 2, CH, NP], BF16)
        ps_t = [s.psum(f"ps_edges_{i}", [P, 512]) for i in range(3)]
        ps_n = [s.psum(f"ps_window_{i}", [P, 512]) for i in range(2)]
        edges_in, filled = s.sem("edges_in"), s.sem("edges_filled")
        step, turned, taken = s.sem("edge_step"), s.sem("edges_turned"), s.sem("edges_taken")
        hot, counted, added = s.sem("onehots_ready"), s.sem("window_counted"), s.sem("window_added")
        distance = s.sbuf("low_distance", [P, 2, CH, P], BF16)
        hot_l, apart = s.sem("low_onehots_ready"), s.sem("low_distance_ready")
        minus_low = s.sbuf("minus_src_low_t", [P, CH, NG], F32)
        zeros = s.sbuf("zero_rows", [P, D], F32)
        zeroed, cleared = s.sem("zero_rows_made"), s.sem("y_rows_cleared")

        FIRST, PREP = 12, 7
        turns = (3, 2)

        def prepare(dve, at, k_turn, k_taken):
            dve.tensor_scalar(rel[:], dst_f[:], base[:, 0:1], None, ALU.subtract).then_inc(step, 1)
            dve.wait_ge(step, at + 1)
            dve.tensor_scalar(inside[:], rel[:], 0.0, None, ALU.is_ge).then_inc(step, 1)
            dve.wait_ge(step, at + 2)
            dve.scalar_tensor_tensor(inside[:], rel[:], float(WIN), inside[:], ALU.is_lt, ALU.mult).then_inc(step, 1)
            dve.scalar_tensor_tensor(place[:], rel[:], 1.0, high_f[:], ALU.add, ALU.add).then_inc(step, 1)
            dve.wait_ge(step, at + 4)
            dve.tensor_tensor(place[:], place[:], inside[:], ALU.mult).then_inc(step, 1)
            dve.tensor_copy(wide[:, 0, 0:1], base[:, 0:1]).then_inc(step, 1)
            dve.wait_ge(turned, k_turn)
            dve.tensor_copy(place_t[:], ps_t[0][:, 0:CH * NG].rearrange("p (c g) -> p c g", c=CH)).then_inc(taken, 1)
            dve.tensor_copy(base_row[:], ps_t[1][0:1, 0:NG]).then_inc(taken, 1)
            dve.tensor_scalar(base[:], base[:], float(WIN), float(NPAD), ALU.add, ALU.min).then_inc(step, 1)
            dve.wait_ge(taken, k_taken)
            dve.wait_ge(step, at + 7)

        def turn_places(pe, at, k_turn):
            pe.wait_ge(step, at + 6)
            for ch in range(CH):
                last = pe.transpose(ps_t[0][:, ch * NG:(ch + 1) * NG], place[:, ch * P:(ch + 1) * P], c["ident"][0:NG, 0:NG])
            last.then_inc(turned, 1)
            pe.transpose(ps_t[1][:, 0:NG], wide[:, 0, :], c["ident"][0:NG, 0:NG]).then_inc(turned, 1)

        def onehots(dve, g, u):
            dve.tensor_scalar(hot_low[:, u, CH - 1, :], count_low[:], minus_low[:, CH - 1, bass.ds(g, 1)], 0.0,
                              ALU.add, ALU.is_equal)
            for ch in range(CH):
                last = dve.tensor_scalar(hot_place[:, u, ch, :], count_place[:], place_t[:, ch, bass.ds(g, 1)],
                                         None, ALU.is_equal)
            last.then_inc(hot, 1)

        def add_window(dve, g, u, done, start):
            at = counts[:, :, bass.ds(start, WIN)]
            dve.wait_ge(counted, done + 1)
            dve.wait_ge(added, done + 1)
            dve.tensor_tensor(at, ps_n[u][:, 0:NP].rearrange("p (a b) -> p a b", b=WIN), at, ALU.add).then_inc(added, 1)

        def base_of(dve, g):
            return dve.value_load(base_row[0:1, bass.ds(g, 1)], min_val=0, max_val=NPAD)

        def count_pass(dve, before):
            onehots(dve, 0, 0)
            with dve.Fori(0, (NG - 1) // 4) as i:
                for u in range(4):
                    g = 4 * i + u
                    onehots(dve, g + 1, 1 - u % 2)
                    add_window(dve, g, u % 2, before + g, base_of(dve, g))
            start = base_of(dve, NG - 1)
            add_window(dve, NG - 1, 0, before + NG - 1, start)
            dve.wait_ge(added, before + NG + 1)

        def low_onehots(act, g, u, before):
            for ch in range(CH - 1):
                last = act.activation(distance[:, u, ch, :], count_low[:], ACT.Abs, bias=minus_low[:, ch, bass.ds(g, 1)])
            last.then_inc(apart, 1)
            act.wait_ge(apart, before + g + 1)
            act.activation(hot_low[:, u, 0:CH - 1, :], distance[:, u, 0:CH - 1, :], ACT.Relu, bias=1.0, scale=-1.0).then_inc(hot_l, 1)

        def low_pass(act, before):
            low_onehots(act, 0, 0, before)
            low_onehots(act, 1, 1, before)
            with act.Fori(0, (NG - 3) // 2) as i:
                for u in range(2):
                    g = 2 * i + u + 2
                    act.wait_ge(counted, before + g - 1)
                    low_onehots(act, g, u, before)
            act.wait_ge(counted, before + NG - 2)
            low_onehots(act, NG - 1, 0, before)

        def multiply(pe, g, u, before):
            pe.wait_ge(hot, before + g + 1)
            pe.wait_ge(hot_l, before + g + 1)
            for ch in range(CH):
                last = pe.matmul(ps_n[u][:, 0:NP], hot_low[:, u, ch, :], hot_place[:, u, ch, :],
                                 start=(ch == 0), stop=(ch == CH - 1))
            last.then_inc(counted, 1)

        def multiply_pass(pe, before):
            multiply(pe, 0, 0, before)
            with pe.Fori(0, (NG - 1) // 2) as i:
                for u in range(2):
                    multiply(pe, 2 * i + u + 1, 1 - u, before)

        with nc.Block() as block:
            @block.sync
            def _(sp):
                sp.wait_ge(filled, 1)
                full = (NG - 1) * GE
                sp.dma_start(edge_src[0:NG - 1, :], src[0:full].rearrange("(g e) -> g e", e=GE)).then_inc(edges_in, 16)
                sp.dma_start(edge_src[NG - 1:NG, 0:TAIL], src[full:E_ALL].rearrange("(g e) -> g e", g=1)).then_inc(edges_in, 16)
                sp.dma_start(edge_dst[0:NG - 1, :], dst[0:full].rearrange("(g e) -> g e", e=GE)).then_inc(edges_in, 16)
                sp.dma_start(edge_dst[NG - 1:NG, 0:TAIL], dst[full:E_ALL].rearrange("(g e) -> g e", g=1)).then_inc(edges_in, 16)
                sp.dma_start(edge_dst[NG - 1:NG, TAIL:GE], dst[E_ALL - (GE - TAIL):E_ALL].rearrange("(g e) -> g e", g=1)).then_inc(edges_in, 16)
                sp.wait_ge(zeroed, 1)
                for b in range(FEWEST * TB, UNITS * TB):
                    sp.dma_start(y_rows[b * P:(b + 1) * P, :], zeros[:]).then_inc(cleared, 16)
                sp.wait_ge(cleared, 16 * (UNITS - FEWEST) * TB)

            @block.scalar
            def _(act):
                act.wait_ge(taken, 1)
                low_pass(act, 0)
                act.wait_ge(taken, 3)
                reach = act.value_load(span_i[0:1, 0:1], min_val=0, max_val=NPAD)
                with act.If(reach > WIN - 1):
                    with act.Fori(1, PASSES) as k:
                        act.wait_ge(added, NG * k + 1)
                        low_pass(act, NG * k)

            @block.gpsimd
            def _(pool):
                pool.memset(zeros[:], 0.0).then_inc(zeroed, 1)
                pool.memset(edge_src[:], -100 * P).then_inc(filled, 1)
                pool.memset(wide[:], 0.0).then_inc(filled, 1)
                pool.iota(count_low[:], pattern=[[1, P]], base=0, channel_multiplier=0,
                          allow_small_or_imprecise_dtypes=True).then_inc(filled, 1)
                pool.iota(count_place[:], pattern=[[1, NP]], base=1, channel_multiplier=0,
                          allow_small_or_imprecise_dtypes=True).then_inc(filled, 1)
                pool.iota(node_row[:], pattern=[[1, NPAD]], base=0, channel_multiplier=0,
                          allow_small_or_imprecise_dtypes=True).then_inc(filled, 1)
                pool.wait_ge(filled, 5)
                pool.wait_ge(based, 1)
                pool.tensor_scalar(reached[:, 0, :], node_row[:], first_base[:, 0:1], None, ALU.is_ge).then_inc(covered, 1)
                pool.tensor_scalar(reached[:, 1, :], node_row[:], top[:, 0:1], None, ALU.is_le).then_inc(covered, 1)
                pool.wait_ge(covered, 2)
                pool.tensor_tensor(reached[:, 0, :], reached[:, 0, :], reached[:, 1, :], ALU.mult).then_inc(covered, 1)

            @block.vector
            def _(dve):
                dve.memset(counts[:], 0.0).then_inc(added, 1)
                dve.wait_ge(filled, 4)
                dve.wait_ge(edges_in, 80)
                dve.tensor_scalar(low_i[:], edge_src[:], P - 1, None, ALU.bitwise_and).then_inc(step, 1)
                dve.tensor_scalar(high_i[:], edge_src[:], 7, None, ALU.arith_shift_right).then_inc(step, 1)
                dve.tensor_copy(dst_f[:], edge_dst[:]).then_inc(step, 1)
                dve.wait_ge(step, 3)
                dve.tensor_copy(low_f[:], low_i[:]).then_inc(step, 1)
                dve.tensor_scalar(high_f[:], high_i[:], float(WIN), None, ALU.mult).then_inc(step, 1)
                dve.tensor_reduce(base[:], dst_f[:], AX.X, ALU.min).then_inc(step, 1)
                dve.tensor_reduce(top[:], dst_f[:], AX.X, ALU.max).then_inc(step, 1)
                dve.wait_ge(step, 7)
                dve.tensor_copy(first_base[:], base[:]).then_inc(based, 1)
                dve.tensor_tensor(wide[:, 1, 0:1], top[:], base[:], ALU.subtract).then_inc(step, 1)
                dve.wait_ge(turned, 2)
                dve.tensor_scalar(minus_low[:], ps_t[2][:, 0:CH * NG].rearrange("p (c g) -> p c g", c=CH), -1.0, None,
                                  ALU.mult).then_inc(taken, 1)
                dve.tensor_reduce(span[0:1, 0:1], ps_t[1][0:1, 0:NG], AX.X, ALU.max).then_inc(step, 1)
                dve.wait_ge(step, 9)
                dve.tensor_copy(span_i[:], span[0:1, 0:1]).then_inc(step, 1)
                dve.wait_ge(step, 10)
                dve.wait_ge(taken, 1)
                prepare(dve, 10, 4, 3)
                count_pass(dve, 0)
                dve.wait_ge(overlaid, 1)
                for i in range(3):
                    dve.tensor_reduce(most[0:1, i:i + 1], ps_t[i][0:1, 0:min(512, NPAD - 512 * i)], AX.X, ALU.max).then_inc(crowd, 1)
                dve.wait_ge(crowd, 3)
                dve.tensor_reduce(most[0:1, 3:4], most[0:1, 0:3], AX.X, ALU.max).then_inc(crowd, 1)
                dve.wait_ge(crowd, 4)
                dve.tensor_copy(crowded[:], most[0:1, 3:4]).then_inc(crowd, 1)
                reach = dve.value_load(span_i[0:1, 0:1], min_val=0, max_val=NPAD)
                with dve.If(reach > WIN - 1):
                    with dve.Fori(1, PASSES) as k:
                        prepare(dve, 10 + 7 * k, 4 + 2 * k, 3 + 2 * k)
                        count_pass(dve, NG * k)

            @block.tensor
            def _(pe):
                pe.wait_ge(step, 8)
                for ch in range(CH):
                    last = pe.transpose(ps_t[2][:, ch * NG:(ch + 1) * NG], low_f[:, ch * P:(ch + 1) * P], c["ident"][0:NG, 0:NG])
                last.then_inc(turned, 1)
                pe.transpose(ps_t[1][:, 0:NG], wide[:, 1, :], c["ident"][0:NG, 0:NG]).then_inc(turned, 1)
                pe.wait_ge(step, 10)
                turn_places(pe, 10, 4)
                multiply_pass(pe, 0)
                pe.wait_ge(covered, 3)
                for i in range(3):
                    width = min(512, NPAD - 512 * i)
                    last = pe.matmul(ps_t[i][0:1, 0:width], c["ones"][0:NG, 0:1], reached[:, 0, 512 * i:512 * i + width],
                                     start=True, stop=True)
                last.then_inc(overlaid, 1)
                reach = pe.value_load(span_i[0:1, 0:1], min_val=0, max_val=NPAD)
                with pe.If(reach > WIN - 1):
                    with pe.Fori(1, PASSES) as k:
                        pe.wait_ge(added, NG * k + 1)
                        pe.wait_ge(crowd, 3)
                        turn_places(pe, 10 + 7 * k, 4 + 2 * k)
                        multiply_pass(pe, NG * k)



class Sage:

    def __init__(self, s, c, crowded, degrees=False):
        self.carrier = c["carrier"]
        self.degrees, self.crowded = degrees, crowded
        self.count_whole = s.sbuf("count_whole", [P, NT, P], F32)
        self.count_rest = s.sbuf("count_rest", [P, NT, P], F32R)
        self.rest_staged = s.sem("count_rest_staged")
        if degrees:
            self.partial = s.sbuf("degree_partial", [P, P], F32)
            self.degree = s.sbuf("degree", [P, 1], F32)
            self.ps_degree = s.psum("ps_degree", [P, 512])
            self.partial_ready = s.sem("degree_partial_ready")
            self.degree_ready = s.sem("degree_ready")
        self.high = s.sbuf("h_high", [P, NT, D], F32R)
        self.low = s.sbuf("h_low", [P, NT, D], F32R)
        self.w_high = s.sbuf("w_high", [P, 2 * KD, D], F32R)
        self.w_low = s.sbuf("w_low", [P, 2 * KD, D], F32R)
        self.count_tile = [s.sbuf(f"count_tile_{u}", [P, NT, P], F32R) for u in range(2)]
        self.h_tile = [s.sbuf(f"h_tile_{u}", [P, D], F32) for u in range(2)]
        self.mean_tile = [s.sbuf(f"mean_tile_{u}", [P, D], F32) for u in range(2)]
        self.ht_high = [s.sbuf(f"ht_high_{u}", [P, KD, P], F32R) for u in range(2)]
        self.ht_low = [s.sbuf(f"ht_low_{u}", [P, KD, P], F32R) for u in range(2)]
        self.mt_high = [s.sbuf(f"mt_high_{u}", [P, KD, P], F32R) for u in range(2)]
        self.mt_low = [s.sbuf(f"mt_low_{u}", [P, KD, P], F32R) for u in range(2)]
        self.ps_h = s.psum("ps_h", [P, KD, P])
        self.ps_m = s.psum("ps_m", [P, KD, P])
        self.ps_sum = [s.psum(f"ps_sum_{u}", [P, D]) for u in range(2)]
        self.ps_y = [s.psum(f"ps_y_{u}", [P, D]) for u in range(2)]
        self.staged = s.sem("tile_staged")
        self.turned_h = s.sem("h_turned")
        self.summed = s.sem("neighbours_summed")
        self.turned_m = s.sem("mean_turned")
        self.multiplied = s.sem("y_multiplied")
        self.high_h = s.sem("ht_high_ready")
        self.mean = s.sem("mean_ready")
        self.high_m = s.sem("mt_high_ready")
        self.low_h = s.sem("ht_low_ready")
        self.low_m = s.sem("mt_low_ready")
        self.finished = s.sem("y_finished")
        self.cut_high = s.sem("h_high_cut")
        self.cut_low = s.sem("h_low_cut")

    def has_rests(self, eng):
        return eng.value_load(self.crowded[0:1, 0:1], min_val=0, max_val=NG) > (1 << 12) // GE - 1

    def act_cut(self, act, h):
        for j in range(NT):
            act.copy(self.high[:, j, :], h[:, j, :]).then_inc(self.cut_high, 1)

    def dve_cut(self, dve, h, before):
        for j in range(NT):
            dve.wait_ge(self.cut_high, before + j + 1)
            dve.tensor_tensor(self.low[:, j, :], h[:, j, :], self.high[:, j, :].bitcast(F32), ALU.subtract).then_inc(self.cut_low, 1)

    def pool_tiles(self, pool, counts, h, before, rests):
        pool.wait_ge(self.cut_high, before + 1)
        pool.sem_inc(self.carrier, 1)
        with pool.Fori(0, NT // 2) as i:
            for u in range(2):
                n = before + 2 * i + u
                pool.wait_ge(self.summed, n + 1)
                pool.tensor_copy(self.count_tile[u][:], counts[:, :, bass.ds((2 * i + u) * P, P)]).then_inc(self.staged, 1)
                with pool.If(rests):
                    pool.wait_ge(self.staged, 2 * n + 1)
                    pool.wait_ge(self.summed, n + 2)
                    pool.sem_inc(self.carrier, 1)
                    pool.tensor_copy(self.count_whole[:], counts[:, :, bass.ds((2 * i + u) * P, P)]).then_inc(self.rest_staged, 1)
                    pool.wait_ge(self.rest_staged, 2 * n + 1)
                    pool.tensor_tensor(self.count_rest[:], self.count_whole[:],
                                       self.count_tile[u][:].bitcast(F32), ALU.subtract).then_inc(self.rest_staged, 1)
                pool.wait_ge(self.turned_h, n + 1)
                pool.tensor_copy(self.h_tile[u][:], h[:, bass.ds(2 * i + u, 1), :].rearrange("p a d -> p (a d)")).then_inc(self.staged, 1)

    def pe_credits(self, pe):
        pe.sem_inc(self.turned_h, 2)
        pe.sem_inc(self.summed, 2)
        pe.sem_inc(self.turned_m, 2)
        pe.sem_inc(self.multiplied, 2)

    def act_credits(self, act):
        act.sem_inc(self.mean, 2)

    def dve_credits(self, dve):
        dve.sem_inc(self.low_h, 1)
        dve.sem_inc(self.low_m, 1)
        dve.sem_inc(self.finished, 2)

    def pe_gather(self, pe, c, n, u, rests, first=False):
        pe.wait_ge(self.staged, 2 * n + 2)
        pe.wait_ge(self.low_h, n + 1)
        for k in range(KD):
            last = pe.transpose(self.ps_h[:, k, :], self.h_tile[u][:, k * P:(k + 1) * P], c["ident"][:])
        last.then_inc(self.turned_h, 1)
        pe.wait_ge(self.mean, n + 1)
        for j in range(NT):
            if first:
                pe.wait_ge(self.cut_low, n + j + 1)
            if j == NT - 1:
                with pe.If(rests):
                    pe.wait_ge(self.rest_staged, 2 * n + 2)
                    for i in range(NT):
                        pe.matmul(self.ps_sum[u][:], self.count_rest[:, i, :], self.high[:, i, :], start=False, stop=False)
            for part, h in enumerate((self.high, self.low)):
                last = pe.matmul(self.ps_sum[u][:], self.count_tile[u][:, j, :], h[:, j, :],
                                 start=(j == 0 and part == 0), stop=(j == NT - 1 and part == 1))
        if self.degrees:
            pe.wait_ge(self.partial_ready, n + 1)
            last = pe.matmul(self.ps_degree[:, 0:1], self.partial[:], c["ones"][:, 0:1], start=True, stop=True)
        last.then_inc(self.summed, 1)

    def products(self, pe, u, high, low, first, start, stop):
        for k in range(KD):
            w = first + k
            pe.matmul(self.ps_y[u][:], high[:, k, :], self.w_high[:, w, :], start=(start and k == 0), stop=False)
            pe.matmul(self.ps_y[u][:], high[:, k, :], self.w_low[:, w, :], start=False, stop=False)
            last = pe.matmul(self.ps_y[u][:], low[:, k, :], self.w_high[:, w, :], start=False,
                             stop=(stop and k == KD - 1))
        return last

    def pe_tile(self, pe, c, n, u, rests, more):
        pe.wait_ge(self.low_h, n + 2)
        pe.wait_ge(self.finished, n + 1)
        self.products(pe, u, self.ht_high[u], self.ht_low[u], 0, True, False)
        pe.wait_ge(self.mean, n + 3)
        pe.wait_ge(self.low_m, n + 1)
        for k in range(KD):
            last = pe.transpose(self.ps_m[:, k, :], self.mean_tile[u][:, k * P:(k + 1) * P], c["ident"][:])
        last.then_inc(self.turned_m, 1)
        if more:
            self.pe_gather(pe, c, n + 1, 1 - u, rests)
        pe.wait_ge(self.low_m, n + 2)
        self.products(pe, u, self.mt_high[u], self.mt_low[u], KD, False, True).then_inc(self.multiplied, 1)

    def pe_tiles(self, pe, c, before, rests, w_cut, parts):
        self.pe_gather(pe, c, before, 0, rests, first=True)
        pe.wait_ge(w_cut, parts)
        pe.sem_inc(self.carrier, 1)
        with pe.Fori(0, NT // 2 - 1) as i:
            for u in range(2):
                self.pe_tile(pe, c, before + 2 * i + u, u, rests, True)
        self.pe_tile(pe, c, before + NT - 2, 0, rests, True)
        self.pe_tile(pe, c, before + NT - 1, 1, rests, False)

    def act_tiles(self, act, inverse, before):
        with act.Fori(0, NT // 2) as i:
            for u in range(2):
                n = before + 2 * i + u
                act.wait_ge(self.turned_h, n + 3)
                act.wait_ge(self.multiplied, n + 1)
                act.copy(self.ht_high[u][:], self.ps_h[:]).then_inc(self.high_h, 1)
                if self.degrees:
                    act.wait_ge(self.degree_ready, 2 * n + 2)
                act.wait_ge(self.summed, n + 3)
                act.wait_ge(self.turned_m, n + 1)
                act.activation(self.mean_tile[u][:], self.ps_sum[u][:], ACT.Copy,
                               scale=inverse[:, bass.ds(2 * i + u, 1)]).then_inc(self.mean, 1)
                act.wait_ge(self.turned_m, n + 3)
                act.copy(self.mt_high[u][:], self.ps_m[:]).then_inc(self.high_m, 1)

    def dve_partial(self, dve, counts, t):
        dve.tensor_reduce(self.partial[:], counts[:, :, bass.ds(t * P, P)].rearrange("p s d -> p d s"), AX.X,
                          ALU.add).then_inc(self.partial_ready, 1)

    def dve_degree(self, dve, inverse, t):
        dve.wait_ge(self.summed, t + 3)
        dve.tensor_scalar(self.degree[:], self.ps_degree[:, 0:1], 1.0, None, ALU.max).then_inc(self.degree_ready, 1)
        dve.wait_ge(self.degree_ready, 2 * t + 1)
        dve.reciprocal(inverse[:, bass.ds(t, 1)], self.degree[:]).then_inc(self.degree_ready, 1)

    def dve_cut_h(self, dve, n, u):
        dve.wait_ge(self.high_h, n + 1)
        dve.tensor_tensor(self.ht_low[u][:], self.ps_h[:], self.ht_high[u][:].bitcast(F32), ALU.subtract).then_inc(self.low_h, 1)

    def dve_tile(self, dve, t, n, u, finish, counts, inverse, more):
        dve.wait_ge(self.high_m, n + 1)
        dve.tensor_tensor(self.mt_low[u][:], self.ps_m[:], self.mt_high[u][:].bitcast(F32), ALU.subtract).then_inc(self.low_m, 1)
        if more:
            if self.degrees:
                self.dve_partial(dve, counts, t + 1)
            self.dve_cut_h(dve, n + 1, 1 - u)
            if self.degrees:
                self.dve_degree(dve, inverse, t + 1)
        dve.wait_ge(self.multiplied, n + 3)
        finish(dve, t, n, u).then_inc(self.finished, 1)

    def dve_tiles(self, dve, before, finish, counts=None, inverse=None):
        if self.degrees:
            self.dve_partial(dve, counts, 0)
        self.dve_cut_h(dve, before, 0)
        if self.degrees:
            self.dve_degree(dve, inverse, 0)
        with dve.Fori(0, NT // 2 - 1) as i:
            for u in range(2):
                self.dve_tile(dve, 2 * i + u, before + 2 * i + u, u, finish, counts, inverse, True)
        self.dve_tile(dve, NT - 2, before + NT - 2, 0, finish, counts, inverse, True)
        self.dve_tile(dve, NT - 1, before + NT - 1, 1, finish, counts, inverse, False)


def sage_layer(nc, c, w, h, x, counts, crowded, inverse):
    with Stage(nc, "sage") as s:
        g = Sage(s, c, crowded, degrees=True)
        natural = s.sbuf("w_natural", [P, KD, 2 * D], F32)
        loaded, turned, w_high, w_low = s.sem("w_loaded"), s.sem("w_turned"), s.sem("w_high_cut"), s.sem("w_low_cut")
        with nc.Block() as block:
            @block.sync
            def _(sp):
                sp.dma_start(natural[:], w.rearrange("(o p) f -> p o f", p=P)).then_inc(loaded, 16)

            @block.gpsimd
            def _(pool):
                g.pool_tiles(pool, counts, h, 0, g.has_rests(pool))

            @block.scalar
            def _(act):
                g.act_credits(act)
                for k in range(2 * KD):
                    act.wait_ge(turned, k + 1)
                    act.copy(g.w_high[:, k, :], g.ps_y[k % 2][:]).then_inc(w_high, 1)
                g.act_cut(act, h)
                g.act_tiles(act, inverse, 0)

            @block.vector
            def _(dve):
                g.dve_credits(dve)
                for k in range(2 * KD):
                    dve.wait_ge(w_high, k + 1)
                    dve.tensor_tensor(g.w_low[:, k, :], g.ps_y[k % 2][:], g.w_high[:, k, :].bitcast(F32),
                                      ALU.subtract).then_inc(w_low, 1)
                g.dve_cut(dve, h, 0)

                def finish(dve, t, n, u):
                    at = x[:, bass.ds(t, 1), :].rearrange("p a d -> p (a d)")
                    return dve.scalar_tensor_tensor(at, g.ps_y[u][:], 0.0, at, ALU.max, ALU.add)

                g.dve_tiles(dve, 0, finish, counts, inverse)

            @block.tensor
            def _(pe):
                g.pe_credits(pe)
                rests = g.has_rests(pe)
                pe.wait_ge(loaded, 16)
                for k in range(2 * KD):
                    if k >= 2:
                        pe.wait_ge(w_low, k - 1)
                    for o in range(KD):
                        last = pe.transpose(g.ps_y[k % 2][:, o * P:(o + 1) * P], natural[:, o, k * P:(k + 1) * P], c["ident"][:])
                    last.then_inc(turned, 1)
                g.pe_tiles(pe, c, 0, rests, w_low, 2 * KD)


def graph_layers(nc, c, ws, wn, bs, h, counts, crowded, inverse):
    L = ws.shape[0]
    with Stage(nc, "layers") as s:
        g = Sage(s, c, crowded)
        w = s.sbuf("w_whole", [P, 2 * KD, D], F32)
        bias = s.sbuf("layer_bias", [P, L, D], F32)
        floor = s.sbuf("relu_floor", [P, L], F32)
        y = s.sbuf("y_with_bias", [P, D], F32)
        loaded, biased, extra = s.sem("w_loaded"), s.sem("y_biased"), s.sem("layer_extra")
        w_high = s.sem("w_high_cut")
        w_low = s.sem("w_low_cut")
        with nc.Block() as block:
            @block.sync
            def _(sp):
                sp.dma_start(bias[:], bs.rearrange("l d -> (l d)").partition_broadcast(P)).then_inc(extra, 16)
                with sp.Fori(0, L) as l:
                    sp.wait_ge(w_low, 2 * KD * (l + 1))
                    sp.dma_start(w[:, 0:KD, :], ws[bass.ds(l, 1), :, :].rearrange("l (k p) d -> p (l k) d", p=P)).then_inc(loaded, 16)
                    sp.dma_start(w[:, KD:2 * KD, :], wn[bass.ds(l, 1), :, :].rearrange("l (k p) d -> p (l k) d", p=P)).then_inc(loaded, 16)

            @block.gpsimd
            def _(pool):
                pool.memset(floor[:, 0:L - 1], 0.0).then_inc(extra, 1)
                pool.memset(floor[:, L - 1:L], -3.4e38).then_inc(extra, 1)
                rests = g.has_rests(pool)
                with pool.Fori(0, L) as l:
                    g.pool_tiles(pool, counts, h, l * NT, rests)

            @block.scalar
            def _(act):
                g.act_credits(act)
                with act.Fori(0, L) as l:
                    act.wait_ge(g.finished, l * NT + 2)
                    g.act_cut(act, h)
                    act.wait_ge(loaded, 32 * l + 32)
                    for k in range(2 * KD):
                        act.copy(g.w_high[:, k, :], w[:, k, :]).then_inc(w_high, 1)
                    g.act_tiles(act, inverse, l * NT)

            @block.vector
            def _(dve):
                g.dve_credits(dve)
                dve.sem_inc(w_low, 2 * KD)
                dve.wait_ge(extra, 18)
                with dve.Fori(0, L) as l:
                    g.dve_cut(dve, h, l * NT)
                    for k in range(2 * KD):
                        dve.wait_ge(w_high, 2 * KD * l + k + 1)
                        dve.tensor_tensor(g.w_low[:, k, :], w[:, k, :], g.w_high[:, k, :].bitcast(F32), ALU.subtract).then_inc(w_low, 1)

                    def finish(dve, t, n, u):
                        dve.wait_ge(g.finished, n + 2)
                        dve.tensor_tensor(y[:], g.ps_y[u][:], bias[:, bass.ds(l, 1), :].rearrange("p a d -> p (a d)"),
                                          ALU.add).then_inc(biased, 1)
                        dve.wait_ge(biased, n + 1)
                        return dve.tensor_scalar(h[:, bass.ds(t, 1), :].rearrange("p a d -> p (a d)"), y[:],
                                                 floor[:, bass.ds(l, 1)], None, ALU.max)

                    g.dve_tiles(dve, l * NT, finish)

            @block.tensor
            def _(pe):
                g.pe_credits(pe)
                rests = g.has_rests(pe)
                with pe.Fori(0, L) as l:
                    g.pe_tiles(pe, c, l * NT, rests, w_low, 2 * KD * (l + 2))


def router_logits(nc, c, tag, h, w, b, E, logits, rows, affine=None):
    with Stage(nc, tag) as s:
        w_rows = s.sbuf("w_rows", [E, D], F32)
        w_t = s.sbuf("w_t", [P, KD, E], F32)
        bias = s.sbuf("bias", [P, E], F32)
        tile_t = [s.sbuf(f"tile_t_{u}", [P, KD, P], F32) for u in range(2)]
        gain = s.sbuf("gain", [P, D], F32)
        shift = s.sbuf("shift", [P, D], F32)
        ps_w = s.psum("ps_w", [P, 512])
        ps_t = [s.psum(f"ps_t_{u}", [P, KD, P]) for u in range(2)]
        ps_l = s.psum("ps_l", [P, NT, E])
        loaded, w_turned, w_ready = s.sem("loaded"), s.sem("w_turned"), s.sem("w_ready")
        scaled, shifted = s.sem("scaled"), s.sem("shifted")
        turned, product = s.sem("turned"), s.sem("product")
        taken, done = s.sem("taken"), s.sem("done")
        summed, stored = s.sem("summed"), s.sem("stored")
        loads = 4 if affine else 2
        with nc.Block() as block:
            @block.sync
            def _(sp):
                if affine:
                    sp.dma_start(gain[:], affine[0].partition_broadcast(P)).then_inc(loaded, 16)
                    sp.dma_start(shift[:], affine[1].partition_broadcast(P)).then_inc(loaded, 16)
                sp.dma_start(w_rows[:], w).then_inc(loaded, 16)
                sp.dma_start(bias[:], b.partition_broadcast(P)).then_inc(loaded, 16)
                for t in range(NT):
                    if affine:
                        sp.wait_ge(shifted, t + 1)
                    sp.dma_start(rows[t * P:(t + 1) * P, :], h[:, t, :]).then_inc(stored, 16)
                sp.wait_ge(stored, 16 * NT)

            @block.gpsimd
            def _(pool):
                if affine:
                    for t in range(NT):
                        pool.tensor_tensor(affine[3][:, t, :], affine[3][:, t, :], affine[2][:, t, :], ALU.add).then_inc(summed, 1)

            @block.scalar
            def _(act):
                for t in range(NT):
                    act.wait_ge(turned, t + 1)
                    if t >= 2:
                        act.wait_ge(product, t - 1)
                    act.copy(tile_t[t % 2][:], ps_t[t % 2][:]).then_inc(taken, 1)

            @block.vector
            def _(dve):
                if affine:
                    dve.wait_ge(loaded, 16 * loads)
                    for t in range(NT + 1):
                        if t < NT:
                            dve.tensor_tensor(h[:, t, :], h[:, t, :], gain[:], ALU.mult).then_inc(scaled, 1)
                        if t >= 1:
                            dve.wait_ge(scaled, t)
                            dve.tensor_tensor(h[:, t - 1, :], h[:, t - 1, :], shift[:], ALU.add).then_inc(shifted, 1)
                        if t == 0:
                            dve.wait_ge(w_turned, 1)
                            dve.tensor_copy(w_t[:], ps_w[:, 0:KD * E].rearrange("p (k e) -> p k e", e=E)).then_inc(w_ready, 1)
                else:
                    dve.wait_ge(w_turned, 1)
                    dve.tensor_copy(w_t[:], ps_w[:, 0:KD * E].rearrange("p (k e) -> p k e", e=E)).then_inc(w_ready, 1)
                    dve.wait_ge(loaded, 16 * loads)
                dve.wait_ge(product, NT)
                dve.tensor_tensor(logits[:], ps_l[:], bias[:].unsqueeze(1).to_broadcast([P, NT, E]), ALU.add).then_inc(done, 1)

            @block.tensor
            def _(pe):
                pe.wait_ge(loaded, 16 * loads)
                for k in range(KD):
                    last = pe.transpose(ps_w[:, k * E:(k + 1) * E], w_rows[:, k * P:(k + 1) * P], c["ident"][0:E, 0:E])
                last.then_inc(w_turned, 1)
                for t in range(NT + 1):
                    if t < NT:
                        if affine:
                            pe.wait_ge(shifted, t + 1)
                        if t >= 2:
                            pe.wait_ge(taken, t - 1)
                        for k in range(KD):
                            last = pe.transpose(ps_t[t % 2][:, k, :], h[:, t, k * P:(k + 1) * P], c["ident"][:])
                        last.then_inc(turned, 1)
                    if t >= 1:
                        if t == 1:
                            pe.wait_ge(w_ready, 1)
                        pe.wait_ge(taken, t)
                        for k in range(KD):
                            last = pe.matmul(ps_l[:, t - 1, :], tile_t[(t - 1) % 2][:, k, :], w_t[:, k, :],
                                             start=(k == 0), stop=(k == KD - 1))
                        last.then_inc(product, 1)


def rank_tokens(nc, c, tag, member, E, rank, total):
    with Stage(nc, tag) as s:
        ps = s.psum("ps_ranks", [P, 2, 256])
        step, summed = s.sem("step"), s.sem("summed")
        flat = member[:].rearrange("p t e -> p (t e)")
        before = s.sbuf("before", [P, NT, E], F32)
        W = NT * E
        with nc.Block() as block:
            @block.tensor
            def _(pe):
                pe.matmul(ps[:, 0, 0:W], c["upper"][:], flat, start=True, stop=True).then_inc(summed, 1)
                pe.matmul(ps[:, 1, 0:W], c["ones"][:], flat, start=True, stop=True).then_inc(summed, 1)

            @block.vector
            def _(dve):
                whole = ps[:, 1, 0:W].rearrange("p (t e) -> p t e", e=E)
                dve.memset(before[:, 0, :], 0.0).then_inc(step, 1)
                dve.wait_ge(summed, 2)
                for t in range(1, NT):
                    dve.wait_ge(step, t)
                    dve.tensor_tensor(before[:, t, :], whole[:, t - 1, :], before[:, t - 1, :], ALU.add).then_inc(step, 1)
                dve.wait_ge(step, NT)
                dve.tensor_tensor(total[:], whole[:, NT - 1, :], before[:, NT - 1, :], ALU.add).then_inc(step, 1)
                dve.tensor_tensor(rank[:], ps[:, 0, 0:W].rearrange("p (t e) -> p t e", e=E), before[:], ALU.add).then_inc(step, 1)


def choose(dve, step, at, logits, best, where):
    for t in range(NT):
        dve.max(best[:, t, :], logits[:, t, :]).then_inc(step, 1)
    for t in range(NT):
        dve.wait_ge(step, at + t + 1)
        dve.max_index(where[:, t, :], best[:, t, :], logits[:, t, :]).then_inc(step, 1)


def store_list(nc, tag, ids, node, slots, columns, beside):
    n_rows = ids.shape[0]
    with Stage(nc, tag) as s:
        zeros = s.sbuf("zeros", [n_rows // P, P], I32)
        filled, stored = s.sem("filled"), s.sem("stored")
        with nc.Block() as block:
            @block.sync
            def _(sp):
                beside(sp)

            @block.gpsimd
            def _(pool):
                pool.memset(zeros[:], 0).then_inc(filled, 1)
                pool.wait_ge(filled, 1)
                pool.dma_start(ids.rearrange("(c p) o -> c (p o)", p=P), zeros[:]).then_inc(stored, 16)
                pool.wait_ge(stored, 16)
                for i in range(columns):
                    t = i % NT
                    real = P if t < NT - 1 else LAST
                    pool.indirect_dma_start(ids, bass.IndirectOffsetOnAxis(ap=slots[0:real, i:i + 1], axis=0),
                                            node[0:real, t:t + 1], None).then_inc(stored, 16)
                pool.wait_ge(stored, 16 * (columns + 1))


def load_list(nc, c, tag, ids, list_t):
    blocks = ids.shape[0] // P
    with Stage(nc, tag) as s:
        rows_i = s.sbuf("rows_i", [blocks, P], I32)
        rows = s.sbuf("rows", [blocks, P], F32)
        ps = s.psum("ps", [P, 512])
        loaded, step, turned = s.sem("loaded"), s.sem("step"), s.sem("turned")
        with nc.Block() as block:
            @block.sync
            def _(sp):
                sp.dma_start(rows_i[:], ids.rearrange("(c p) o -> c (p o)", p=P)).then_inc(loaded, 16)

            @block.vector
            def _(dve):
                dve.wait_ge(loaded, 16)
                dve.tensor_copy(rows[:], rows_i[:]).then_inc(step, 1)
                dve.wait_ge(turned, 1)
                dve.tensor_copy(list_t[:], ps[:, 0:blocks]).then_inc(step, 1)

            @block.tensor
            def _(pe):
                pe.wait_ge(step, 1)
                pe.transpose(ps[:, 0:blocks], rows[:], c["ident"][0:blocks, 0:blocks]).then_inc(turned, 1)


def route_top2(nc, c, h, w_r, b_r, rows, affine, gates, slots, unit_expert, unit_tokens, n_units):
    E = E1
    with Stage(nc, "top2") as s:
        logits = s.sbuf("logits", [P, NT, E], F32)
        best = s.sbuf("best", [P, NT, 8], F32)
        where = s.sbuf("where", [P, NT, 8], U32)
        column = s.sbuf("expert_column", [P, NT, E], F32)
        chosen = s.sbuf("chosen", [P, 2, NT], F32)
        one = [s.sbuf(f"onehot_{k}", [P, NT, E], F32) for k in range(2)]
        member = s.sbuf("member", [P, NT, E], F32)
        rank = s.sbuf("rank", [P, NT, E], F32)
        total = s.sbuf("total", [P, E], F32)
        gap = s.sbuf("gap", [P, NT], F32)
        small = s.sbuf("small_exp", [P, NT], F32)
        started, step, risen = s.sem("started"), s.sem("step"), s.sem("risen")
        router_logits(nc, c, "logits2", h, w_r, b_r, E, logits, rows, affine)
        with nc.Block() as block:
            @block.gpsimd
            def _(pool):
                pool.iota(column[:], pattern=[[0, NT], [1, E]], base=0, channel_multiplier=0,
                          allow_small_or_imprecise_dtypes=True).then_inc(started, 1)

            @block.vector
            def _(dve):
                choose(dve, step, 0, logits, best, where)
                n = 2 * NT
                dve.wait_ge(step, n)
                dve.tensor_tensor(gap[:], best[:, :, 1], best[:, :, 0], ALU.subtract).then_inc(step, 1)
                for k in range(2):
                    dve.tensor_copy(chosen[:, k, :], where[:, :, k]).then_inc(step, 1)
                dve.wait_ge(step, n + 3)
                dve.wait_ge(started, 1)
                for k in range(2):
                    dve.tensor_tensor(one[k][:], column[:], chosen[:, k, :].unsqueeze(2).to_broadcast([P, NT, E]),
                                      ALU.is_equal).then_inc(step, 1)
                dve.wait_ge(step, n + 5)
                dve.tensor_tensor(member[:], one[0][:], one[1][:], ALU.add).then_inc(step, 1)
                dve.wait_ge(step, n + 6)
                dve.tensor_tensor(member[:], member[:], c["real"][:].unsqueeze(2).to_broadcast([P, NT, E]), ALU.mult).then_inc(step, 1)
                dve.wait_ge(risen, 1)
                dve.tensor_scalar(gates[:, 0, :], small[:], 1.0, None, ALU.add).then_inc(step, 1)
                dve.wait_ge(step, n + 8)
                dve.reciprocal(gates[:, 0, :], gates[:, 0, :]).then_inc(step, 1)
                dve.wait_ge(step, n + 9)
                dve.tensor_tensor(gates[:, 1, :], gates[:, 0, :], small[:], ALU.mult).then_inc(step, 1)

            @block.scalar
            def _(act):
                act.wait_ge(step, 2 * NT + 1)
                act.activation(small[:], gap[:], ACT.Exp).then_inc(risen, 1)
        rank_tokens(nc, c, "rank2", member, E, rank, total)
        units = s.sbuf("units", [P, E], F32)
        above = s.sbuf("above", [P, E], F32)
        ends = s.sbuf("unit_ends", [P, E], F32)
        starts = s.sbuf("unit_starts", [P, E], F32)
        ones = s.sbuf("ones_e", [P, E], F32)
        product = s.sbuf("product", [P, NT, E], F32)
        slot = s.sbuf("slot", [P, 2, NT], F32)
        unit_no = s.sbuf("unit_no", [1, UNITS + 1, E], F32)
        begun = s.sbuf("unit_begun", [1, UNITS + 1, E], F32)
        over = s.sbuf("unit_over", [1, UNITS + 1, E], F32)
        rest = s.sbuf("expert_rest", [1, UNITS + 1, E], F32)
        held = s.sbuf("unit_held", [1, UNITS + 1], F32)
        passed = s.sbuf("units_passed", [1, UNITS + 1], F32)
        with nc.Block() as block:
            step, began = s.sem("slot_step"), s.sem("slot_began")

            @block.gpsimd
            def _(pool):
                pool.iota(unit_no[:], pattern=[[1, UNITS + 1], [0, E]], base=0, channel_multiplier=0,
                          allow_small_or_imprecise_dtypes=True).then_inc(began, 1)
                pool.memset(ones[:], 1.0).then_inc(began, 1)

            @block.vector
            def _(dve):
                dve.wait_ge(began, 2)
                dve.tensor_scalar(units[:], total[:], 0.0, None, ALU.is_gt).then_inc(step, 1)
                n = 1
                for b in range(1, -(-N // T)):
                    dve.tensor_scalar(above[:], total[:], float(b * T), None, ALU.is_gt).then_inc(step, 1)
                    dve.wait_ge(step, n + 1)
                    dve.tensor_tensor(units[:], units[:], above[:], ALU.add).then_inc(step, 1)
                    n += 2
                    dve.wait_ge(step, n)
                dve.tensor_tensor_scan(ends[:], ones[:], units[:], 0.0, ALU.mult, ALU.add).then_inc(step, 1)
                dve.wait_ge(step, n + 1)
                dve.tensor_tensor(starts[:], ends[:], units[:], ALU.subtract).then_inc(step, 1)
                dve.wait_ge(step, n + 2)
                dve.tensor_scalar(starts[:], starts[:], float(T), None, ALU.mult).then_inc(step, 1)
                dve.wait_ge(step, n + 3)
                dve.tensor_tensor(rank[:], rank[:], starts[:].unsqueeze(1).to_broadcast([P, NT, E]), ALU.add).then_inc(step, 1)
                n += 4
                dve.wait_ge(step, n)
                for k in range(2):
                    dve.tensor_tensor(product[:], one[k][:], rank[:], ALU.mult).then_inc(step, 1)
                    dve.wait_ge(step, n + 1)
                    dve.tensor_reduce(slot[:, k, :], product[:], AX.X, ALU.add).then_inc(step, 1)
                    dve.wait_ge(step, n + 2)
                    dve.tensor_tensor(slots[:, k * NT:(k + 1) * NT], slot[:, k, :], c["real"][:], ALU.mult).then_inc(step, 1)
                    n += 3
                wide = [1, UNITS + 1, E]
                dve.tensor_tensor(over[:], unit_no[:], ends[0:1, :].unsqueeze(1).to_broadcast(wide), ALU.is_ge).then_inc(step, 1)
                dve.tensor_scalar(rest[:], unit_no[:], float(-T), None, ALU.mult).then_inc(step, 1)
                dve.tensor_tensor(total[:], total[:], starts[:], ALU.add).then_inc(step, 1)
                dve.wait_ge(step, n + 3)
                dve.tensor_reduce(passed[:], over[:], AX.X, ALU.add).then_inc(step, 1)
                dve.tensor_tensor(begun[:], rest[:], starts[0:1, :].unsqueeze(1).to_broadcast(wide), ALU.add).then_inc(step, 1)
                dve.tensor_tensor(rest[:], rest[:], total[0:1, :].unsqueeze(1).to_broadcast(wide), ALU.add).then_inc(step, 1)
                dve.wait_ge(step, n + 6)
                dve.tensor_scalar(begun[:], begun[:], 0.0, None, ALU.is_le).then_inc(step, 1)
                dve.tensor_scalar(unit_expert[:], passed[:], float(E - 1), None, ALU.min).then_inc(step, 1)
                dve.tensor_copy(n_units[:], ends[0:1, E - 1:E]).then_inc(step, 1)
                dve.wait_ge(step, n + 9)
                dve.tensor_tensor(begun[:], begun[:], over[:], ALU.subtract).then_inc(step, 1)
                dve.wait_ge(step, n + 10)
                dve.tensor_tensor(rest[:], rest[:], begun[:], ALU.mult).then_inc(step, 1)
                dve.wait_ge(step, n + 11)
                dve.tensor_reduce(held[:], rest[:], AX.X, ALU.add).then_inc(step, 1)
                dve.wait_ge(step, n + 12)
                dve.tensor_scalar(unit_tokens[:], held[:], float(T), None, ALU.min).then_inc(step, 1)


def top2_experts(nc, c, rows, W1, b1, W2, b2, unit_expert, unit_tokens, n_units, ids, slots, list_t, y_rows):
    NB = TB
    with Stage(nc, "ffn") as s:
        raw1 = [s.sbuf(f"w1_raw_{u}", [P, KD, FB], F32) for u in range(2)]
        raw2 = [s.sbuf(f"w2_raw_{u}", [P, KD, D], F32) for u in range(2)]
        w1h = [s.sbuf(f"w1_high_{u}", [P, KD, FB], F32R) for u in range(2)]
        w1l = [s.sbuf(f"w1_low_{u}", [P, KD, FB], F32R) for u in range(2)]
        w2h = [s.sbuf(f"w2_high_{u}", [P, KD, D], F32R) for u in range(2)]
        w2l = [s.sbuf(f"w2_low_{u}", [P, KD, D], F32R) for u in range(2)]
        token = [s.sbuf(f"token_{j}", [P, D], F32) for j in range(NB)]
        index = [s.sbuf(f"index_{j}", [P, 1], I32) for j in range(NB)]
        xh = s.sbuf("x_high", [P, KD, T], F32R)
        xl = s.sbuf("x_low", [P, KD, T], F32R)
        hid = s.sbuf("hidden", [P, KD, T], F32)
        hh = s.sbuf("hidden_high", [P, KD, T], F32R)
        hl = s.sbuf("hidden_low", [P, KD, T], F32R)
        y = s.sbuf("y", [P, NB, D], F32)
        bias1_rows = s.sbuf("b1_rows", [P, P], F32)
        bias1 = s.sbuf("b1_t", [P, E1 * F1 // P], F32)
        bias2 = s.sbuf("b2", [P, D], F32)
        ps_h = [s.psum(f"ps_hidden_{u}", [P, 512]) for u in range(2)]
        ps_y = [s.psum(f"ps_y_{j}", [P, D]) for j in range(NB)]
        ps_x = s.psum("ps_x", [P, KD, P])
        W = 2 * KD
        biases, turned_b, biases_t = s.sem("biases"), s.sem("b1_turned"), s.sem("b1_ready")
        loaded = [s.sem(f"w_loaded_{u}") for u in range(2)]
        gathered = [s.sem(f"gathered_{j}") for j in range(NB)]
        index_set = s.sem("index_set")
        w_high = s.sem("w_high")
        w_low = s.sem("w_low")
        turned = s.sem("x_turned")
        x_high = s.sem("x_high_ready")
        x_low = s.sem("x_low_ready")
        first = s.sem("first_product")
        gelu = s.sem("gelu_done")
        h_high = s.sem("hidden_high_ready")
        h_low = s.sem("hidden_low_ready")
        second = s.sem("second_product")
        biased = s.sem("y_biased")
        stored = s.sem("y_stored")
        all_stored = s.sem("all_stored")
        bias2_in = s.sem("b2_loaded")
        cleared = s.sem("ps_cleared")

        def each_unit(eng, body):
            units = eng.value_load(n_units[0:1, 0:1], min_val=0, max_val=UNITS)
            with eng.Fori(0, UNITS) as v:
                with eng.If(units > v):
                    body(v)
            return units

        def expert_of(eng, v):
            return eng.value_load(unit_expert[0:1, bass.ds(v, 1)], min_val=0, max_val=E1 - 1)

        def load(sp, v, f, after=None):
            e, u = expert_of(sp, v), f % 2
            if after is not None:
                sp.wait_ge(w_low, after)
            sp.dma_start(raw1[u][:], W1[bass.ds(e, 1), :, f * FB:(f + 1) * FB].rearrange("e (k p) f -> p (e k) f", p=P)).then_inc(loaded[u], 16)
            sp.dma_start(raw2[u][:], W2[bass.ds(e, 1), f * FB:(f + 1) * FB, :].rearrange("e (k p) d -> p (e k) d", p=P)).then_inc(loaded[u], 16)

        def load_bias2(sp, v):
            e = expert_of(sp, v)
            sp.dma_start(bias2[:], b2[bass.ds(e, 1), :].rearrange("e d -> (e d)").partition_broadcast(P)).then_inc(bias2_in, 16)

        def first_loads(sp):
            sp.dma_start(bias1_rows[:], b1.rearrange("e (c f) -> (e c) f", f=P)).then_inc(biases, 16)
            load(sp, 0, 0)
            load(sp, 0, 1)
            load_bias2(sp, 0)

        store_list(nc, "list2", ids, c["node"], slots, 2 * NT, first_loads)
        load_list(nc, c, "loadlist2", ids, list_t)
        with nc.Block() as block:
            @block.sync
            def _(sp):
                def load_after(v, f):
                    load(sp, v, f, after=W * (NFB * v + f) + W)

                def unit(v):
                    load_after(v, 2)
                    load_after(v, 3)
                    load_after(v + 1, 0)
                    load_after(v + 1, 1)
                    sp.wait_ge(biased, NB * v + 2 * NB)
                    sp.dma_start(y_rows[bass.ds(v * T, T), :].rearrange("(j p) d -> p j d", p=P), y[:]).then_inc(stored, 16)
                    load_bias2(sp, v + 1)

                units = each_unit(sp, unit)
                sp.wait_ge(stored, 16 * units + 16)
                sp.wait_ge(loaded[1], 64 * units + 32)
                sp.wait_ge(bias2_in, 16 * units + 16)
                sp.sem_inc(all_stored, 1)

            @block.gpsimd
            def _(pool):
                def gather(v):
                    for j in range(NB):
                        pool.wait_ge(turned, NB * v + j + 1)
                        pool.tensor_copy(index[j][:], list_t[:, bass.ds(NB * v + j, 1)]).then_inc(index_set, 1)
                        pool.wait_ge(index_set, NB * v + j + 1)
                        pool.sem_inc(c["carrier"], 1)
                        pool.indirect_dma_start(token[j][:], None, rows, bass.IndirectOffsetOnAxis(ap=index[j][:, 0:1], axis=0)).then_inc(gathered[j], 16)

                gather(0)
                each_unit(pool, lambda v: gather(v + 1))

            @block.scalar
            def _(act):
                act.sem_inc(gelu, 2)

                def cut_w(part, u, k):
                    raw, high = ((raw1, w1h), (raw2, w2h))[part]
                    act.copy(high[u][:, k, :], raw[u][:, k, :]).then_inc(w_high, 1)

                def cut_x(v, j):
                    act.wait_ge(turned, NB * v + j + 1 + NB)
                    act.copy(xh[:, :, j * P:(j + 1) * P], ps_x[:]).then_inc(x_high, 1)

                act.wait_ge(loaded[0], 32)
                for k in range(2 * KD):
                    cut_w(k // KD, 0, k % KD)
                act.wait_ge(biases_t, 1)
                for j in range(NB):
                    cut_x(0, j)
                act.wait_ge(cleared, NB + 2)

                def unit(v):
                    e = expert_of(act, v)
                    for f in range(NFB):
                        n = NFB * v + f
                        nu = (f + 1) % 2
                        for m in range(KD):
                            q = 4 * n + m
                            act.wait_ge(first, q + 1)
                            act.wait_ge(h_low, q + 1)
                            act.activation(hid[:, m, :], ps_h[m % 2][:], ACT.Gelu,
                                           bias=bias1[:, bass.ds(e * (F1 // P) + f * KD + m, 1)]).then_inc(gelu, 1)
                            act.wait_ge(gelu, q + 3)
                            act.wait_ge(second, q + 1)
                            act.copy(hh[:, m, :], hid[:, m, :]).then_inc(h_high, 1)
                        act.wait_ge(loaded[nu], 64 * v + 32 * ((f + 1) // 2) + 32)
                        act.wait_ge(second, 4 * n + 4)
                        for k in range(KD):
                            if f == NFB - 1:
                                cut_x(v + 1, k)
                            cut_w(0, nu, k)
                        for k in range(KD):
                            cut_w(1, nu, k)

                each_unit(act, unit)

            @block.vector
            def _(dve):
                dve.sem_inc(w_low, 2 * W)
                dve.sem_inc(x_low, 1)
                dve.sem_inc(h_low, 4)
                dve.sem_inc(biased, NB)
                dve.sem_inc(stored, 16)

                def cut_w(n, part, u, k):
                    raw, high, low = ((raw1, w1h, w1l), (raw2, w2h, w2l))[part]
                    dve.wait_ge(w_high, W * n + KD * part + k + 1)
                    dve.tensor_tensor(low[u][:, k, :], raw[u][:, k, :], high[u][:, k, :].bitcast(F32), ALU.subtract).then_inc(w_low, 1)

                def cut_x(v, j):
                    dve.wait_ge(x_high, NB * v + j + 1)
                    dve.tensor_tensor(xl[:, :, j * P:(j + 1) * P], ps_x[:], xh[:, :, j * P:(j + 1) * P].bitcast(F32),
                                      ALU.subtract).then_inc(x_low, 1)

                for ps in ps_h + ps_y:
                    dve.memset(ps[:], 0.0).then_inc(cleared, 1)
                dve.wait_ge(turned_b, 1)
                dve.tensor_copy(bias1[:], ps_x[:, 0, :]).then_inc(biases_t, 1)
                for k in range(2 * KD):
                    cut_w(0, k // KD, 0, k % KD)
                for j in range(NB):
                    cut_x(0, j)

                def unit(v):
                    for f in range(NFB):
                        n = NFB * v + f
                        for m in range(KD):
                            q = 4 * n + m
                            dve.wait_ge(h_high, q + 1)
                            dve.tensor_tensor(hl[:, m, :], hid[:, m, :], hh[:, m, :].bitcast(F32), ALU.subtract).then_inc(h_low, 1)
                        for k in range(KD):
                            if f == NFB - 1:
                                cut_x(v + 1, k)
                            cut_w(n + 1, 0, (f + 1) % 2, k)
                        for k in range(KD):
                            cut_w(n + 1, 1, (f + 1) % 2, k)
                    dve.wait_ge(second, 4 * NFB * (v + 1) + 4)
                    dve.wait_ge(stored, 16 * v + 16)
                    dve.wait_ge(bias2_in, 16 * v + 16)
                    for j in range(NB):
                        dve.tensor_tensor(y[:, j, :], ps_y[j][:], bias2[:], ALU.add).then_inc(biased, 1)

                each_unit(dve, unit)

            @block.tensor
            def _(pe):
                pe.sem_inc(turned, NB)
                pe.sem_inc(second, 4)
                pe.wait_ge(biases, 16)
                pe.transpose(ps_x[:, 0, :], bias1_rows[:], c["ident"][:]).then_inc(turned_b, 1)
                pe.wait_ge(biases_t, 1)

                def turn(v, j):
                    pe.wait_ge(gathered[j], 16 * v + 16)
                    pe.wait_ge(x_low, NB * v + j + 1)
                    for k in range(KD):
                        last = pe.transpose(ps_x[:, k, :], token[j][:, k * P:(k + 1) * P], c["ident"][:])
                    last.then_inc(turned, 1)

                for j in range(NB):
                    turn(0, j)
                pe.wait_ge(cleared, NB + 2)

                def multiply(v, tiles):
                    width = tiles * P
                    pe.wait_ge(x_low, NB * v + NB + 1)
                    for f in range(NFB):
                        n = NFB * v + f
                        u = f % 2
                        pe.wait_ge(w_low, W * n + KD + 2 * W)
                        for m in range(KD):
                            q = 4 * n + m
                            pe.wait_ge(gelu, q + 1)
                            out = ps_h[m % 2][:, 0:width]
                            for k in range(KD):
                                cols = slice(m * P, (m + 1) * P)
                                pe.matmul(out, w1h[u][:, k, cols], xh[:, k, 0:width], start=(k == 0), stop=False)
                                pe.matmul(out, w1h[u][:, k, cols], xl[:, k, 0:width], start=False, stop=False)
                                last = pe.matmul(out, w1l[u][:, k, cols], xh[:, k, 0:width], start=False, stop=(k == KD - 1))
                            last.then_inc(first, 1)
                        pe.wait_ge(w_low, W * n + W + 2 * W)
                        for m in range(KD):
                            q = 4 * n + m
                            if f == NFB - 1:
                                turn(v + 1, m)
                            pe.wait_ge(h_low, q + 5)
                            if f == 0 and m == 0:
                                pe.wait_ge(biased, NB * v + NB)
                            for j in range(tiles):
                                cols = slice(j * P, (j + 1) * P)
                                pe.matmul(ps_y[j][:], hh[:, m, cols], w2h[u][:, m, :], start=(f == 0 and m == 0), stop=False)
                                pe.matmul(ps_y[j][:], hh[:, m, cols], w2l[u][:, m, :], start=False, stop=False)
                                last = pe.matmul(ps_y[j][:], hl[:, m, cols], w2h[u][:, m, :], start=False,
                                                 stop=(f == NFB - 1 and m == KD - 1))
                            last.then_inc(second, 1)

                def unit(v):
                    tokens = pe.value_load(unit_tokens[0:1, bass.ds(v, 1)], min_val=0, max_val=T)
                    with pe.If(tokens > 3 * P):
                        multiply(v, 4)
                    with pe.Else():
                        with pe.If(tokens > 2 * P):
                            multiply(v, 3)
                        with pe.Else():
                            multiply(v, 2)

                each_unit(pe, unit)


def gather_top2(nc, c, y_rows, slots, gates, nodes):
    with Stage(nc, "mix") as s:
        index = [s.sbuf(f"index_{k}", [P, 1], I32) for k in range(2)]
        y = [s.sbuf(f"y_{k}", [P, D], F32) for k in range(2)]
        index_set = s.sem("index_set")
        gathered = [s.sem(f"gathered_{k}") for k in range(2)]
        mixed = s.sem("mixed")
        with nc.Block() as block:
            @block.gpsimd
            def _(pool):
                with pool.Fori(0, NT) as t:
                    for k in range(2):
                        pool.wait_ge(mixed, 2 * t + k + 1)
                        pool.tensor_copy(index[k][:], slots[:, bass.ds(k * NT + t, 1)]).then_inc(index_set, 1)
                        pool.wait_ge(index_set, 2 * t + k + 1)
                        pool.sem_inc(c["carrier"], 1)
                        pool.indirect_dma_start(y[k][:], None, y_rows, bass.IndirectOffsetOnAxis(ap=index[k][:, 0:1], axis=0)).then_inc(gathered[k], 16)

            @block.vector
            def _(dve):
                dve.sem_inc(mixed, 2)
                with dve.Fori(0, NT) as t:
                    at = nodes[:, bass.ds(t, 1), :].rearrange("p a d -> p (a d)")
                    for k in range(2):
                        dve.wait_ge(gathered[k], 16 * t + 16)
                        dve.wait_ge(mixed, 2 * t + k + 2)
                        dve.scalar_tensor_tensor(at, y[k][:], gates[:, k, bass.ds(t, 1)], at, ALU.mult, ALU.add).then_inc(mixed, 1)


def route_switch(nc, c, h, sw_w, sw_b, rows, keep_weight, pass_weight, places, list_place):
    E = E2
    with Stage(nc, "switch") as s:
        logits = s.sbuf("logits", [P, NT, E], F32)
        best = s.sbuf("best", [P, NT, 8], F32)
        where = s.sbuf("where", [P, NT, 8], U32)
        column = s.sbuf("expert_column", [P, NT, E], F32)
        chosen = s.sbuf("chosen", [P, NT], F32)
        one = s.sbuf("onehot", [P, NT, E], F32)
        member = s.sbuf("member", [P, NT, E], F32)
        rank = s.sbuf("rank", [P, NT, E], F32)
        total = s.sbuf("total", [P, E], F32)
        shifted = s.sbuf("shifted", [P, NT, E], F32)
        powers = s.sbuf("powers", [P, NT, E], F32)
        prob = s.sbuf("prob", [P, NT], F32)
        started, step, risen = s.sem("started"), s.sem("step"), s.sem("risen")
        router_logits(nc, c, "logits1", h, sw_w, sw_b, E, logits, rows)
        with nc.Block() as block:
            @block.gpsimd
            def _(pool):
                pool.iota(column[:], pattern=[[0, NT], [1, E]], base=0, channel_multiplier=0,
                          allow_small_or_imprecise_dtypes=True).then_inc(started, 1)

            @block.vector
            def _(dve):
                choose(dve, step, 0, logits, best, where)
                n = 2 * NT
                dve.wait_ge(step, n)
                dve.tensor_tensor(shifted[:], logits[:], best[:, :, 0:1].to_broadcast([P, NT, E]), ALU.subtract).then_inc(step, 1)
                dve.tensor_copy(chosen[:], where[:, :, 0]).then_inc(step, 1)
                dve.wait_ge(step, n + 2)
                dve.wait_ge(started, 1)
                dve.tensor_tensor(one[:], column[:], chosen[:].unsqueeze(2).to_broadcast([P, NT, E]), ALU.is_equal).then_inc(step, 1)
                dve.wait_ge(step, n + 3)
                dve.tensor_tensor(member[:], one[:], c["real"][:].unsqueeze(2).to_broadcast([P, NT, E]), ALU.mult).then_inc(step, 1)
                dve.wait_ge(risen, 1)
                dve.tensor_reduce(prob[:], powers[:], AX.X, ALU.add).then_inc(step, 1)
                dve.wait_ge(step, n + 5)
                dve.reciprocal(prob[:], prob[:]).then_inc(step, 1)

            @block.scalar
            def _(act):
                act.wait_ge(step, 2 * NT + 1)
                act.activation(powers[:], shifted[:], ACT.Exp).then_inc(risen, 1)
        rank_tokens(nc, c, "rank1", member, E, rank, total)
        pos = s.sbuf("position", [P, NT], F32)
        kept = s.sbuf("kept", [P, NT], F32)
        left = s.sbuf("left", [P, NT], F32)
        start = s.sbuf("expert_start", [P, NT], F32)
        place = s.sbuf("place", [P, NT], F32)
        spare = s.sbuf("spare_place", [P, NT], F32)
        with nc.Block() as block:
            step, began = s.sem("place_step"), s.sem("place_began")

            @block.gpsimd
            def _(pool):
                pool.iota(spare[:], pattern=[[P, NT]], base=PLACES, channel_multiplier=1,
                          allow_small_or_imprecise_dtypes=True).then_inc(began, 1)

            @block.vector
            def _(dve):
                dve.wait_ge(began, 1)
                dve.tensor_tensor(one[:], one[:], rank[:], ALU.mult).then_inc(step, 1)
                dve.tensor_scalar(start[:], chosen[:], float(P), None, ALU.mult).then_inc(step, 1)
                dve.wait_ge(step, 2)
                dve.tensor_reduce(pos[:], one[:], AX.X, ALU.add).then_inc(step, 1)
                dve.wait_ge(step, 3)
                dve.scalar_tensor_tensor(kept[:], pos[:], float(CAP), c["real"][:], ALU.is_lt, ALU.mult).then_inc(step, 1)
                dve.scalar_tensor_tensor(place[:], pos[:], float(CAP - 1), start[:], ALU.min, ALU.add).then_inc(step, 1)
                dve.wait_ge(step, 5)
                dve.tensor_copy(places[:], place[:]).then_inc(step, 1)
                dve.tensor_scalar(left[:], kept[:], -1.0, 1.0, ALU.mult, ALU.add).then_inc(step, 1)
                dve.tensor_tensor(keep_weight[:], kept[:], prob[:], ALU.mult).then_inc(step, 1)
                dve.wait_ge(step, 8)
                dve.tensor_tensor(pass_weight[:], left[:], prob[:], ALU.mult).then_inc(step, 1)
                dve.tensor_tensor(spare[:], spare[:], left[:], ALU.mult).then_inc(step, 1)
                dve.tensor_tensor(place[:], place[:], kept[:], ALU.mult).then_inc(step, 1)
                dve.wait_ge(step, 11)
                dve.tensor_tensor(list_place[:], place[:], spare[:], ALU.add).then_inc(step, 1)


def switch_experts(nc, c, rows, ex_w, ex_b, ids, list_place, list_t, y_rows):
    with Stage(nc, "experts") as s:
        w = [s.sbuf(f"w_{u}", [P, KD, D], F32) for u in range(2)]
        token = [s.sbuf(f"token_{u}", [P, D], F32) for u in range(2)]
        index = [s.sbuf(f"index_{u}", [P, 1], I32) for u in range(2)]
        wh = [s.sbuf(f"w_high_{u}", [P, KD, D], F32R) for u in range(2)]
        wl = [s.sbuf(f"w_low_{u}", [P, KD, D], F32R) for u in range(2)]
        xh = [s.sbuf(f"x_high_{u}", [P, KD, P], F32R) for u in range(2)]
        xl = [s.sbuf(f"x_low_{u}", [P, KD, P], F32R) for u in range(2)]
        y = [s.sbuf(f"y_{u}", [P, D], F32) for u in range(2)]
        bias = s.sbuf("bias", [P, E2, D], F32)
        ps_t = [s.psum(f"ps_t_{i}", [P, 512]) for i in range(5)]
        ps_y = [s.psum(f"ps_y_{u}", [P, D]) for u in range(2)]
        biases, index_set = s.sem("biases"), s.sem("index_set")
        loaded = [s.sem(f"loaded_{u}") for u in range(2)]
        gathered = [s.sem(f"gathered_{u}") for u in range(2)]
        turned = s.sem("turned")
        high = s.sem("high")
        low = s.sem("low")
        product = s.sem("product")
        biased = s.sem("biased")
        stored = [s.sem(f"stored_{u}") for u in range(2)]

        def load(sp, e, u):
            sp.dma_start(w[u][:], ex_w[bass.ds(e, 1), :, :].rearrange("e (o p) d -> p (e o) d", p=P)).then_inc(loaded[u], 16)

        def first_loads(sp):
            load(sp, 0, 0)
            load(sp, 1, 1)
            sp.dma_start(bias[:], ex_b.rearrange("e d -> (e d)").partition_broadcast(P)).then_inc(biases, 16)

        store_list(nc, "list1", ids, c["node"], list_place, NT, first_loads)
        load_list(nc, c, "loadlist1", ids, list_t)
        with nc.Block() as block:
            @block.sync
            def _(sp):
                with sp.Fori(0, E2 // 2 - 1) as i:
                    for u in range(2):
                        sp.wait_ge(turned, 5 * (2 * i + u) + 15)
                        load(sp, 2 * i + u + 2, u)

            @block.gpsimd
            def _(pool):
                with pool.Fori(0, E2 // 2) as i:
                    for u in range(2):
                        e = 2 * i + u
                        pool.wait_ge(turned, 5 * e + 1)
                        pool.tensor_copy(index[u][:], list_t[:, bass.ds(e, 1)]).then_inc(index_set, 1)
                        pool.wait_ge(index_set, e + 1)
                        pool.sem_inc(c["carrier"], 1)
                        pool.indirect_dma_start(token[u][:], None, rows, bass.IndirectOffsetOnAxis(ap=index[u][:, 0:1], axis=0)).then_inc(gathered[u], 16)

            @block.scalar
            def _(act):
                for u in range(2):
                    act.sem_inc(stored[u], 16)

                def cut(e, u):
                    act.wait_ge(product, e + 1)
                    for j in range(5):
                        act.wait_ge(turned, 5 * e + j + 11)
                        target = xh[u][:].rearrange("p k n -> p (k n)") if j == 0 else wh[u][:, j - 1, :]
                        act.copy(target, ps_t[j][:]).then_inc(high, 1)

                def store(e, u):
                    act.wait_ge(biased, e + 3)
                    act.dma_start(y_rows[bass.ds(e * P, P), :], y[u][:]).then_inc(stored[u], 16)

                cut(0, 0)
                with act.Fori(0, E2 // 2 - 1) as i:
                    cut(2 * i + 1, 1)
                    cut(2 * i + 2, 0)
                    store(2 * i, 0)
                    store(2 * i + 1, 1)
                cut(E2 - 1, 1)
                store(E2 - 2, 0)
                store(E2 - 1, 1)
                for u in range(2):
                    act.wait_ge(stored[u], 16 * (E2 // 2 + 1))

            @block.vector
            def _(dve):
                dve.sem_inc(low, 5)
                dve.sem_inc(biased, 2)
                dve.wait_ge(biases, 16)

                def cut(e, u):
                    for j in range(5):
                        dve.wait_ge(high, 5 * e + j + 1)
                        if j == 0:
                            target, upper = xl[u][:].rearrange("p k n -> p (k n)"), xh[u][:].rearrange("p k n -> p (k n)")
                        else:
                            target, upper = wl[u][:, j - 1, :], wh[u][:, j - 1, :]
                        dve.tensor_tensor(target, ps_t[j][:], upper.bitcast(F32), ALU.subtract).then_inc(low, 1)

                def finish(e, i, u):
                    dve.wait_ge(product, e + 3)
                    dve.wait_ge(stored[u], 16 * i + 16)
                    dve.tensor_tensor(y[u][:], ps_y[u][:], bias[:, bass.ds(e, 1), :].rearrange("p a d -> p (a d)"), ALU.add).then_inc(biased, 1)

                cut(0, 0)
                with dve.Fori(0, E2 // 2 - 1) as i:
                    cut(2 * i + 1, 1)
                    finish(2 * i, i, 0)
                    cut(2 * i + 2, 0)
                    finish(2 * i + 1, i, 1)
                cut(E2 - 1, 1)
                finish(E2 - 2, E2 // 2 - 1, 0)
                finish(E2 - 1, E2 // 2 - 1, 1)

            @block.tensor
            def _(pe):
                pe.sem_inc(turned, 10)
                pe.sem_inc(product, 2)

                def turn(e, i, u):
                    pe.wait_ge(gathered[u], 16 * i + 16)
                    pe.wait_ge(loaded[u], 16 * i + 16)
                    for j in range(5):
                        pe.wait_ge(low, 5 * e + j + 1)
                        for o in range(KD):
                            src = token[u][:, o * P:(o + 1) * P] if j == 0 else w[u][:, o, (j - 1) * P:j * P]
                            last = pe.transpose(ps_t[j][:, o * P:(o + 1) * P], src, c["ident"][:])
                        last.then_inc(turned, 1)

                def multiply(e, u):
                    pe.wait_ge(low, 5 * e + 10)
                    pe.wait_ge(biased, e + 1)
                    for k in range(KD):
                        pe.matmul(ps_y[u][:], xh[u][:, k, :], wh[u][:, k, :], start=(k == 0), stop=False)
                        pe.matmul(ps_y[u][:], xh[u][:, k, :], wl[u][:, k, :], start=False, stop=False)
                        last = pe.matmul(ps_y[u][:], xl[u][:, k, :], wh[u][:, k, :], start=False, stop=(k == KD - 1))
                    last.then_inc(product, 1)

                turn(0, 0, 0)
                with pe.Fori(0, E2 // 2 - 1) as i:
                    turn(2 * i + 1, i, 1)
                    multiply(2 * i, 0)
                    turn(2 * i + 2, i + 1, 0)
                    multiply(2 * i + 1, 1)
                turn(E2 - 1, E2 // 2 - 1, 1)
                multiply(E2 - 2, 0)
                multiply(E2 - 1, 1)


def switch_output(nc, c, y_rows, places, keep_weight, pass_weight, h, nodes, out):
    with Stage(nc, "output") as s:
        index = [s.sbuf(f"index_{u}", [P, 1], I32) for u in range(2)]
        y = [s.sbuf(f"y_{u}", [P, D], F32) for u in range(2)]
        index_set, step, stored = s.sem("index_set"), s.sem("step"), s.sem("stored")
        gathered = [s.sem(f"gathered_{u}") for u in range(2)]
        with nc.Block() as block:
            @block.gpsimd
            def _(pool):
                with pool.Fori(0, NT // 2) as i:
                    for u in range(2):
                        t = 2 * i + u
                        pool.wait_ge(step, 2 * t + 2)
                        pool.tensor_copy(index[u][:], places[:, bass.ds(t, 1)]).then_inc(index_set, 1)
                        pool.wait_ge(index_set, t + 1)
                        pool.sem_inc(c["carrier"], 1)
                        pool.indirect_dma_start(y[u][:], None, y_rows, bass.IndirectOffsetOnAxis(ap=index[u][:, 0:1], axis=0)).then_inc(gathered[u], 16)

            @block.vector
            def _(dve):
                dve.sem_inc(step, 4)
                with dve.Fori(0, NT // 2) as i:
                    for u in range(2):
                        t = 2 * i + u
                        at = nodes[:, bass.ds(t, 1), :].rearrange("p a d -> p (a d)")
                        dve.scalar_tensor_tensor(at, h[:, bass.ds(t, 1), :].rearrange("p a d -> p (a d)"), pass_weight[:, bass.ds(t, 1)], at,
                                                 ALU.mult, ALU.add).then_inc(step, 1)
                        dve.wait_ge(gathered[u], 16 * i + 16)
                        dve.wait_ge(step, 2 * t + 5)
                        dve.scalar_tensor_tensor(at, y[u][:], keep_weight[:, bass.ds(t, 1)], at, ALU.mult, ALU.add).then_inc(step, 1)

            @block.sync
            def _(sp):
                with sp.Fori(0, NT - 1) as t:
                    sp.wait_ge(step, 2 * t + 6)
                    sp.dma_start(out[bass.ds(t * P, P), :], nodes[:, bass.ds(t, 1), :].rearrange("p a d -> p (a d)")).then_inc(stored, 16)
                sp.wait_ge(step, 2 * NT + 4)
                sp.dma_start(out[(NT - 1) * P:N, :], nodes[0:LAST, NT - 1, :]).then_inc(stored, 16)
                sp.wait_ge(stored, 16 * NT)


def add_nodes(nc, h, nodes):
    with Stage(nc, "residual") as s:
        added = s.sem("added")
        with nc.Block() as block:
            @block.vector
            def _(dve):
                dve.tensor_tensor(nodes[:], nodes[:], h[:], ALU.add).then_inc(added, 1)


def load_nodes(nc, x, nodes):
    with Stage(nc, "load") as s:
        cleared, loaded = s.sem("cleared"), s.sem("loaded")
        with nc.Block() as block:
            @block.vector
            def _(dve):
                dve.memset(nodes[:, NT - 1, :], 0.0).then_inc(cleared, 1)

            @block.sync
            def _(sp):
                sp.dma_start(nodes[:, 0:NT - 1, :], by_tile(x[0:(NT - 1) * P, :])).then_inc(loaded, 16)
                sp.wait_ge(cleared, 1)
                sp.dma_start(nodes[0:LAST, NT - 1, :], x[(NT - 1) * P:N, :]).then_inc(loaded, 16)
                sp.wait_ge(loaded, 32)


def program(nc, x, src, dst, gnn_w, ln_g, ln_b, w_r, b_r, W1, b1, W2, b2, Ws, Wn, bs, sw_w, sw_b, ex_w, ex_b, out):
    rows = nc.dram_tensor("token_rows", [NPAD, D], F32, kind="Internal").ap()
    rows2 = nc.dram_tensor("token_rows_2", [NPAD, D], F32, kind="Internal").ap()
    ids = nc.dram_tensor("unit_list", [SLOTS + T, 1], I32, kind="Internal").ap()
    ids2 = nc.dram_tensor("expert_list", [PLACES + NPAD, 1], I32, kind="Internal").ap()
    y_rows = nc.dram_tensor("unit_rows", [SLOTS, D], F32, kind="Internal").ap()
    y_rows2 = nc.dram_tensor("expert_rows", [PLACES, D], F32, kind="Internal").ap()
    with Stage(nc, "keep") as keep:
        c = make_constants(nc, keep)
        normalize = Normalizer(keep)
        counts = keep.sbuf("edge_counts", [P, NT, AW], U16)
        nodes = keep.sbuf("nodes", [P, NT, D], F32)
        inverse = keep.sbuf("inverse_degree", [P, NT], F32)
        load_nodes(nc, x, nodes)
        crowded = keep.sbuf("crowded", [1, 1], I32)
        build_adjacency(nc, c, keep, src, dst, counts, crowded, y_rows)
        with Stage(nc, "a") as s:
            h = s.sbuf("h", [P, NT, D], F32)
            normalize(nc, c, "ln0", nodes, h)
            sage_layer(nc, c, gnn_w, h, nodes, counts, crowded, inverse)
        with Stage(nc, "b") as s:
            gates = s.sbuf("gates", [P, 2, NT], F32)
            slots = s.sbuf("slots", [P, 2 * NT], I32)
            unit_expert = s.sbuf("unit_expert", [1, UNITS + 1], I32)
            unit_tokens = s.sbuf("unit_tokens", [1, UNITS + 1], I32)
            n_units = s.sbuf("n_units", [1, 1], I32)
            list_t = s.sbuf("list", [P, (SLOTS + T) // P], I32)
            with Stage(nc, "b2") as q:
                h = q.sbuf("h", [P, NT, D], F32)
                hn = q.sbuf("h_norm", [P, NT, D], F32)
                normalize(nc, c, "ln1", nodes, h)
                normalize(nc, c, "ln2", h, hn)
                route_top2(nc, c, hn, w_r, b_r, rows, (ln_g, ln_b, h, nodes), gates, slots, unit_expert, unit_tokens, n_units)
            top2_experts(nc, c, rows, W1, b1, W2, b2, unit_expert, unit_tokens, n_units, ids, slots, list_t, y_rows)
            gather_top2(nc, c, y_rows, slots, gates, nodes)
        with Stage(nc, "c") as s:
            h = s.sbuf("h", [P, NT, D], F32)
            normalize(nc, c, "ln3", nodes, h)
            graph_layers(nc, c, Ws, Wn, bs, h, counts, crowded, inverse)
            add_nodes(nc, h, nodes)
        with Stage(nc, "d") as s:
            h = s.sbuf("h", [P, NT, D], F32)
            keep_weight = s.sbuf("keep_weight", [P, NT], F32)
            pass_weight = s.sbuf("pass_weight", [P, NT], F32)
            places = s.sbuf("places", [P, NT], I32)
            list_t = s.sbuf("list", [P, (PLACES + NPAD) // P], I32)
            normalize(nc, c, "ln4", nodes, h)
            list_place = s.sbuf("list_place", [P, NT], I32)
            route_switch(nc, c, h, sw_w, sw_b, rows2, keep_weight, pass_weight, places, list_place)
            switch_experts(nc, c, rows2, ex_w, ex_b, ids2, list_place, list_t, y_rows2)
            switch_output(nc, c, y_rows2, places, keep_weight, pass_weight, h, nodes, out)


_INS = ["x", "src", "dst", "L0_gnn_w", "L0_ffn_ln_g", "L0_ffn_ln_b", "L0_ffn_w_r", "L0_ffn_b_r", "L0_ffn_W1",
        "L0_ffn_b1", "L0_ffn_W2", "L0_ffn_b2", "L1_gnn_Ws_self", "L1_gnn_Ws_neigh", "L1_gnn_bs",
        "L1_ffn_switch_w", "L1_ffn_switch_b", "L1_ffn_expert_w", "L1_ffn_expert_b"]


def kernel(**inputs):
    import numpy as _np
    import concourse.bacc as _bacc
    from concourse import mybir as _mybir
    from concourse.bass_utils import run_bass_kernel_spmd as _run

    nc = _bacc.Bacc("TRN2", target_bir_lowering=False, num_devices=1)
    arrays, args = {}, []
    for name in _INS:
        a = _np.ascontiguousarray(inputs[name])
        arrays[f"in_{name}"] = a
        args.append(nc.dram_tensor(f"in_{name}", a.shape, _mybir.dt.from_np(a.dtype), kind="ExternalInput").ap())
    result = nc.dram_tensor("result", (N, D), F32, kind="ExternalOutput").ap()
    program(nc, *args, result)
    r = _run(nc, [arrays], core_ids=[0])
    return r.results[0]["result"]
```

```python
from contextlib import ExitStack

import numpy as np
import concourse.bass as bass
import concourse.mybir as mybir

ALU = mybir.AluOpType
ACT = mybir.ActivationFunctionType
AX = mybir.AxisListType
F32 = mybir.dt.float32
F32R = mybir.dt.float32r
BF16 = mybir.dt.bfloat16
I32 = mybir.dt.int32
U32 = mybir.dt.uint32
I16 = mybir.dt.int16
U16 = mybir.dt.uint16

P = 128
N = 1250
D = 512
E_ALL = 41250
NT = -(-N // P)
NPAD = NT * P
LAST = N - (NT - 1) * P
KD = D // P
EPS = 1e-5

CH = 4
GE = CH * P
NG = -(-E_ALL // GE)
TAIL = E_ALL - (NG - 1) * GE
WIN = 32
AW = NPAD + WIN
PASSES = -(-N // WIN)

E1 = 8
F1 = 2048
FB = 512
NFB = F1 // FB
T = 512
TB = T // P
UNITS = E1 + 2 * N // T
SLOTS = UNITS * T
FEWEST = -(-2 * N // T)

E2 = 16
CAP = int(1.2 * N / E2)
PLACES = E2 * P


class Stage:

    def __init__(self, nc, tag):
        self.nc, self.tag, self.ctx = nc, tag, ExitStack()

    def __enter__(self):
        self.ctx.__enter__()
        return self

    def __exit__(self, *a):
        return self.ctx.__exit__(*a)

    def sbuf(self, name, shape, dt):
        return self.ctx.enter_context(self.nc.sbuf_tensor(f"{self.tag}_{name}", shape, dt))

    def psum(self, name, shape, dt=F32):
        return self.ctx.enter_context(self.nc.psum_tensor(f"{self.tag}_{name}", shape, dt))

    def sem(self, name):
        return self.ctx.enter_context(self.nc.semaphore(f"{self.tag}_{name}"))



def by_tile(ap):
    return ap.rearrange("(t p) d -> p t d", p=P)


def make_constants(nc, keep):
    c = {
        "ident": keep.sbuf("ident", [P, P], F32),
        "upper": keep.sbuf("upper", [P, P], F32),
        "ones": keep.sbuf("ones", [P, P], F32),
        "half": keep.sbuf("minus_half", [P, NT], F32),
        "real": keep.sbuf("real_node", [P, NT], F32),
        "node": keep.sbuf("node_id", [P, NT], I32),
    }
    c["carrier"] = keep.sem("wait_carrier")
    for name in ("rank_step", "rank_summed", "list_loaded", "list_step", "list_turned"):
        c[name] = keep.sem(name)
    made = keep.sem("constants_made")
    with nc.Block() as block:
        @block.gpsimd
        def _(pool):
            pool.memset(c["ident"][:], 0.0).then_inc(made, 1)
            pool.memset(c["upper"][:], 1.0).then_inc(made, 1)
            pool.memset(c["ones"][:], 1.0).then_inc(made, 1)
            pool.memset(c["half"][:], -0.5).then_inc(made, 1)
            pool.memset(c["real"][:], 1.0).then_inc(made, 1)
            pool.iota(c["node"][:], pattern=[[P, NT]], base=0, channel_multiplier=1).then_inc(made, 1)
            pool.wait_ge(made, 6)
            pool.affine_select(out=c["ident"][:], in_=c["ident"][:], compare_op=ALU.not_equal, fill=1.0,
                               base=0, pattern=[[-1, P]], channel_multiplier=1).then_inc(made, 1)
            pool.affine_select(out=c["upper"][:], in_=c["upper"][:], compare_op=ALU.is_gt, fill=0.0,
                               base=0, pattern=[[1, P]], channel_multiplier=-1).then_inc(made, 1)
            pool.affine_select(out=c["real"][:], in_=c["real"][:], compare_op=ALU.is_gt, fill=0.0,
                               base=N, pattern=[[-P, NT]], channel_multiplier=-1).then_inc(made, 1)
            pool.wait_ge(made, 9)
    return c


class Normalizer:

    ON_DVE = NT // 2

    def __init__(self, keep):
        self.summed_up, self.scaled, self.done = keep.sem("ln_measured"), keep.sem("ln_scaled"), keep.sem("ln_done")

    def begin(self, s):
        self.stats = s.sbuf("bn_stats", [P, NT, 6], F32)
        self.mean_var = s.sbuf("mean_var", [P, NT, 2], F32)
        self.rstd = s.sbuf("rstd", [P, NT], F32)
        self.shift = s.sbuf("ln_shift", [P, NT], F32)

    def tile_sums(self, dve, source, t):
        if t < NT:
            dve.bn_stats(self.stats[:, t, :], source[:, t, :]).then_inc(self.summed_up, 1)
        if t >= 1:
            dve.wait_ge(self.summed_up, 2 * t - 1)
            dve.bn_aggr(self.mean_var[:, t - 1, :], self.stats[:, t - 1, :]).then_inc(self.summed_up, 1)

    def pool_scales(self, pool, c):
        pool.wait_ge(self.summed_up, 2 * NT)
        pool.tensor_scalar(self.rstd[:], self.mean_var[:, :, 1], EPS, None, ALU.add).then_inc(self.scaled, 1)
        pool.tensor_scalar(self.shift[:], self.mean_var[:, :, 0], -1.0, None, ALU.mult).then_inc(self.scaled, 1)
        pool.wait_ge(self.scaled, 1)
        pool.tensor_tensor(self.rstd[:], self.rstd[:], c["half"][:], ALU.pow).then_inc(self.scaled, 1)
        pool.wait_ge(self.scaled, 3)
        pool.tensor_tensor(self.shift[:], self.shift[:], self.rstd[:], ALU.mult).then_inc(self.scaled, 1)

    def apply_dve(self, dve, source, target):
        dve.wait_ge(self.scaled, 3)
        for t in range(self.ON_DVE):
            dve.tensor_scalar(target[:, t, :], source[:, t, :], self.mean_var[:, t, 0:1], self.rstd[:, t:t + 1],
                              ALU.subtract, ALU.mult).then_inc(self.done, 1)

    def apply_act(self, act, source, target):
        act.wait_ge(self.scaled, 4)
        for t in range(self.ON_DVE, NT):
            act.activation(target[:, t, :], source[:, t, :], ACT.Identity, scale=self.rstd[:, t:t + 1],
                           bias=self.shift[:, t:t + 1]).then_inc(self.done, 1)


def build_adjacency(nc, c, src, dst, counts, crowded, y_rows, x, h, w, natural):
    NP = 10 * WIN
    with Stage(nc, "adjacency") as s:
        edge_src = s.sbuf("edge_src", [NG, GE], I32)
        edge_dst = s.sbuf("edge_dst", [NG, GE], I32)
        low_i = s.sbuf("src_low_i", [NG, GE], I32)
        high_i = s.sbuf("src_high_i", [NG, GE], I32)
        dst_f = s.sbuf("dst_f", [NG, GE], F32)
        low_f = s.sbuf("src_low_f", [NG, GE], F32)
        high_f = s.sbuf("src_high_f", [NG, GE], F32)
        rel = s.sbuf("dst_in_window", [NG, GE], F32)
        inside = s.sbuf("inside_window", [NG, GE], F32)
        place = s.sbuf("place", [NG, GE], F32)
        base = s.sbuf("window_base", [NG, 1], F32)
        top = s.sbuf("greatest_dst", [NG, 1], F32)
        wide = s.sbuf("wide_columns", [NG, 2, P], F32)
        place_t = s.sbuf("place_t", [P, CH, NG], F32)
        base_row = s.sbuf("base_row", [1, NG], I32)
        span = s.sbuf("greatest_span", [1, 2], F32)
        span_i = s.sbuf("greatest_span_i", [1, 1], I32)
        mean = s.sbuf("mean", [P, NT], F32)
        rstd = s.sbuf("rstd", [P, NT], F32)
        squares = s.sbuf("squares", [P, NT, D], F32)
        normed = s.sem("layernorm_step")
        first_base = s.sbuf("first_base", [NG, 1], F32)
        node_row = s.sbuf("node_row", [NG, NPAD], F32)
        reached = s.sbuf("reached", [NG, 2, NPAD], F32)
        most = s.sbuf("most_groups", [1, 4], F32)
        based, covered = s.sem("first_base_kept"), s.sem("groups_reach")
        overlaid, crowd = s.sem("groups_overlaid"), s.sem("crowd_step")
        count_low = s.sbuf("count_low", [P, P], I16)
        count_place = s.sbuf("count_place", [P, NP], I16)
        hot_low = s.sbuf("onehot_low", [P, 2, CH, P], BF16)
        hot_place = s.sbuf("onehot_place", [P, 2, CH, NP], BF16)
        ps_t = [s.psum(f"ps_edges_{i}", [P, 512]) for i in range(3)]
        ps_n = [s.psum(f"ps_window_{i}", [P, 512]) for i in range(2)]
        edges_in, filled = s.sem("edges_in"), s.sem("edges_filled")
        step, turned, taken = s.sem("edge_step"), s.sem("edges_turned"), s.sem("edges_taken")
        hot, counted, added = s.sem("onehots_ready"), s.sem("window_counted"), s.sem("window_added")
        distance = s.sbuf("low_distance", [P, 2, CH, P], BF16)
        hot_l, apart = s.sem("low_onehots_ready"), s.sem("low_distance_ready")
        minus_low = s.sbuf("minus_src_low_t", [P, CH, NG], F32)
        zeros = s.sbuf("zero_rows", [P, D], F32)
        zeroed, cleared = s.sem("zero_rows_made"), s.sem("y_rows_cleared")

        def prepare(dve, at, k_turn, k_taken):
            dve.tensor_scalar(rel[:], dst_f[:], base[:, 0:1], None, ALU.subtract).then_inc(step, 1)
            dve.wait_ge(step, at + 1)
            dve.tensor_scalar(inside[:], rel[:], 0.0, None, ALU.is_ge).then_inc(step, 1)
            dve.wait_ge(step, at + 2)
            dve.scalar_tensor_tensor(inside[:], rel[:], float(WIN), inside[:], ALU.is_lt, ALU.mult).then_inc(step, 1)
            dve.scalar_tensor_tensor(place[:], rel[:], 1.0, high_f[:], ALU.add, ALU.add).then_inc(step, 1)
            dve.wait_ge(step, at + 4)
            dve.tensor_tensor(place[:], place[:], inside[:], ALU.mult).then_inc(step, 1)
            dve.tensor_copy(wide[:, 0, 0:1], base[:, 0:1]).then_inc(step, 1)
            dve.wait_ge(turned, k_turn)
            dve.tensor_copy(place_t[:], ps_t[0][:, 0:CH * NG].rearrange("p (c g) -> p c g", c=CH)).then_inc(taken, 1)
            dve.tensor_copy(base_row[:], ps_t[1][0:1, 0:NG]).then_inc(taken, 1)
            dve.tensor_scalar(base[:], base[:], float(WIN), float(NPAD), ALU.add, ALU.min).then_inc(step, 1)
            dve.wait_ge(taken, k_taken)
            dve.wait_ge(step, at + 7)

        def turn_places(pe, at, k_turn):
            pe.wait_ge(step, at + 6)
            for ch in range(CH):
                last = pe.transpose(ps_t[0][:, ch * NG:(ch + 1) * NG], place[:, ch * P:(ch + 1) * P], c["ident"][0:NG, 0:NG])
            last.then_inc(turned, 1)
            pe.transpose(ps_t[1][:, 0:NG], wide[:, 0, :], c["ident"][0:NG, 0:NG]).then_inc(turned, 1)

        def onehots(dve, g, u):
            dve.tensor_scalar(hot_low[:, u, CH - 1, :], count_low[:], minus_low[:, CH - 1, bass.ds(g, 1)], 0.0,
                              ALU.add, ALU.is_equal)
            for ch in range(CH):
                last = dve.tensor_scalar(hot_place[:, u, ch, :], count_place[:], place_t[:, ch, bass.ds(g, 1)],
                                         None, ALU.is_equal)
            last.then_inc(hot, 1)

        def add_window(dve, g, u, done, start):
            at = counts[:, :, bass.ds(start, WIN)]
            dve.wait_ge(counted, done + 1)
            dve.wait_ge(added, done + 1)
            dve.tensor_tensor(at, ps_n[u][:, 0:NP].rearrange("p (a b) -> p a b", b=WIN), at, ALU.add).then_inc(added, 1)

        def base_of(dve, g):
            return dve.value_load(base_row[0:1, bass.ds(g, 1)], min_val=0, max_val=NPAD)

        def count_pass(dve, before):
            onehots(dve, 0, 0)
            with dve.Fori(0, (NG - 1) // 4) as i:
                for u in range(4):
                    g = 4 * i + u
                    onehots(dve, g + 1, 1 - u % 2)
                    add_window(dve, g, u % 2, before + g, base_of(dve, g))
            start = base_of(dve, NG - 1)
            add_window(dve, NG - 1, 0, before + NG - 1, start)
            dve.wait_ge(added, before + NG + 1)

        def low_onehots(act, g, u, before):
            for ch in range(CH - 1):
                last = act.activation(distance[:, u, ch, :], count_low[:], ACT.Abs, bias=minus_low[:, ch, bass.ds(g, 1)])
            last.then_inc(apart, 1)
            act.wait_ge(apart, before + g + 1)
            act.activation(hot_low[:, u, 0:CH - 1, :], distance[:, u, 0:CH - 1, :], ACT.Relu, bias=1.0, scale=-1.0).then_inc(hot_l, 1)

        def low_pass(act, before):
            low_onehots(act, 0, 0, before)
            low_onehots(act, 1, 1, before)
            with act.Fori(0, (NG - 3) // 2) as i:
                for u in range(2):
                    g = 2 * i + u + 2
                    act.wait_ge(counted, before + g - 1)
                    low_onehots(act, g, u, before)
            act.wait_ge(counted, before + NG - 2)
            low_onehots(act, NG - 1, 0, before)

        def multiply(pe, g, u, before):
            pe.wait_ge(hot, before + g + 1)
            pe.wait_ge(hot_l, before + g + 1)
            for ch in range(CH):
                last = pe.matmul(ps_n[u][:, 0:NP], hot_low[:, u, ch, :], hot_place[:, u, ch, :],
                                 start=(ch == 0), stop=(ch == CH - 1))
            last.then_inc(counted, 1)

        def multiply_pass(pe, before):
            multiply(pe, 0, 0, before)
            with pe.Fori(0, (NG - 1) // 2) as i:
                for u in range(2):
                    multiply(pe, 2 * i + u + 1, 1 - u, before)

        with nc.Block() as block:
            @block.sync
            def _(sp):
                sp.wait_ge(filled, 1)
                full = (NG - 1) * GE
                sp.dma_start(edge_src[0:NG - 1, :], src[0:full].rearrange("(g e) -> g e", e=GE)).then_inc(edges_in, 16)
                sp.dma_start(edge_src[NG - 1:NG, 0:TAIL], src[full:E_ALL].rearrange("(g e) -> g e", g=1)).then_inc(edges_in, 16)
                sp.dma_start(edge_dst[0:NG - 1, :], dst[0:full].rearrange("(g e) -> g e", e=GE)).then_inc(edges_in, 16)
                sp.dma_start(edge_dst[NG - 1:NG, 0:TAIL], dst[full:E_ALL].rearrange("(g e) -> g e", g=1)).then_inc(edges_in, 16)
                sp.dma_start(edge_dst[NG - 1:NG, TAIL:GE], dst[E_ALL - (GE - TAIL):E_ALL].rearrange("(g e) -> g e", g=1)).then_inc(edges_in, 16)
                sp.wait_ge(zeroed, 1)
                for b in range(FEWEST * TB, UNITS * TB):
                    sp.dma_start(y_rows[b * P:(b + 1) * P, :], zeros[:]).then_inc(cleared, 16)
                sp.dma_start(natural[:], w.rearrange("(o p) f -> p o f", p=P)).then_inc(cleared, 16)
                sp.wait_ge(cleared, 16 * (UNITS - FEWEST) * TB + 16)

            @block.scalar
            def _(act):
                act.wait_ge(taken, 1)
                low_pass(act, 0)
                act.wait_ge(taken, 3)
                reach = act.value_load(span_i[0:1, 0:1], min_val=0, max_val=NPAD)
                with act.If(reach > WIN - 1):
                    with act.Fori(1, PASSES) as k:
                        act.wait_ge(added, NG * k + 1)
                        low_pass(act, NG * k)

            @block.gpsimd
            def _(pool):
                pool.memset(zeros[:], 0.0).then_inc(zeroed, 1)
                pool.memset(edge_src[:], -100 * P).then_inc(filled, 1)
                pool.memset(wide[:], 0.0).then_inc(filled, 1)
                pool.iota(count_low[:], pattern=[[1, P]], base=0, channel_multiplier=0,
                          allow_small_or_imprecise_dtypes=True).then_inc(filled, 1)
                pool.iota(count_place[:], pattern=[[1, NP]], base=1, channel_multiplier=0,
                          allow_small_or_imprecise_dtypes=True).then_inc(filled, 1)
                pool.iota(node_row[:], pattern=[[1, NPAD]], base=0, channel_multiplier=0,
                          allow_small_or_imprecise_dtypes=True).then_inc(filled, 1)
                pool.wait_ge(filled, 5)
                pool.wait_ge(based, 1)
                pool.tensor_scalar(reached[:, 0, :], node_row[:], first_base[:, 0:1], None, ALU.is_ge).then_inc(covered, 1)
                pool.tensor_scalar(reached[:, 1, :], node_row[:], top[:, 0:1], None, ALU.is_le).then_inc(covered, 1)
                pool.wait_ge(covered, 2)
                pool.tensor_tensor(reached[:, 0, :], reached[:, 0, :], reached[:, 1, :], ALU.mult).then_inc(covered, 1)
                whole = [P, NT, D]

                def fold(source, at):
                    half = D // 2
                    pool.tensor_tensor(squares[:, :, 0:half], source[:, :, 0:half], source[:, :, half:D], ALU.add).then_inc(normed, 1)
                    while half > 1:
                        at += 1
                        half //= 2
                        pool.wait_ge(normed, at)
                        pool.tensor_tensor(squares[:, :, 0:half], squares[:, :, 0:half], squares[:, :, half:2 * half],
                                           ALU.add).then_inc(normed, 1)

                folds = D.bit_length() - 1
                fold(x, 0)
                pool.wait_ge(normed, folds)
                pool.tensor_scalar(mean[:], squares[:, :, 0], 1.0 / D, None, ALU.mult).then_inc(normed, 1)
                pool.wait_ge(normed, folds + 1)
                pool.tensor_tensor(h[:], x[:], mean[:].unsqueeze(2).to_broadcast(whole), ALU.subtract).then_inc(normed, 1)
                pool.wait_ge(normed, folds + 2)
                pool.tensor_tensor(squares[:], h[:], h[:], ALU.mult).then_inc(normed, 1)
                pool.wait_ge(normed, folds + 3)
                fold(squares, folds + 3)
                pool.wait_ge(normed, 2 * folds + 3)
                pool.tensor_scalar(rstd[:], squares[:, :, 0], 1.0 / D, EPS, ALU.mult, ALU.add).then_inc(normed, 1)
                pool.wait_ge(normed, 2 * folds + 4)
                pool.tensor_tensor(rstd[:], rstd[:], c["half"][:], ALU.pow).then_inc(normed, 1)
                pool.wait_ge(normed, 2 * folds + 5)
                pool.tensor_tensor(h[:], h[:], rstd[:].unsqueeze(2).to_broadcast(whole), ALU.mult).then_inc(normed, 1)

            @block.vector
            def _(dve):
                dve.memset(counts[:], 0.0).then_inc(added, 1)
                dve.wait_ge(filled, 4)
                dve.wait_ge(edges_in, 80)
                dve.tensor_scalar(low_i[:], edge_src[:], P - 1, None, ALU.bitwise_and).then_inc(step, 1)
                dve.tensor_scalar(high_i[:], edge_src[:], 7, None, ALU.arith_shift_right).then_inc(step, 1)
                dve.tensor_copy(dst_f[:], edge_dst[:]).then_inc(step, 1)
                dve.wait_ge(step, 3)
                dve.tensor_copy(low_f[:], low_i[:]).then_inc(step, 1)
                dve.tensor_scalar(high_f[:], high_i[:], float(WIN), None, ALU.mult).then_inc(step, 1)
                dve.tensor_reduce(base[:], dst_f[:], AX.X, ALU.min).then_inc(step, 1)
                dve.tensor_reduce(top[:], dst_f[:], AX.X, ALU.max).then_inc(step, 1)
                dve.wait_ge(step, 7)
                dve.tensor_copy(first_base[:], base[:]).then_inc(based, 1)
                dve.tensor_tensor(wide[:, 1, 0:1], top[:], base[:], ALU.subtract).then_inc(step, 1)
                dve.wait_ge(turned, 2)
                dve.tensor_scalar(minus_low[:], ps_t[2][:, 0:CH * NG].rearrange("p (c g) -> p c g", c=CH), -1.0, None,
                                  ALU.mult).then_inc(taken, 1)
                dve.tensor_reduce(span[0:1, 0:1], ps_t[1][0:1, 0:NG], AX.X, ALU.max).then_inc(step, 1)
                dve.wait_ge(step, 9)
                dve.tensor_copy(span_i[:], span[0:1, 0:1]).then_inc(step, 1)
                dve.wait_ge(step, 10)
                dve.wait_ge(taken, 1)
                prepare(dve, 10, 4, 3)
                count_pass(dve, 0)
                dve.wait_ge(overlaid, 1)
                for i in range(3):
                    dve.tensor_reduce(most[0:1, i:i + 1], ps_t[i][0:1, 0:min(512, NPAD - 512 * i)], AX.X, ALU.max).then_inc(crowd, 1)
                dve.wait_ge(crowd, 3)
                dve.tensor_reduce(most[0:1, 3:4], most[0:1, 0:3], AX.X, ALU.max).then_inc(crowd, 1)
                dve.wait_ge(crowd, 4)
                dve.tensor_copy(crowded[:], most[0:1, 3:4]).then_inc(crowd, 1)
                reach = dve.value_load(span_i[0:1, 0:1], min_val=0, max_val=NPAD)
                with dve.If(reach > WIN - 1):
                    with dve.Fori(1, PASSES) as k:
                        prepare(dve, 10 + 7 * k, 4 + 2 * k, 3 + 2 * k)
                        count_pass(dve, NG * k)

            @block.tensor
            def _(pe):
                pe.wait_ge(step, 8)
                for ch in range(CH):
                    last = pe.transpose(ps_t[2][:, ch * NG:(ch + 1) * NG], low_f[:, ch * P:(ch + 1) * P], c["ident"][0:NG, 0:NG])
                last.then_inc(turned, 1)
                pe.transpose(ps_t[1][:, 0:NG], wide[:, 1, :], c["ident"][0:NG, 0:NG]).then_inc(turned, 1)
                pe.wait_ge(step, 10)
                turn_places(pe, 10, 4)
                multiply_pass(pe, 0)
                pe.wait_ge(covered, 3)
                for i in range(3):
                    width = min(512, NPAD - 512 * i)
                    last = pe.matmul(ps_t[i][0:1, 0:width], c["ones"][0:NG, 0:1], reached[:, 0, 512 * i:512 * i + width],
                                     start=True, stop=True)
                last.then_inc(overlaid, 1)
                reach = pe.value_load(span_i[0:1, 0:1], min_val=0, max_val=NPAD)
                with pe.If(reach > WIN - 1):
                    with pe.Fori(1, PASSES) as k:
                        pe.wait_ge(added, NG * k + 1)
                        pe.wait_ge(crowd, 3)
                        turn_places(pe, 10 + 7 * k, 4 + 2 * k)
                        multiply_pass(pe, NG * k)



class Sage:

    def __init__(self, s, c, crowded, degrees=False):
        self.carrier = c["carrier"]
        self.degrees, self.crowded = degrees, crowded
        self.count_whole = s.sbuf("count_whole", [P, NT, P], F32)
        self.count_rest = s.sbuf("count_rest", [P, NT, P], F32R)
        self.rest_staged = s.sem("count_rest_staged")
        if degrees:
            self.partial = s.sbuf("degree_partial", [P, P], F32)
            self.degree = s.sbuf("degree", [P, 1], F32)
            self.ps_degree = s.psum("ps_degree", [P, 512])
            self.partial_ready = s.sem("degree_partial_ready")
            self.degree_ready = s.sem("degree_ready")
        self.high = s.sbuf("h_high", [P, NT, D], F32R)
        self.low = s.sbuf("h_low", [P, NT, D], F32R)
        self.w_high = s.sbuf("w_high", [P, 2 * KD, D], F32R)
        self.w_low = s.sbuf("w_low", [P, 2 * KD, D], F32R)
        self.count_tile = [s.sbuf(f"count_tile_{u}", [P, NT, P], F32R) for u in range(2)]
        self.h_tile = [s.sbuf(f"h_tile_{u}", [P, D], F32) for u in range(2)]
        self.mean_tile = [s.sbuf(f"mean_tile_{u}", [P, D], F32) for u in range(2)]
        self.ht_high = [s.sbuf(f"ht_high_{u}", [P, KD, P], F32R) for u in range(2)]
        self.ht_low = [s.sbuf(f"ht_low_{u}", [P, KD, P], F32R) for u in range(2)]
        self.mt_high = [s.sbuf(f"mt_high_{u}", [P, KD, P], F32R) for u in range(2)]
        self.mt_low = [s.sbuf(f"mt_low_{u}", [P, KD, P], F32R) for u in range(2)]
        self.ps_h = s.psum("ps_h", [P, KD, P])
        self.ps_m = s.psum("ps_m", [P, KD, P])
        self.ps_sum = [s.psum(f"ps_sum_{u}", [P, D]) for u in range(2)]
        self.ps_y = [s.psum(f"ps_y_{u}", [P, D]) for u in range(2)]
        self.staged = s.sem("tile_staged")
        self.turned_h = s.sem("h_turned")
        self.summed = s.sem("neighbours_summed")
        self.turned_m = s.sem("mean_turned")
        self.multiplied = s.sem("y_multiplied")
        self.high_h = s.sem("ht_high_ready")
        self.mean = s.sem("mean_ready")
        self.high_m = s.sem("mt_high_ready")
        self.low_h = s.sem("ht_low_ready")
        self.low_m = s.sem("mt_low_ready")
        self.finished = s.sem("y_finished")
        self.cut_high = s.sem("h_high_cut")
        self.cut_low = s.sem("h_low_cut")

    def has_rests(self, eng):
        return eng.value_load(self.crowded[0:1, 0:1], min_val=0, max_val=NG) > (1 << 12) // GE - 1

    def act_cut(self, act, h, first, end):
        for j in range(first, end):
            act.copy(self.high[:, j, :], h[:, j, :]).then_inc(self.cut_high, 1)

    def dve_cut(self, dve, h, before, first, end):
        for j in range(first, end):
            dve.wait_ge(self.cut_high, before + j + 1)
            dve.tensor_tensor(self.low[:, j, :], h[:, j, :], self.high[:, j, :].bitcast(F32), ALU.subtract).then_inc(self.cut_low, 1)

    def pool_tiles(self, pool, counts, h, before, rests):
        with pool.Fori(0, NT // 2) as i:
            for u in range(2):
                n = before + 2 * i + u
                pool.wait_ge(self.summed, n + 1)
                pool.tensor_copy(self.count_tile[u][:], counts[:, :, bass.ds((2 * i + u) * P, P)]).then_inc(self.staged, 1)
                with pool.If(rests):
                    pool.wait_ge(self.staged, 2 * n + 1)
                    pool.wait_ge(self.summed, n + 2)
                    pool.sem_inc(self.carrier, 1)
                    pool.tensor_copy(self.count_whole[:], counts[:, :, bass.ds((2 * i + u) * P, P)]).then_inc(self.rest_staged, 1)
                    pool.wait_ge(self.rest_staged, 2 * n + 1)
                    pool.tensor_tensor(self.count_rest[:], self.count_whole[:],
                                       self.count_tile[u][:].bitcast(F32), ALU.subtract).then_inc(self.rest_staged, 1)
                pool.wait_ge(self.turned_h, n + 1)
                pool.wait_ge(self.finished, before + 2)
                pool.tensor_copy(self.h_tile[u][:], h[:, bass.ds(2 * i + u, 1), :].rearrange("p a d -> p (a d)")).then_inc(self.staged, 1)

    def pe_credits(self, pe):
        pe.sem_inc(self.turned_h, 2)
        pe.sem_inc(self.summed, 2)
        pe.sem_inc(self.turned_m, 2)
        pe.sem_inc(self.multiplied, 2)

    def act_credits(self, act):
        act.sem_inc(self.mean, 2)

    def dve_credits(self, dve):
        dve.sem_inc(self.low_h, 1)
        dve.sem_inc(self.low_m, 1)
        dve.sem_inc(self.finished, 2)

    def pe_gather(self, pe, c, n, u, rests, first=False):
        pe.wait_ge(self.staged, 2 * n + 2)
        pe.wait_ge(self.low_h, n + 1)
        for k in range(KD):
            last = pe.transpose(self.ps_h[:, k, :], self.h_tile[u][:, k * P:(k + 1) * P], c["ident"][:])
        last.then_inc(self.turned_h, 1)
        pe.wait_ge(self.mean, n + 1)
        for j in range(NT):
            if first:
                pe.wait_ge(self.cut_low, n + j + 1)
            if j == NT - 1:
                with pe.If(rests):
                    pe.wait_ge(self.rest_staged, 2 * n + 2)
                    for i in range(NT):
                        pe.matmul(self.ps_sum[u][:], self.count_rest[:, i, :], self.high[:, i, :], start=False, stop=False)
            for part, h in enumerate((self.high, self.low)):
                last = pe.matmul(self.ps_sum[u][:], self.count_tile[u][:, j, :], h[:, j, :],
                                 start=(j == 0 and part == 0), stop=(j == NT - 1 and part == 1))
        if self.degrees:
            pe.wait_ge(self.partial_ready, n + 1)
            last = pe.matmul(self.ps_degree[:, 0:1], self.partial[:], c["ones"][:, 0:1], start=True, stop=True)
        last.then_inc(self.summed, 1)

    def products(self, pe, u, high, low, first, start, stop):
        for k in range(KD):
            w = first + k
            pe.matmul(self.ps_y[u][:], high[:, k, :], self.w_high[:, w, :], start=(start and k == 0), stop=False)
            pe.matmul(self.ps_y[u][:], high[:, k, :], self.w_low[:, w, :], start=False, stop=False)
            last = pe.matmul(self.ps_y[u][:], low[:, k, :], self.w_high[:, w, :], start=False,
                             stop=(stop and k == KD - 1))
        return last

    def pe_tile(self, pe, c, n, u, rests, more):
        pe.wait_ge(self.low_h, n + 2)
        pe.wait_ge(self.finished, n + 1)
        self.products(pe, u, self.ht_high[u], self.ht_low[u], 0, True, False)
        pe.wait_ge(self.mean, n + 3)
        pe.wait_ge(self.low_m, n + 1)
        for k in range(KD):
            last = pe.transpose(self.ps_m[:, k, :], self.mean_tile[u][:, k * P:(k + 1) * P], c["ident"][:])
        last.then_inc(self.turned_m, 1)
        if more:
            self.pe_gather(pe, c, n + 1, 1 - u, rests)
        pe.wait_ge(self.low_m, n + 2)
        self.products(pe, u, self.mt_high[u], self.mt_low[u], KD, False, True).then_inc(self.multiplied, 1)

    def pe_tiles(self, pe, c, before, rests, w_cut, parts):
        self.pe_gather(pe, c, before, 0, rests, first=True)
        pe.wait_ge(w_cut, parts)
        pe.sem_inc(self.carrier, 1)
        with pe.Fori(0, NT // 2 - 1) as i:
            for u in range(2):
                self.pe_tile(pe, c, before + 2 * i + u, u, rests, True)
        self.pe_tile(pe, c, before + NT - 2, 0, rests, True)
        self.pe_tile(pe, c, before + NT - 1, 1, rests, False)

    def act_cut_h(self, act, n, u):
        act.wait_ge(self.turned_h, n + 3)
        act.wait_ge(self.multiplied, n + 1)
        act.copy(self.ht_high[u][:], self.ps_h[:]).then_inc(self.high_h, 1)

    def act_mean(self, act, inverse, t, n, u):
        if self.degrees:
            act.wait_ge(self.degree_ready, 2 * n + 2)
        act.wait_ge(self.summed, n + 3)
        act.wait_ge(self.turned_m, n + 1)
        act.activation(self.mean_tile[u][:], self.ps_sum[u][:], ACT.Copy, scale=inverse[:, bass.ds(t, 1)]).then_inc(self.mean, 1)

    def act_cut_mean(self, act, n, u):
        act.wait_ge(self.turned_m, n + 3)
        act.copy(self.mt_high[u][:], self.ps_m[:]).then_inc(self.high_m, 1)

    def act_tiles(self, act, inverse, before, h=None):
        with act.Fori(0, NT // 2 - 1) as i:
            for u in range(2):
                n = before + 2 * i + u
                self.act_cut_h(act, n, u)
                self.act_mean(act, inverse, 2 * i + u, n, u)
                self.act_cut_mean(act, n, u)
        for t in (NT - 2, NT - 1):
            n = before + t
            self.act_cut_h(act, n, t % 2)
            self.act_mean(act, inverse, t, n, t % 2)
            if h is not None and t == NT - 1:
                act.wait_ge(self.finished, n + 1)
                self.act_cut(act, h, 0, NT - 2)
            self.act_cut_mean(act, n, t % 2)
        if h is not None:
            act.wait_ge(self.finished, before + NT + 1)
            self.act_cut(act, h, NT - 2, NT - 1)
            act.wait_ge(self.finished, before + NT + 2)
            self.act_cut(act, h, NT - 1, NT)

    def dve_partial(self, dve, counts, t):
        dve.tensor_reduce(self.partial[:], counts[:, :, bass.ds(t * P, P)].rearrange("p s d -> p d s"), AX.X,
                          ALU.add).then_inc(self.partial_ready, 1)

    def dve_degree(self, dve, inverse, t):
        dve.wait_ge(self.summed, t + 3)
        dve.tensor_scalar(self.degree[:], self.ps_degree[:, 0:1], 1.0, None, ALU.max).then_inc(self.degree_ready, 1)
        dve.wait_ge(self.degree_ready, 2 * t + 1)
        dve.reciprocal(inverse[:, bass.ds(t, 1)], self.degree[:]).then_inc(self.degree_ready, 1)

    def dve_cut_h(self, dve, n, u):
        dve.wait_ge(self.high_h, n + 1)
        dve.tensor_tensor(self.ht_low[u][:], self.ps_h[:], self.ht_high[u][:].bitcast(F32), ALU.subtract).then_inc(self.low_h, 1)

    def dve_tile(self, dve, t, n, u, finish, counts, inverse, more, h=None, after=None):
        early = (NT - 2) // 2
        if h is not None:
            self.dve_cut(dve, h, after, 0, early)
        dve.wait_ge(self.high_m, n + 1)
        dve.tensor_tensor(self.mt_low[u][:], self.ps_m[:], self.mt_high[u][:].bitcast(F32), ALU.subtract).then_inc(self.low_m, 1)
        if more:
            if self.degrees:
                self.dve_partial(dve, counts, t + 1)
            self.dve_cut_h(dve, n + 1, 1 - u)
            if self.degrees:
                self.dve_degree(dve, inverse, t + 1)
        if h is not None:
            self.dve_cut(dve, h, after, early, NT - 2)
        dve.wait_ge(self.multiplied, n + 3)
        finish(dve, t, n, u).then_inc(self.finished, 1)
        if h is not None:
            self.dve_cut(dve, h, after, NT - 2, NT)

    def dve_tiles(self, dve, before, finish, counts=None, inverse=None, h=None):
        if self.degrees:
            self.dve_partial(dve, counts, 0)
        self.dve_cut_h(dve, before, 0)
        if self.degrees:
            self.dve_degree(dve, inverse, 0)
        with dve.Fori(0, NT // 2 - 1) as i:
            for u in range(2):
                self.dve_tile(dve, 2 * i + u, before + 2 * i + u, u, finish, counts, inverse, True)
        self.dve_tile(dve, NT - 2, before + NT - 2, 0, finish, counts, inverse, True)
        self.dve_tile(dve, NT - 1, before + NT - 1, 1, finish, counts, inverse, False, h, before + NT)


def sage_layer(nc, c, natural, h, x, counts, crowded, inverse):
    with Stage(nc, "sage") as s:
        g = Sage(s, c, crowded, degrees=True)
        turned, w_high, w_low = s.sem("w_turned"), s.sem("w_high_cut"), s.sem("w_low_cut")
        with nc.Block() as block:
            @block.gpsimd
            def _(pool):
                g.pool_tiles(pool, counts, h, 0, g.has_rests(pool))

            @block.scalar
            def _(act):
                g.act_credits(act)
                for k in range(2 * KD):
                    act.wait_ge(turned, k + 1)
                    act.copy(g.w_high[:, k, :], g.ps_y[k % 2][:]).then_inc(w_high, 1)
                g.act_cut(act, h, 0, NT)
                g.act_tiles(act, inverse, 0)

            @block.vector
            def _(dve):
                g.dve_credits(dve)
                for k in range(2 * KD):
                    dve.wait_ge(w_high, k + 1)
                    dve.tensor_tensor(g.w_low[:, k, :], g.ps_y[k % 2][:], g.w_high[:, k, :].bitcast(F32),
                                      ALU.subtract).then_inc(w_low, 1)
                g.dve_cut(dve, h, 0, 0, NT)

                def finish(dve, t, n, u):
                    at = x[:, bass.ds(t, 1), :].rearrange("p a d -> p (a d)")
                    return dve.scalar_tensor_tensor(at, g.ps_y[u][:], 0.0, at, ALU.max, ALU.add)

                g.dve_tiles(dve, 0, finish, counts, inverse)

            @block.tensor
            def _(pe):
                g.pe_credits(pe)
                rests = g.has_rests(pe)
                for k in range(2 * KD):
                    if k >= 2:
                        pe.wait_ge(w_low, k - 1)
                    for o in range(KD):
                        last = pe.transpose(g.ps_y[k % 2][:, o * P:(o + 1) * P], natural[:, o, k * P:(k + 1) * P], c["ident"][:])
                    last.then_inc(turned, 1)
                g.pe_tiles(pe, c, 0, rests, w_low, 2 * KD)


def graph_layers(nc, c, ws, wn, bs, h, counts, crowded, inverse):
    L = ws.shape[0]
    with Stage(nc, "layers") as s:
        g = Sage(s, c, crowded)
        w = s.sbuf("w_whole", [P, 2 * KD, D], F32)
        bias = s.sbuf("layer_bias", [P, L, D], F32)
        floor = s.sbuf("relu_floor", [P, L], F32)
        y = s.sbuf("y_with_bias", [P, D], F32)
        loaded, biased, extra = s.sem("w_loaded"), s.sem("y_biased"), s.sem("layer_extra")
        w_high = s.sem("w_high_cut")
        w_low = s.sem("w_low_cut")
        with nc.Block() as block:
            @block.sync
            def _(sp):
                sp.dma_start(bias[:], bs.rearrange("l d -> (l d)").partition_broadcast(P)).then_inc(extra, 16)
                with sp.Fori(0, L) as l:
                    sp.wait_ge(w_low, 2 * KD * (l + 1))
                    sp.dma_start(w[:, 0:KD, :], ws[bass.ds(l, 1), :, :].rearrange("l (k p) d -> p (l k) d", p=P)).then_inc(loaded, 16)
                    sp.dma_start(w[:, KD:2 * KD, :], wn[bass.ds(l, 1), :, :].rearrange("l (k p) d -> p (l k) d", p=P)).then_inc(loaded, 16)

            @block.gpsimd
            def _(pool):
                pool.memset(floor[:, 0:L - 1], 0.0).then_inc(extra, 1)
                pool.memset(floor[:, L - 1:L], -3.4e38).then_inc(extra, 1)
                rests = g.has_rests(pool)
                with pool.Fori(0, L) as l:
                    g.pool_tiles(pool, counts, h, l * NT, rests)

            @block.scalar
            def _(act):
                g.act_credits(act)
                g.act_cut(act, h, 0, NT)
                with act.Fori(0, L) as l:
                    act.wait_ge(g.finished, l * NT + 2)
                    act.wait_ge(loaded, 32 * l + 32)
                    for k in range(2 * KD):
                        act.copy(g.w_high[:, k, :], w[:, k, :]).then_inc(w_high, 1)
                    g.act_tiles(act, inverse, l * NT, h)

            @block.vector
            def _(dve):
                g.dve_credits(dve)
                dve.sem_inc(w_low, 2 * KD)
                dve.wait_ge(extra, 18)
                g.dve_cut(dve, h, 0, 0, NT)
                with dve.Fori(0, L) as l:
                    for k in range(2 * KD):
                        dve.wait_ge(w_high, 2 * KD * l + k + 1)
                        dve.tensor_tensor(g.w_low[:, k, :], w[:, k, :], g.w_high[:, k, :].bitcast(F32), ALU.subtract).then_inc(w_low, 1)

                    def finish(dve, t, n, u):
                        dve.wait_ge(g.finished, n + 2)
                        dve.tensor_tensor(y[:], g.ps_y[u][:], bias[:, bass.ds(l, 1), :].rearrange("p a d -> p (a d)"),
                                          ALU.add).then_inc(biased, 1)
                        dve.wait_ge(biased, n + 1)
                        return dve.tensor_scalar(h[:, bass.ds(t, 1), :].rearrange("p a d -> p (a d)"), y[:],
                                                 floor[:, bass.ds(l, 1)], None, ALU.max)

                    g.dve_tiles(dve, l * NT, finish, h=h)

            @block.tensor
            def _(pe):
                g.pe_credits(pe)
                rests = g.has_rests(pe)
                with pe.Fori(0, L) as l:
                    g.pe_tiles(pe, c, l * NT, rests, w_low, 2 * KD * (l + 2))


def router_logits(nc, c, tag, x, h, w, b, E, logits, rows, add=None, affine=None):
    PAIRS, NORMS = NT // 2, 2 if affine else 1
    with Stage(nc, tag) as s:
        w_rows = s.sbuf("w_rows", [E, D], F32)
        w_t = s.sbuf("w_t", [P, KD, E], F32)
        bias = s.sbuf("bias", [P, E], F32)
        stats = s.sbuf("bn_stats", [P, 2, 6], F32)
        mean_var = s.sbuf("mean_var", [P, NORMS, NT, 2], F32)
        rstd = s.sbuf("rstd", [P, NORMS, NT], F32)
        offset = s.sbuf("ln_offset", [P, NORMS, NT], F32)
        tile_t = [s.sbuf(f"tile_t_{u}", [P, KD, P], F32) for u in range(2)]
        gain = s.sbuf("gain", [P, D], F32)
        shift = s.sbuf("shift", [P, D], F32)
        ps_w = s.psum("ps_w", [P, 512])
        ps_t = [s.psum(f"ps_t_{u}", [P, KD, P]) for u in range(2)]
        ps_l = s.psum("ps_l", [P, NT, E])
        loaded, w_turned, w_ready = s.sem("loaded"), s.sem("w_turned"), s.sem("w_ready")
        measured = s.sem("measured")
        scaled = s.sem("scaled")
        normed = s.sem("normed")
        turned, product = s.sem("turned"), s.sem("product")
        taken = s.sem("taken")
        stored = s.sem("stored")
        if affine:
            gained, shifted = s.sem("gained"), s.sem("shifted")
            summed = s.sem("summed")
        ready = shifted if affine else normed
        if add is not None:
            added = s.sem("added")
        loads = 4 if affine else 2
        first = affine[2] if affine else h
        source, target = (x, first), (first, h)

        def turn_of(norm, q):
            return q if NORMS == 1 else (2 * q - (q > 0) if norm == 0 else 2 * q + 2 - (q == PAIRS - 1))

        with nc.Block() as block:
            @block.sync
            def _(sp):
                if affine:
                    sp.dma_start(gain[:], affine[0].partition_broadcast(P)).then_inc(loaded, 16)
                    sp.dma_start(shift[:], affine[1].partition_broadcast(P)).then_inc(loaded, 16)
                sp.dma_start(w_rows[:], w).then_inc(loaded, 16)
                sp.dma_start(bias[:], b.partition_broadcast(P)).then_inc(loaded, 16)
                for t in range(NT):
                    sp.wait_ge(ready, t + 1)
                    sp.dma_start(rows[t * P:(t + 1) * P, :], h[:, t, :]).then_inc(stored, 16)
                sp.wait_ge(stored, 16 * NT)

            @block.gpsimd
            def _(pool):
                def scales(norm, q):
                    pair, n = slice(2 * q, 2 * q + 2), turn_of(norm, q)
                    pool.wait_ge(measured, 4 * n + 4)
                    pool.tensor_scalar(rstd[:, norm, pair], mean_var[:, norm, pair, 1], EPS, None, ALU.add).then_inc(scaled, 1)
                    pool.tensor_scalar(offset[:, norm, pair], mean_var[:, norm, pair, 0], -1.0, None, ALU.mult).then_inc(scaled, 1)
                    pool.wait_ge(scaled, 4 * n + 2)
                    pool.tensor_tensor(rstd[:, norm, pair], rstd[:, norm, pair], c["half"][:, pair], ALU.pow).then_inc(scaled, 1)
                    pool.wait_ge(scaled, 4 * n + 3)
                    pool.tensor_tensor(offset[:, norm, pair], offset[:, norm, pair], rstd[:, norm, pair], ALU.mult).then_inc(scaled, 1)

                for q in range(PAIRS + NORMS - 1):
                    if q < PAIRS:
                        scales(0, q)
                    if affine and q >= 1:
                        scales(1, q - 1)
                        for t in (2 * q - 2, 2 * q - 1):
                            pool.tensor_tensor(x[:, t, :], x[:, t, :], first[:, t, :], ALU.add).then_inc(summed, 1)

            @block.scalar
            def _(act):
                def norm_pair(norm, q):
                    n = turn_of(norm, q)
                    act.wait_ge(scaled, 4 * n + 4)
                    for t in (2 * q, 2 * q + 1):
                        act.activation(target[norm][:, t, :], source[norm][:, t, :], ACT.Identity,
                                       scale=rstd[:, norm, t:t + 1], bias=offset[:, norm, t:t + 1]).then_inc(normed, 1)

                for q in range(PAIRS + NORMS):
                    if q < PAIRS:
                        norm_pair(0, q)
                    if affine and 1 <= q <= PAIRS:
                        norm_pair(1, q - 1)
                    if q >= NORMS:
                        for t in (2 * (q - NORMS), 2 * (q - NORMS) + 1):
                            act.wait_ge(turned, t + 1)
                            if t >= 2:
                                act.wait_ge(product, t - 1)
                            act.copy(tile_t[t % 2][:], ps_t[t % 2][:]).then_inc(taken, 1)

            @block.vector
            def _(dve):
                def measure_pair(norm, q):
                    n = turn_of(norm, q)
                    if norm:
                        dve.wait_ge(normed, 2 * turn_of(0, q) + 2)
                    if n:
                        dve.wait_ge(measured, 4 * n)
                    for i in range(2):
                        dve.bn_stats(stats[:, i, :], source[norm][:, 2 * q + i, :]).then_inc(measured, 1)
                    dve.wait_ge(measured, 4 * n + 2)
                    for i in range(2):
                        dve.bn_aggr(mean_var[:, norm, 2 * q + i, :], stats[:, i, :]).then_inc(measured, 1)

                def add_pair(q):
                    pair = slice(2 * q, 2 * q + 2)
                    dve.tensor_tensor(x[:, pair, :], x[:, pair, :], add[:, pair, :], ALU.add).then_inc(added, 1)

                if add is not None:
                    add_pair(0)
                for q in range(PAIRS + NORMS):
                    if q < PAIRS:
                        if add is not None:
                            if q + 1 < PAIRS:
                                add_pair(q + 1)
                            dve.wait_ge(added, q + 1)
                        measure_pair(0, q)
                    if affine and 1 <= q <= PAIRS:
                        measure_pair(1, q - 1)
                    if q == 0:
                        dve.wait_ge(w_turned, 1)
                        dve.tensor_copy(w_t[:], ps_w[:, 0:KD * E].rearrange("p (k e) -> p k e", e=E)).then_inc(w_ready, 1)
                        dve.wait_ge(loaded, 16 * loads)
                    if affine and q >= 2:
                        pair = slice(2 * q - 4, 2 * q - 2)
                        dve.wait_ge(normed, 2 * turn_of(1, q - 2) + 2)
                        for t in (2 * q - 4, 2 * q - 3):
                            dve.tensor_tensor(h[:, t, :], h[:, t, :], gain[:], ALU.mult).then_inc(gained, 1)
                        for t in (2 * q - 4, 2 * q - 3):
                            dve.wait_ge(gained, t + 1)
                            dve.tensor_tensor(h[:, t, :], h[:, t, :], shift[:], ALU.add).then_inc(shifted, 1)
                dve.wait_ge(product, NT)
                dve.tensor_tensor(logits[:], ps_l[:], bias[:].unsqueeze(1).to_broadcast([P, NT, E]), ALU.add)

            @block.tensor
            def _(pe):
                pe.wait_ge(loaded, 16 * loads)
                for k in range(KD):
                    last = pe.transpose(ps_w[:, k * E:(k + 1) * E], w_rows[:, k * P:(k + 1) * P], c["ident"][0:E, 0:E])
                last.then_inc(w_turned, 1)
                for t in range(NT + 1):
                    if t < NT:
                        pe.wait_ge(ready, t + 1)
                        if t >= 2:
                            pe.wait_ge(taken, t - 1)
                        for k in range(KD):
                            last = pe.transpose(ps_t[t % 2][:, k, :], h[:, t, k * P:(k + 1) * P], c["ident"][:])
                        last.then_inc(turned, 1)
                    if t >= 1:
                        if t == 1:
                            pe.wait_ge(w_ready, 1)
                        pe.wait_ge(taken, t)
                        for k in range(KD):
                            last = pe.matmul(ps_l[:, t - 1, :], tile_t[(t - 1) % 2][:, k, :], w_t[:, k, :],
                                             start=(k == 0), stop=(k == KD - 1))
                        last.then_inc(product, 1)


def rank_tokens(nc, c, tag, turn, member, E, rank, total):
    with Stage(nc, tag) as s:
        ps = s.psum("ps_ranks", [P, 2, 256])
        step, summed = c["rank_step"], c["rank_summed"]
        at = (NT + 2) * turn
        flat = member[:].rearrange("p t e -> p (t e)")
        before = s.sbuf("before", [P, NT, E], F32)
        W = NT * E
        with nc.Block() as block:
            @block.tensor
            def _(pe):
                pe.matmul(ps[:, 0, 0:W], c["upper"][:], flat, start=True, stop=True).then_inc(summed, 1)
                pe.matmul(ps[:, 1, 0:W], c["ones"][:], flat, start=True, stop=True).then_inc(summed, 1)

            @block.vector
            def _(dve):
                whole = ps[:, 1, 0:W].rearrange("p (t e) -> p t e", e=E)
                dve.memset(before[:, 0, :], 0.0).then_inc(step, 1)
                dve.wait_ge(summed, 2 * turn + 2)
                for t in range(1, NT):
                    dve.wait_ge(step, at + t)
                    dve.tensor_tensor(before[:, t, :], whole[:, t - 1, :], before[:, t - 1, :], ALU.add).then_inc(step, 1)
                dve.wait_ge(step, at + NT)
                dve.tensor_tensor(total[:], whole[:, NT - 1, :], before[:, NT - 1, :], ALU.add).then_inc(step, 1)
                dve.tensor_tensor(rank[:], ps[:, 0, 0:W].rearrange("p (t e) -> p t e", e=E), before[:], ALU.add).then_inc(step, 1)


def choose(dve, step, at, logits, best, where):
    for t in range(NT):
        dve.max(best[:, t, :], logits[:, t, :]).then_inc(step, 1)
    for t in range(NT):
        dve.wait_ge(step, at + t + 1)
        dve.max_index(where[:, t, :], best[:, t, :], logits[:, t, :]).then_inc(step, 1)


def store_list(nc, tag, ids, node, slots, columns, beside_sp, beside_act, beside_dve):
    n_rows = ids.shape[0]
    with Stage(nc, tag) as s:
        zeros = s.sbuf("zeros", [n_rows // P, P], I32)
        filled, stored = s.sem("filled"), s.sem("stored")
        with nc.Block() as block:
            @block.sync
            def _(sp):
                beside_sp(sp)

            @block.scalar
            def _(act):
                beside_act(act)

            @block.vector
            def _(dve):
                beside_dve(dve)

            @block.gpsimd
            def _(pool):
                pool.memset(zeros[:], 0).then_inc(filled, 1)
                pool.wait_ge(filled, 1)
                pool.dma_start(ids.rearrange("(c p) o -> c (p o)", p=P), zeros[:]).then_inc(stored, 16)
                pool.wait_ge(stored, 16)
                for i in range(columns):
                    t = i % NT
                    real = P if t < NT - 1 else LAST
                    pool.indirect_dma_start(ids, bass.IndirectOffsetOnAxis(ap=slots[0:real, i:i + 1], axis=0),
                                            node[0:real, t:t + 1], None).then_inc(stored, 16)
                pool.wait_ge(stored, 16 * (columns + 1))


def load_list(nc, c, tag, turn, ids, list_t, ps):
    blocks = ids.shape[0] // P
    with Stage(nc, tag) as s:
        rows_i = s.sbuf("rows_i", [blocks, P], I32)
        rows = s.sbuf("rows", [blocks, P], F32)
        loaded, step, turned = c["list_loaded"], c["list_step"], c["list_turned"]
        with nc.Block() as block:
            @block.sync
            def _(sp):
                sp.dma_start(rows_i[:], ids.rearrange("(c p) o -> c (p o)", p=P)).then_inc(loaded, 16)

            @block.vector
            def _(dve):
                dve.wait_ge(loaded, 16 * turn + 16)
                dve.tensor_copy(rows[:], rows_i[:]).then_inc(step, 1)
                dve.wait_ge(turned, turn + 1)
                dve.tensor_copy(list_t[:], ps[:, 0:blocks]).then_inc(step, 1)

            @block.tensor
            def _(pe):
                pe.wait_ge(step, 2 * turn + 1)
                pe.transpose(ps[:, 0:blocks], rows[:], c["ident"][0:blocks, 0:blocks]).then_inc(turned, 1)


def route_top2(nc, c, x, h, w_r, b_r, rows, affine, gates, slots, unit_expert, unit_tokens, n_units):
    E = E1
    with Stage(nc, "top2") as s:
        logits = s.sbuf("logits", [P, NT, E], F32)
        best = s.sbuf("best", [P, NT, 8], F32)
        where = s.sbuf("where", [P, NT, 8], U32)
        column = s.sbuf("expert_column", [P, NT, E], F32)
        chosen = s.sbuf("chosen", [P, 2, NT], F32)
        one = [s.sbuf(f"onehot_{k}", [P, NT, E], F32) for k in range(2)]
        member = s.sbuf("member", [P, NT, E], F32)
        rank = s.sbuf("rank", [P, NT, E], F32)
        total = s.sbuf("total", [P, E], F32)
        gap = s.sbuf("gap", [P, NT], F32)
        small = s.sbuf("small_exp", [P, NT], F32)
        started, step, risen = s.sem("started"), s.sem("step"), s.sem("risen")
        router_logits(nc, c, "logits2", x, h, w_r, b_r, E, logits, rows, affine=affine)
        with nc.Block() as block:
            @block.gpsimd
            def _(pool):
                pool.iota(column[:], pattern=[[0, NT], [1, E]], base=0, channel_multiplier=0,
                          allow_small_or_imprecise_dtypes=True).then_inc(started, 1)

            @block.vector
            def _(dve):
                choose(dve, step, 0, logits, best, where)
                n = 2 * NT
                dve.wait_ge(step, n)
                dve.tensor_tensor(gap[:], best[:, :, 1], best[:, :, 0], ALU.subtract).then_inc(step, 1)
                for k in range(2):
                    dve.tensor_copy(chosen[:, k, :], where[:, :, k]).then_inc(step, 1)
                dve.wait_ge(step, n + 3)
                dve.wait_ge(started, 1)
                for k in range(2):
                    dve.tensor_tensor(one[k][:], column[:], chosen[:, k, :].unsqueeze(2).to_broadcast([P, NT, E]),
                                      ALU.is_equal).then_inc(step, 1)
                dve.wait_ge(step, n + 5)
                dve.tensor_tensor(member[:], one[0][:], one[1][:], ALU.add).then_inc(step, 1)
                dve.wait_ge(step, n + 6)
                dve.tensor_tensor(member[:], member[:], c["real"][:].unsqueeze(2).to_broadcast([P, NT, E]), ALU.mult).then_inc(step, 1)
                dve.wait_ge(risen, 1)
                dve.tensor_scalar(gates[:, 0, :], small[:], 1.0, None, ALU.add).then_inc(step, 1)
                dve.wait_ge(step, n + 8)
                dve.reciprocal(gates[:, 0, :], gates[:, 0, :]).then_inc(step, 1)
                dve.wait_ge(step, n + 9)
                dve.tensor_tensor(gates[:, 1, :], gates[:, 0, :], small[:], ALU.mult).then_inc(step, 1)

            @block.scalar
            def _(act):
                act.wait_ge(step, 2 * NT + 1)
                act.activation(small[:], gap[:], ACT.Exp).then_inc(risen, 1)
        rank_tokens(nc, c, "rank2", 0, member, E, rank, total)
        units = s.sbuf("units", [P, E], F32)
        above = s.sbuf("above", [P, E], F32)
        ends = s.sbuf("unit_ends", [P, E], F32)
        starts = s.sbuf("unit_starts", [P, E], F32)
        ones = s.sbuf("ones_e", [P, E], F32)
        product = s.sbuf("product", [P, NT, E], F32)
        slot = s.sbuf("slot", [P, 2, NT], F32)
        unit_no = s.sbuf("unit_no", [1, UNITS + 1, E], F32)
        begun = s.sbuf("unit_begun", [1, UNITS + 1, E], F32)
        over = s.sbuf("unit_over", [1, UNITS + 1, E], F32)
        rest = s.sbuf("expert_rest", [1, UNITS + 1, E], F32)
        held = s.sbuf("unit_held", [1, UNITS + 1], F32)
        passed = s.sbuf("units_passed", [1, UNITS + 1], F32)
        with nc.Block() as block:
            step, began = s.sem("slot_step"), s.sem("slot_began")

            @block.gpsimd
            def _(pool):
                pool.iota(unit_no[:], pattern=[[1, UNITS + 1], [0, E]], base=0, channel_multiplier=0,
                          allow_small_or_imprecise_dtypes=True).then_inc(began, 1)
                pool.memset(ones[:], 1.0).then_inc(began, 1)

            @block.vector
            def _(dve):
                dve.wait_ge(began, 2)
                dve.tensor_scalar(units[:], total[:], 0.0, None, ALU.is_gt).then_inc(step, 1)
                n = 1
                for b in range(1, -(-N // T)):
                    dve.tensor_scalar(above[:], total[:], float(b * T), None, ALU.is_gt).then_inc(step, 1)
                    dve.wait_ge(step, n + 1)
                    dve.tensor_tensor(units[:], units[:], above[:], ALU.add).then_inc(step, 1)
                    n += 2
                    dve.wait_ge(step, n)
                dve.tensor_tensor_scan(ends[:], ones[:], units[:], 0.0, ALU.mult, ALU.add).then_inc(step, 1)
                dve.wait_ge(step, n + 1)
                dve.tensor_tensor(starts[:], ends[:], units[:], ALU.subtract).then_inc(step, 1)
                dve.wait_ge(step, n + 2)
                dve.tensor_scalar(starts[:], starts[:], float(T), None, ALU.mult).then_inc(step, 1)
                dve.wait_ge(step, n + 3)
                dve.tensor_tensor(rank[:], rank[:], starts[:].unsqueeze(1).to_broadcast([P, NT, E]), ALU.add).then_inc(step, 1)
                n += 4
                dve.wait_ge(step, n)
                for k in range(2):
                    dve.tensor_tensor(product[:], one[k][:], rank[:], ALU.mult).then_inc(step, 1)
                    dve.wait_ge(step, n + 1)
                    dve.tensor_reduce(slot[:, k, :], product[:], AX.X, ALU.add).then_inc(step, 1)
                    dve.wait_ge(step, n + 2)
                    dve.tensor_tensor(slots[:, k * NT:(k + 1) * NT], slot[:, k, :], c["real"][:], ALU.mult).then_inc(step, 1)
                    n += 3
                wide = [1, UNITS + 1, E]
                dve.tensor_tensor(over[:], unit_no[:], ends[0:1, :].unsqueeze(1).to_broadcast(wide), ALU.is_ge).then_inc(step, 1)
                dve.tensor_scalar(rest[:], unit_no[:], float(-T), None, ALU.mult).then_inc(step, 1)
                dve.tensor_tensor(total[:], total[:], starts[:], ALU.add).then_inc(step, 1)
                dve.wait_ge(step, n + 3)
                dve.tensor_reduce(passed[:], over[:], AX.X, ALU.add).then_inc(step, 1)
                dve.tensor_tensor(begun[:], rest[:], starts[0:1, :].unsqueeze(1).to_broadcast(wide), ALU.add).then_inc(step, 1)
                dve.tensor_tensor(rest[:], rest[:], total[0:1, :].unsqueeze(1).to_broadcast(wide), ALU.add).then_inc(step, 1)
                dve.wait_ge(step, n + 6)
                dve.tensor_scalar(begun[:], begun[:], 0.0, None, ALU.is_le).then_inc(step, 1)
                dve.tensor_scalar(unit_expert[:], passed[:], float(E - 1), None, ALU.min).then_inc(step, 1)
                dve.tensor_copy(n_units[:], ends[0:1, E - 1:E]).then_inc(step, 1)
                dve.wait_ge(step, n + 9)
                dve.tensor_tensor(begun[:], begun[:], over[:], ALU.subtract).then_inc(step, 1)
                dve.wait_ge(step, n + 10)
                dve.tensor_tensor(rest[:], rest[:], begun[:], ALU.mult).then_inc(step, 1)
                dve.wait_ge(step, n + 11)
                dve.tensor_reduce(held[:], rest[:], AX.X, ALU.add).then_inc(step, 1)
                dve.wait_ge(step, n + 12)
                dve.tensor_scalar(unit_tokens[:], held[:], float(T), None, ALU.min).then_inc(step, 1)


def top2_experts(nc, c, rows, W1, b1, W2, b2, unit_expert, unit_tokens, n_units, ids, slots, list_t, y_rows):
    NB = TB
    with Stage(nc, "ffn") as s:
        raw1 = [s.sbuf(f"w1_raw_{u}", [P, KD, FB], F32) for u in range(2)]
        raw2 = [s.sbuf(f"w2_raw_{u}", [P, KD, D], F32) for u in range(2)]
        w1h = [s.sbuf(f"w1_high_{u}", [P, KD, FB], F32R) for u in range(2)]
        w1l = [s.sbuf(f"w1_low_{u}", [P, KD, FB], F32R) for u in range(2)]
        w2h = [s.sbuf(f"w2_high_{u}", [P, KD, D], F32R) for u in range(2)]
        w2l = [s.sbuf(f"w2_low_{u}", [P, KD, D], F32R) for u in range(2)]
        token = [s.sbuf(f"token_{j}", [P, D], F32) for j in range(NB)]
        index = [s.sbuf(f"index_{j}", [P, 1], I32) for j in range(NB)]
        xh = s.sbuf("x_high", [P, KD, T], F32R)
        xl = s.sbuf("x_low", [P, KD, T], F32R)
        hid = s.sbuf("hidden", [P, KD, T], F32)
        hh = s.sbuf("hidden_high", [P, KD, T], F32R)
        hl = s.sbuf("hidden_low", [P, KD, T], F32R)
        y = s.sbuf("y", [P, NB, D], F32)
        bias1_rows = s.sbuf("b1_rows", [P, P], F32)
        bias1 = s.sbuf("b1_t", [P, E1 * F1 // P], F32)
        bias2 = s.sbuf("b2", [P, D], F32)
        ps_h = [s.psum(f"ps_hidden_{u}", [P, 512]) for u in range(2)]
        ps_y = [s.psum(f"ps_y_{j}", [P, D]) for j in range(NB)]
        ps_x = [s.psum(f"ps_x_{u}", [P, KD, P]) for u in range(2)]
        W = 2 * KD
        biases, turned_b, biases_t = s.sem("biases"), s.sem("b1_turned"), s.sem("b1_ready")
        loaded = [s.sem(f"w_loaded_{u}") for u in range(2)]
        gathered = [s.sem(f"gathered_{j}") for j in range(NB)]
        index_set = s.sem("index_set")
        w_high = s.sem("w_high")
        w_low = s.sem("w_low")
        turned = s.sem("x_turned")
        x_high = s.sem("x_high_ready")
        x_low = s.sem("x_low_ready")
        first = s.sem("first_product")
        gelu = s.sem("gelu_done")
        h_high = s.sem("hidden_high_ready")
        h_low = s.sem("hidden_low_ready")
        second = s.sem("second_product")
        biased = s.sem("y_biased")
        stored = s.sem("y_stored")
        all_stored = s.sem("all_stored")
        bias2_in = s.sem("b2_loaded")
        cleared = s.sem("ps_cleared")

        def each_unit(eng, body):
            units = eng.value_load(n_units[0:1, 0:1], min_val=0, max_val=UNITS)
            with eng.Fori(0, UNITS) as v:
                with eng.If(units > v):
                    body(v)
            return units

        def expert_of(eng, v):
            return eng.value_load(unit_expert[0:1, bass.ds(v, 1)], min_val=0, max_val=E1 - 1)

        def load(sp, v, f, after=None):
            e, u = expert_of(sp, v), f % 2
            if after is not None:
                sp.wait_ge(w_low, after)
            sp.dma_start(raw1[u][:], W1[bass.ds(e, 1), :, f * FB:(f + 1) * FB].rearrange("e (k p) f -> p (e k) f", p=P)).then_inc(loaded[u], 16)
            sp.dma_start(raw2[u][:], W2[bass.ds(e, 1), f * FB:(f + 1) * FB, :].rearrange("e (k p) d -> p (e k) d", p=P)).then_inc(loaded[u], 16)

        def load_bias2(sp, v):
            e = expert_of(sp, v)
            sp.dma_start(bias2[:], b2[bass.ds(e, 1), :].rearrange("e d -> (e d)").partition_broadcast(P)).then_inc(bias2_in, 16)

        def first_loads(sp):
            sp.dma_start(bias1_rows[:], b1.rearrange("e (c f) -> (e c) f", f=P)).then_inc(biases, 16)
            load(sp, 0, 0)
            load(sp, 0, 1)
            load_bias2(sp, 0)

        def act_cut_w(act, part, u, k):
            raw, high = ((raw1, w1h), (raw2, w2h))[part]
            act.copy(high[u][:, k, :], raw[u][:, k, :]).then_inc(w_high, 1)

        def dve_cut_w(dve, n, part, u, k):
            raw, high, low = ((raw1, w1h, w1l), (raw2, w2h, w2l))[part]
            dve.wait_ge(w_high, W * n + KD * part + k + 1)
            dve.tensor_tensor(low[u][:, k, :], raw[u][:, k, :], high[u][:, k, :].bitcast(F32), ALU.subtract).then_inc(w_low, 1)

        def first_highs(act):
            act.wait_ge(loaded[0], 32)
            for k in range(W):
                act_cut_w(act, k // KD, 0, k % KD)

        def first_lows(dve):
            dve.sem_inc(w_low, 2 * W)
            for ps in ps_h + ps_y:
                dve.memset(ps[:], 0.0).then_inc(cleared, 1)
            for k in range(W):
                dve_cut_w(dve, 0, k // KD, 0, k % KD)

        store_list(nc, "list2", ids, c["node"], slots, 2 * NT, first_loads, first_highs, first_lows)
        load_list(nc, c, "loadlist2", 0, ids, list_t, ps_x[0][:, 0, :])
        with nc.Block() as block:
            @block.sync
            def _(sp):
                def load_after(v, f):
                    load(sp, v, f, after=W * (NFB * v + f) + W)

                def unit(v):
                    load_after(v, 2)
                    load_after(v, 3)
                    load_after(v + 1, 0)
                    load_after(v + 1, 1)
                    sp.wait_ge(biased, NB * v + 2 * NB)
                    sp.dma_start(y_rows[bass.ds(v * T, T), :].rearrange("(j p) d -> p j d", p=P), y[:]).then_inc(stored, 16)
                    load_bias2(sp, v + 1)

                sp.wait_ge(turned, 2 * NB)
                units = each_unit(sp, unit)
                sp.wait_ge(stored, 16 * units + 16)
                sp.wait_ge(loaded[1], 64 * units + 32)
                sp.wait_ge(bias2_in, 16 * units + 16)
                sp.sem_inc(all_stored, 1)

            @block.gpsimd
            def _(pool):
                def gather(v):
                    for j in range(NB):
                        pool.wait_ge(turned, NB * v + j + 1)
                        pool.tensor_copy(index[j][:], list_t[:, bass.ds(NB * v + j, 1)]).then_inc(index_set, 1)
                        pool.wait_ge(index_set, NB * v + j + 1)
                        pool.sem_inc(c["carrier"], 1)
                        pool.indirect_dma_start(token[j][:], None, rows, bass.IndirectOffsetOnAxis(ap=index[j][:, 0:1], axis=0)).then_inc(gathered[j], 16)

                gather(0)
                each_unit(pool, lambda v: gather(v + 1))

            @block.scalar
            def _(act):
                act.sem_inc(gelu, 2)

                def cut_x(v, j):
                    act.wait_ge(turned, NB * v + j + 1 + NB)
                    act.copy(xh[:, :, j * P:(j + 1) * P], ps_x[j % 2][:]).then_inc(x_high, 1)

                act.wait_ge(biases_t, 1)
                for j in range(NB):
                    cut_x(0, j)
                act.wait_ge(cleared, NB + 2)

                def unit(v):
                    e = expert_of(act, v)
                    for f in range(NFB):
                        n = NFB * v + f
                        nu = (f + 1) % 2
                        for m in range(KD):
                            q = 4 * n + m
                            act.wait_ge(first, q + 1)
                            act.wait_ge(h_low, q + 1)
                            act.activation(hid[:, m, :], ps_h[m % 2][:], ACT.Gelu,
                                           bias=bias1[:, bass.ds(e * (F1 // P) + f * KD + m, 1)]).then_inc(gelu, 1)
                            act.wait_ge(gelu, q + 3)
                            act.wait_ge(second, q + 1)
                            act.copy(hh[:, m, :], hid[:, m, :]).then_inc(h_high, 1)
                        act.wait_ge(loaded[nu], 64 * v + 32 * ((f + 1) // 2) + 32)
                        act.wait_ge(second, 4 * n + 4)
                        for k in range(KD):
                            if f == NFB - 1:
                                cut_x(v + 1, k)
                            act_cut_w(act, 0, nu, k)
                        for k in range(KD):
                            act_cut_w(act, 1, nu, k)

                each_unit(act, unit)

            @block.vector
            def _(dve):
                dve.sem_inc(x_low, 2)
                dve.sem_inc(h_low, 4)
                dve.sem_inc(biased, NB)
                dve.sem_inc(stored, 16)

                def cut_x(v, j):
                    dve.wait_ge(x_high, NB * v + j + 1)
                    dve.tensor_tensor(xl[:, :, j * P:(j + 1) * P], ps_x[j % 2][:], xh[:, :, j * P:(j + 1) * P].bitcast(F32),
                                      ALU.subtract).then_inc(x_low, 1)

                dve.wait_ge(turned_b, 1)
                dve.tensor_copy(bias1[:], ps_x[0][:, 0, :]).then_inc(biases_t, 1)
                for j in range(NB):
                    cut_x(0, j)

                def unit(v):
                    for f in range(NFB):
                        n = NFB * v + f
                        for m in range(KD):
                            q = 4 * n + m
                            dve.wait_ge(h_high, q + 1)
                            dve.tensor_tensor(hl[:, m, :], hid[:, m, :], hh[:, m, :].bitcast(F32), ALU.subtract).then_inc(h_low, 1)
                        for k in range(KD):
                            if f == NFB - 1:
                                cut_x(v + 1, k)
                            dve_cut_w(dve, n + 1, 0, (f + 1) % 2, k)
                        for k in range(KD):
                            dve_cut_w(dve, n + 1, 1, (f + 1) % 2, k)
                    dve.wait_ge(second, 4 * NFB * (v + 1) + 4)
                    dve.wait_ge(stored, 16 * v + 16)
                    dve.wait_ge(bias2_in, 16 * v + 16)
                    for j in range(NB):
                        dve.tensor_tensor(y[:, j, :], ps_y[j][:], bias2[:], ALU.add).then_inc(biased, 1)

                each_unit(dve, unit)

            @block.tensor
            def _(pe):
                pe.sem_inc(turned, NB)
                pe.sem_inc(second, 4)
                pe.wait_ge(biases, 16)
                pe.transpose(ps_x[0][:, 0, :], bias1_rows[:], c["ident"][:]).then_inc(turned_b, 1)
                pe.wait_ge(biases_t, 1)

                def turn(v, j):
                    pe.wait_ge(gathered[j], 16 * v + 16)
                    pe.wait_ge(x_low, NB * v + j + 1)
                    for k in range(KD):
                        last = pe.transpose(ps_x[j % 2][:, k, :], token[j][:, k * P:(k + 1) * P], c["ident"][:])
                    last.then_inc(turned, 1)

                for j in range(NB):
                    turn(0, j)
                pe.wait_ge(cleared, NB + 2)

                def multiply(v, width):
                    tiles = -(-width // P)
                    pe.wait_ge(x_low, NB * v + NB + 2)
                    for f in range(NFB):
                        n = NFB * v + f
                        u = f % 2
                        pe.wait_ge(w_low, W * n + KD + 2 * W)
                        for m in range(KD):
                            q = 4 * n + m
                            pe.wait_ge(gelu, q + 1)
                            out = ps_h[m % 2][:, 0:width]
                            for k in range(KD):
                                cols = slice(m * P, (m + 1) * P)
                                pe.matmul(out, w1h[u][:, k, cols], xh[:, k, 0:width], start=(k == 0), stop=False)
                                pe.matmul(out, w1h[u][:, k, cols], xl[:, k, 0:width], start=False, stop=False)
                                last = pe.matmul(out, w1l[u][:, k, cols], xh[:, k, 0:width], start=False, stop=(k == KD - 1))
                            last.then_inc(first, 1)
                        pe.wait_ge(w_low, W * n + W + 2 * W)
                        for m in range(KD):
                            q = 4 * n + m
                            if f == NFB - 1:
                                turn(v + 1, m)
                            pe.wait_ge(h_low, q + 5)
                            if f == 0 and m == 0:
                                pe.wait_ge(biased, NB * v + NB)
                            for j in range(tiles):
                                cols = slice(j * P, (j + 1) * P)
                                pe.matmul(ps_y[j][:], hh[:, m, cols], w2h[u][:, m, :], start=(f == 0 and m == 0), stop=False)
                                pe.matmul(ps_y[j][:], hh[:, m, cols], w2l[u][:, m, :], start=False, stop=False)
                                last = pe.matmul(ps_y[j][:], hl[:, m, cols], w2h[u][:, m, :], start=False,
                                                 stop=(f == NFB - 1 and m == KD - 1))
                            last.then_inc(second, 1)

                def unit(v):
                    tokens = pe.value_load(unit_tokens[0:1, bass.ds(v, 1)], min_val=0, max_val=T)
                    with pe.If(tokens > 3 * P):
                        with pe.If(tokens > 3 * P + P // 2):
                            multiply(v, 4 * P)
                        with pe.Else():
                            multiply(v, 3 * P + P // 2)
                    with pe.Else():
                        with pe.If(tokens > 2 * P):
                            with pe.If(tokens > 2 * P + P // 2):
                                multiply(v, 3 * P)
                            with pe.Else():
                                multiply(v, 2 * P + P // 2)
                        with pe.Else():
                            multiply(v, 2 * P)

                each_unit(pe, unit)


def gather_top2(nc, c, normalize, y_rows, slots, gates, nodes, h):
    RING = 4
    with Stage(nc, "mix") as s:
        y = [s.sbuf(f"y_{r}", [P, D], F32) for r in range(RING)]
        gathered = [s.sem(f"gathered_{r}") for r in range(RING)]
        mixed = s.sem("mixed")
        normalize.begin(s)
        with nc.Block() as block:
            @block.gpsimd
            def _(pool):
                for n in range(2 * NT):
                    t, k = n // 2, n % 2
                    if n >= RING:
                        pool.wait_ge(mixed, n - RING + 1)
                    pool.indirect_dma_start(y[n % RING][:], None, y_rows,
                                            bass.IndirectOffsetOnAxis(ap=slots[:, k * NT + t:k * NT + t + 1], axis=0)).then_inc(gathered[n % RING], 16)
                normalize.pool_scales(pool, c)

            @block.vector
            def _(dve):
                for t in range(NT):
                    for k in range(2):
                        n = 2 * t + k
                        dve.wait_ge(gathered[n % RING], 16 * (n // RING + 1))
                        if k:
                            dve.wait_ge(mixed, n)
                        dve.scalar_tensor_tensor(nodes[:, t, :], y[n % RING][:], gates[:, k, t:t + 1], nodes[:, t, :],
                                                 ALU.mult, ALU.add).then_inc(mixed, 1)
                    dve.wait_ge(mixed, 2 * t + 2)
                    normalize.tile_sums(dve, nodes, t)
                normalize.tile_sums(dve, nodes, NT)
                normalize.apply_dve(dve, nodes, h)

            @block.scalar
            def _(act):
                normalize.apply_act(act, nodes, h)


def route_switch(nc, c, x, add, h, sw_w, sw_b, rows, keep_weight, pass_weight, places, list_place):
    E = E2
    with Stage(nc, "switch") as s:
        logits = s.sbuf("logits", [P, NT, E], F32)
        best = s.sbuf("best", [P, NT, 8], F32)
        where = s.sbuf("where", [P, NT, 8], U32)
        column = s.sbuf("expert_column", [P, NT, E], F32)
        chosen = s.sbuf("chosen", [P, NT], F32)
        one = s.sbuf("onehot", [P, NT, E], F32)
        member = s.sbuf("member", [P, NT, E], F32)
        rank = s.sbuf("rank", [P, NT, E], F32)
        total = s.sbuf("total", [P, E], F32)
        shifted = s.sbuf("shifted", [P, NT, E], F32)
        powers = s.sbuf("powers", [P, NT, E], F32)
        prob = s.sbuf("prob", [P, NT], F32)
        started, step, risen = s.sem("started"), s.sem("step"), s.sem("risen")
        router_logits(nc, c, "logits1", x, h, sw_w, sw_b, E, logits, rows, add=add)
        with nc.Block() as block:
            @block.gpsimd
            def _(pool):
                pool.iota(column[:], pattern=[[0, NT], [1, E]], base=0, channel_multiplier=0,
                          allow_small_or_imprecise_dtypes=True).then_inc(started, 1)

            @block.vector
            def _(dve):
                choose(dve, step, 0, logits, best, where)
                n = 2 * NT
                dve.wait_ge(step, n)
                dve.tensor_tensor(shifted[:], logits[:], best[:, :, 0:1].to_broadcast([P, NT, E]), ALU.subtract).then_inc(step, 1)
                dve.tensor_copy(chosen[:], where[:, :, 0]).then_inc(step, 1)
                dve.wait_ge(step, n + 2)
                dve.wait_ge(started, 1)
                dve.tensor_tensor(one[:], column[:], chosen[:].unsqueeze(2).to_broadcast([P, NT, E]), ALU.is_equal).then_inc(step, 1)
                dve.wait_ge(step, n + 3)
                dve.tensor_tensor(member[:], one[:], c["real"][:].unsqueeze(2).to_broadcast([P, NT, E]), ALU.mult).then_inc(step, 1)
                dve.wait_ge(risen, 1)
                dve.tensor_reduce(prob[:], powers[:], AX.X, ALU.add).then_inc(step, 1)
                dve.wait_ge(step, n + 5)
                dve.reciprocal(prob[:], prob[:]).then_inc(step, 1)

            @block.scalar
            def _(act):
                act.wait_ge(step, 2 * NT + 1)
                act.activation(powers[:], shifted[:], ACT.Exp).then_inc(risen, 1)
        rank_tokens(nc, c, "rank1", 1, member, E, rank, total)
        pos = s.sbuf("position", [P, NT], F32)
        kept = s.sbuf("kept", [P, NT], F32)
        left = s.sbuf("left", [P, NT], F32)
        start = s.sbuf("expert_start", [P, NT], F32)
        place = s.sbuf("place", [P, NT], F32)
        spare = s.sbuf("spare_place", [P, NT], F32)
        with nc.Block() as block:
            step, began = s.sem("place_step"), s.sem("place_began")

            @block.gpsimd
            def _(pool):
                pool.iota(spare[:], pattern=[[P, NT]], base=PLACES, channel_multiplier=1,
                          allow_small_or_imprecise_dtypes=True).then_inc(began, 1)

            @block.vector
            def _(dve):
                dve.wait_ge(began, 1)
                dve.tensor_tensor(one[:], one[:], rank[:], ALU.mult).then_inc(step, 1)
                dve.tensor_scalar(start[:], chosen[:], float(P), None, ALU.mult).then_inc(step, 1)
                dve.wait_ge(step, 2)
                dve.tensor_reduce(pos[:], one[:], AX.X, ALU.add).then_inc(step, 1)
                dve.wait_ge(step, 3)
                dve.scalar_tensor_tensor(kept[:], pos[:], float(CAP), c["real"][:], ALU.is_lt, ALU.mult).then_inc(step, 1)
                dve.scalar_tensor_tensor(place[:], pos[:], float(CAP - 1), start[:], ALU.min, ALU.add).then_inc(step, 1)
                dve.wait_ge(step, 5)
                dve.tensor_copy(places[:], place[:]).then_inc(step, 1)
                dve.tensor_scalar(left[:], kept[:], -1.0, 1.0, ALU.mult, ALU.add).then_inc(step, 1)
                dve.tensor_tensor(keep_weight[:], kept[:], prob[:], ALU.mult).then_inc(step, 1)
                dve.wait_ge(step, 8)
                dve.tensor_tensor(pass_weight[:], left[:], prob[:], ALU.mult).then_inc(step, 1)
                dve.tensor_tensor(spare[:], spare[:], left[:], ALU.mult).then_inc(step, 1)
                dve.tensor_tensor(place[:], place[:], kept[:], ALU.mult).then_inc(step, 1)
                dve.wait_ge(step, 11)
                dve.tensor_tensor(list_place[:], place[:], spare[:], ALU.add).then_inc(step, 1)


def switch_experts(nc, c, rows, ex_w, ex_b, ids, list_place, list_t, y_rows):
    with Stage(nc, "experts") as s:
        w = [s.sbuf(f"w_{u}", [P, KD, D], F32) for u in range(2)]
        token = [s.sbuf(f"token_{u}", [P, D], F32) for u in range(2)]
        index = [s.sbuf(f"index_{u}", [P, 1], I32) for u in range(2)]
        wh = [s.sbuf(f"w_high_{u}", [P, KD, D], F32R) for u in range(2)]
        wl = [s.sbuf(f"w_low_{u}", [P, KD, D], F32R) for u in range(2)]
        xh = [s.sbuf(f"x_high_{u}", [P, KD, P], F32R) for u in range(2)]
        xl = [s.sbuf(f"x_low_{u}", [P, KD, P], F32R) for u in range(2)]
        y = [s.sbuf(f"y_{u}", [P, D], F32) for u in range(2)]
        bias = s.sbuf("bias", [P, E2, D], F32)
        ps_t = [s.psum(f"ps_t_{i}", [P, 512]) for i in range(5)]
        ps_y = [s.psum(f"ps_y_{u}", [P, D]) for u in range(2)]
        biases, index_set = s.sem("biases"), s.sem("index_set")
        loaded = [s.sem(f"loaded_{u}") for u in range(2)]
        gathered = [s.sem(f"gathered_{u}") for u in range(2)]
        turned = s.sem("turned")
        high = s.sem("high")
        low = s.sem("low")
        product = s.sem("product")
        biased = s.sem("biased")
        stored = [s.sem(f"stored_{u}") for u in range(2)]

        def load(sp, e, u):
            sp.dma_start(w[u][:], ex_w[bass.ds(e, 1), :, :].rearrange("e (o p) d -> p (e o) d", p=P)).then_inc(loaded[u], 16)

        def first_loads(sp):
            load(sp, 0, 0)
            load(sp, 1, 1)
            sp.dma_start(bias[:], ex_b.rearrange("e d -> (e d)").partition_broadcast(P)).then_inc(biases, 16)

        store_list(nc, "list1", ids, c["node"], list_place, NT, first_loads, lambda act: None, lambda dve: None)
        load_list(nc, c, "loadlist1", 1, ids, list_t, ps_t[0])
        with nc.Block() as block:
            @block.sync
            def _(sp):
                with sp.Fori(0, E2 // 2 - 1) as i:
                    for u in range(2):
                        sp.wait_ge(turned, 5 * (2 * i + u) + 15)
                        load(sp, 2 * i + u + 2, u)

            @block.gpsimd
            def _(pool):
                with pool.Fori(0, E2 // 2) as i:
                    for u in range(2):
                        e = 2 * i + u
                        pool.wait_ge(turned, 5 * e + 1)
                        pool.tensor_copy(index[u][:], list_t[:, bass.ds(e, 1)]).then_inc(index_set, 1)
                        pool.wait_ge(index_set, e + 1)
                        pool.sem_inc(c["carrier"], 1)
                        pool.indirect_dma_start(token[u][:], None, rows, bass.IndirectOffsetOnAxis(ap=index[u][:, 0:1], axis=0)).then_inc(gathered[u], 16)

            @block.scalar
            def _(act):
                for u in range(2):
                    act.sem_inc(stored[u], 16)

                def cut(e, u):
                    act.wait_ge(product, e + 1)
                    for j in range(5):
                        act.wait_ge(turned, 5 * e + j + 11)
                        target = xh[u][:].rearrange("p k n -> p (k n)") if j == 0 else wh[u][:, j - 1, :]
                        act.copy(target, ps_t[j][:]).then_inc(high, 1)

                def store(e, u):
                    act.wait_ge(biased, e + 3)
                    act.dma_start(y_rows[bass.ds(e * P, P), :], y[u][:]).then_inc(stored[u], 16)

                cut(0, 0)
                with act.Fori(0, E2 // 2 - 1) as i:
                    cut(2 * i + 1, 1)
                    cut(2 * i + 2, 0)
                    store(2 * i, 0)
                    store(2 * i + 1, 1)
                cut(E2 - 1, 1)
                store(E2 - 2, 0)
                store(E2 - 1, 1)
                for u in range(2):
                    act.wait_ge(stored[u], 16 * (E2 // 2 + 1))

            @block.vector
            def _(dve):
                dve.sem_inc(low, 5)
                dve.sem_inc(biased, 2)
                dve.wait_ge(biases, 16)

                def cut(e, u):
                    for j in range(5):
                        dve.wait_ge(high, 5 * e + j + 1)
                        if j == 0:
                            target, upper = xl[u][:].rearrange("p k n -> p (k n)"), xh[u][:].rearrange("p k n -> p (k n)")
                        else:
                            target, upper = wl[u][:, j - 1, :], wh[u][:, j - 1, :]
                        dve.tensor_tensor(target, ps_t[j][:], upper.bitcast(F32), ALU.subtract).then_inc(low, 1)

                def finish(e, i, u):
                    dve.wait_ge(product, e + 3)
                    dve.wait_ge(stored[u], 16 * i + 16)
                    dve.tensor_tensor(y[u][:], ps_y[u][:], bias[:, bass.ds(e, 1), :].rearrange("p a d -> p (a d)"), ALU.add).then_inc(biased, 1)

                cut(0, 0)
                with dve.Fori(0, E2 // 2 - 1) as i:
                    cut(2 * i + 1, 1)
                    finish(2 * i, i, 0)
                    cut(2 * i + 2, 0)
                    finish(2 * i + 1, i, 1)
                cut(E2 - 1, 1)
                finish(E2 - 2, E2 // 2 - 1, 0)
                finish(E2 - 1, E2 // 2 - 1, 1)

            @block.tensor
            def _(pe):
                pe.sem_inc(turned, 10)
                pe.sem_inc(product, 2)

                def turn(e, i, u):
                    pe.wait_ge(gathered[u], 16 * i + 16)
                    pe.wait_ge(loaded[u], 16 * i + 16)
                    for j in range(5):
                        pe.wait_ge(low, 5 * e + j + 1)
                        for o in range(KD):
                            src = token[u][:, o * P:(o + 1) * P] if j == 0 else w[u][:, o, (j - 1) * P:j * P]
                            last = pe.transpose(ps_t[j][:, o * P:(o + 1) * P], src, c["ident"][:])
                        last.then_inc(turned, 1)

                def multiply(e, u):
                    pe.wait_ge(low, 5 * e + 10)
                    pe.wait_ge(biased, e + 1)
                    for k in range(KD):
                        pe.matmul(ps_y[u][:], xh[u][:, k, :], wh[u][:, k, :], start=(k == 0), stop=False)
                        pe.matmul(ps_y[u][:], xh[u][:, k, :], wl[u][:, k, :], start=False, stop=False)
                        last = pe.matmul(ps_y[u][:], xl[u][:, k, :], wh[u][:, k, :], start=False, stop=(k == KD - 1))
                    last.then_inc(product, 1)

                turn(0, 0, 0)
                with pe.Fori(0, E2 // 2 - 1) as i:
                    turn(2 * i + 1, i, 1)
                    multiply(2 * i, 0)
                    turn(2 * i + 2, i + 1, 0)
                    multiply(2 * i + 1, 1)
                turn(E2 - 1, E2 // 2 - 1, 1)
                multiply(E2 - 2, 0)
                multiply(E2 - 1, 1)


def switch_output(nc, c, y_rows, places, keep_weight, pass_weight, h, nodes, out):
    RING = 4
    with Stage(nc, "output") as s:
        y = [s.sbuf(f"y_{r}", [P, D], F32) for r in range(RING)]
        passed, added, stored = s.sem("passed"), s.sem("added"), s.sem("stored")
        gathered = [s.sem(f"gathered_{r}") for r in range(RING)]
        with nc.Block() as block:
            @block.gpsimd
            def _(pool):
                for t in range(NT):
                    if t >= RING:
                        pool.wait_ge(added, t - RING + 1)
                    pool.indirect_dma_start(y[t % RING][:], None, y_rows,
                                            bass.IndirectOffsetOnAxis(ap=places[:, t:t + 1], axis=0)).then_inc(gathered[t % RING], 16)

            @block.vector
            def _(dve):
                for t in range(NT):
                    dve.scalar_tensor_tensor(nodes[:, t, :], h[:, t, :], pass_weight[:, t:t + 1], nodes[:, t, :],
                                             ALU.mult, ALU.add).then_inc(passed, 1)
                    dve.wait_ge(gathered[t % RING], 16 * (t // RING + 1))
                    dve.wait_ge(passed, t + 1)
                    dve.scalar_tensor_tensor(nodes[:, t, :], y[t % RING][:], keep_weight[:, t:t + 1], nodes[:, t, :],
                                             ALU.mult, ALU.add).then_inc(added, 1)

            @block.sync
            def _(sp):
                for t in range(NT):
                    real = P if t < NT - 1 else LAST
                    sp.wait_ge(added, t + 1)
                    sp.dma_start(out[t * P:t * P + real, :], nodes[0:real, t, :]).then_inc(stored, 16)
                sp.wait_ge(stored, 16 * NT)


def load_nodes(nc, x, nodes):
    with Stage(nc, "load") as s:
        cleared, loaded = s.sem("cleared"), s.sem("loaded")
        with nc.Block() as block:
            @block.vector
            def _(dve):
                dve.memset(nodes[:, NT - 1, :], 0.0).then_inc(cleared, 1)

            @block.sync
            def _(sp):
                sp.dma_start(nodes[:, 0:NT - 1, :], by_tile(x[0:(NT - 1) * P, :])).then_inc(loaded, 16)
                sp.wait_ge(cleared, 1)
                sp.dma_start(nodes[0:LAST, NT - 1, :], x[(NT - 1) * P:N, :]).then_inc(loaded, 16)
                sp.wait_ge(loaded, 32)


def program(nc, x, src, dst, gnn_w, ln_g, ln_b, w_r, b_r, W1, b1, W2, b2, Ws, Wn, bs, sw_w, sw_b, ex_w, ex_b, out):
    rows = nc.dram_tensor("token_rows", [NPAD, D], F32, kind="Internal").ap()
    rows2 = nc.dram_tensor("token_rows_2", [NPAD, D], F32, kind="Internal").ap()
    ids = nc.dram_tensor("unit_list", [SLOTS + T, 1], I32, kind="Internal").ap()
    ids2 = nc.dram_tensor("expert_list", [PLACES + NPAD, 1], I32, kind="Internal").ap()
    y_rows = nc.dram_tensor("unit_rows", [SLOTS, D], F32, kind="Internal").ap()
    y_rows2 = nc.dram_tensor("expert_rows", [PLACES, D], F32, kind="Internal").ap()
    with Stage(nc, "keep") as keep:
        c = make_constants(nc, keep)
        normalize = Normalizer(keep)
        counts = keep.sbuf("edge_counts", [P, NT, AW], U16)
        nodes = keep.sbuf("nodes", [P, NT, D], F32)
        inverse = keep.sbuf("inverse_degree", [P, NT], F32)
        load_nodes(nc, x, nodes)
        crowded = keep.sbuf("crowded", [1, 1], I32)
        with Stage(nc, "a") as s:
            h = s.sbuf("h", [P, NT, D], F32)
            natural = s.sbuf("w_natural", [P, KD, 2 * D], F32)
            build_adjacency(nc, c, src, dst, counts, crowded, y_rows, nodes, h, gnn_w, natural)
            sage_layer(nc, c, natural, h, nodes, counts, crowded, inverse)
        with Stage(nc, "b") as s:
            gates = s.sbuf("gates", [P, 2, NT], F32)
            slots = s.sbuf("slots", [P, 2 * NT], I32)
            unit_expert = s.sbuf("unit_expert", [1, UNITS + 1], I32)
            unit_tokens = s.sbuf("unit_tokens", [1, UNITS + 1], I32)
            n_units = s.sbuf("n_units", [1, 1], I32)
            with Stage(nc, "b2") as q:
                h = q.sbuf("h", [P, NT, D], F32)
                hn = q.sbuf("h_norm", [P, NT, D], F32)
                route_top2(nc, c, nodes, hn, w_r, b_r, rows, (ln_g, ln_b, h), gates, slots, unit_expert, unit_tokens, n_units)
            with Stage(nc, "b3") as q:
                list_t = q.sbuf("list", [P, (SLOTS + T) // P], I32)
                top2_experts(nc, c, rows, W1, b1, W2, b2, unit_expert, unit_tokens, n_units, ids, slots, list_t, y_rows)
            with Stage(nc, "c") as q:
                h = q.sbuf("h", [P, NT, D], F32)
                gather_top2(nc, c, normalize, y_rows, slots, gates, nodes, h)
                graph_layers(nc, c, Ws, Wn, bs, h, counts, crowded, inverse)
                hn = q.sbuf("h_norm", [P, NT, D], F32)
                keep_weight = q.sbuf("keep_weight", [P, NT], F32)
                pass_weight = q.sbuf("pass_weight", [P, NT], F32)
                places = q.sbuf("places", [P, NT], I32)
                list_t = q.sbuf("list", [P, (PLACES + NPAD) // P], I32)
                list_place = q.sbuf("list_place", [P, NT], I32)
                route_switch(nc, c, nodes, h, hn, sw_w, sw_b, rows2, keep_weight, pass_weight, places, list_place)
                switch_experts(nc, c, rows2, ex_w, ex_b, ids2, list_place, list_t, y_rows2)
                switch_output(nc, c, y_rows2, places, keep_weight, pass_weight, hn, nodes, out)


_INS = ["x", "src", "dst", "L0_gnn_w", "L0_ffn_ln_g", "L0_ffn_ln_b", "L0_ffn_w_r", "L0_ffn_b_r", "L0_ffn_W1",
        "L0_ffn_b1", "L0_ffn_W2", "L0_ffn_b2", "L1_gnn_Ws_self", "L1_gnn_Ws_neigh", "L1_gnn_bs",
        "L1_ffn_switch_w", "L1_ffn_switch_b", "L1_ffn_expert_w", "L1_ffn_expert_b"]


def kernel(**inputs):
    import numpy as _np
    import concourse.bacc as _bacc
    from concourse import mybir as _mybir
    from concourse.bass_utils import run_bass_kernel_spmd as _run

    nc = _bacc.Bacc("TRN2", target_bir_lowering=False, num_devices=1)
    arrays, args = {}, []
    for name in _INS:
        a = _np.ascontiguousarray(inputs[name])
        arrays[f"in_{name}"] = a
        args.append(nc.dram_tensor(f"in_{name}", a.shape, _mybir.dt.from_np(a.dtype), kind="ExternalInput").ap())
    result = nc.dram_tensor("result", (N, D), F32, kind="ExternalOutput").ap()
    program(nc, *args, result)
    r = _run(nc, [arrays], core_ids=[0])
    return r.results[0]["result"]
```
